# Optimizing a Trainium2 kernel written in Bass

```python
import numpy as np
import jax
import jax.numpy as jnp

def _softmax(x, axis=-1):
    return jax.nn.softmax(x, axis=axis)

def _gelu(x):
    return jax.nn.gelu(x, approximate=True)

def _silu(x):
    return jax.nn.silu(x)

def _sigmoid(x):
    return jax.nn.sigmoid(x)

def _layernorm(x, axis=-1, eps=1e-05):
    m = jnp.mean(x, axis=axis, keepdims=True)
    v = jnp.var(x, axis=axis, keepdims=True)
    return (x - m) / jnp.sqrt(v + eps)

def _scatter_add(tgt, idx, src, axis=0):
    return tgt.at[idx].add(src)

def _segment_sum(src, seg, n):
    return jax.ops.segment_sum(src, seg, n)
kernel_name = 'mk_decoder_preln_d2_seqx_r8_1da5e3'

def setup_inputs(seed: int=0):
    np.random.seed(seed)
    _w = jnp.asarray

    def _rec_inputs():
        import jax
        import jax.numpy as jnp
        _rk = jax.random.key(seed)
        x = 7.22e-05 + 1 * jax.random.normal(jax.random.fold_in(_rk, 1), (32, 64, 256), jnp.float32)
        _lenS = 64 - jax.random.randint(jax.random.fold_in(_rk, 7), (32,), 0, max(1, 64 // 4) + 1, jnp.int32)
        _lenS2 = 64 - jax.random.randint(jax.random.fold_in(_rk, 8), (32,), 0, max(1, 64 // 4) + 1, jnp.int32)
        _ctx_2048P = jax.random.normal(jax.random.fold_in(_rk, 11), (32, 16, 256), jnp.float32)
        _ctx_2048c = jax.random.dirichlet(jax.random.fold_in(_rk, 511), 0.3 * jnp.ones((16,), jnp.float32), (32, 64))
        _ctx_2048t = jnp.einsum('bsk,bkd->bsd', _ctx_2048c, _ctx_2048P)
        _ctx_2048t = _ctx_2048t * jax.lax.rsqrt(jnp.mean(jnp.square(_ctx_2048t)) + 1e-12) * 0.953939
        ctx_2048 = -0.000514642 + 1.00011 * (_ctx_2048t + 0.3 * jax.random.normal(jax.random.fold_in(_rk, 611), (32, 64, 256), jnp.float32))
        return (x, ctx_2048)
    x, ctx_2048 = _rec_inputs()

    def _L0_attn_setup():
        import jax, jax.numpy as jnp
        import numpy as np
        BLOCK = 32
        NUM_HEADS = 16
        HEAD_DIM = 128
        FP4_GRID = jnp.array([0.0, 0.5, 1.0, 1.5, 2.0, 3.0, 4.0, 6.0], dtype=jnp.float32)

        def quantize_to_mxfp4(w, block_size=BLOCK):
            D, F = w.shape
            blocks = w.reshape(D // block_size, block_size, F)
            amax = jnp.max(jnp.abs(blocks), axis=1)
            e = jnp.floor(jnp.log2(jnp.maximum(amax, 1e-12) / 6.0))
            scale = jnp.exp2(e)
            v = blocks / scale[:, None, :]
            idx = jnp.argmin(jnp.abs(jnp.abs(v)[..., None] - FP4_GRID), axis=-1)
            codes = jnp.sign(v) * FP4_GRID[idx]
            return (codes.reshape(D, F).astype(jnp.float32), scale.astype(jnp.float32))

        def _mxfp4_matmul(x, codes, scales, block_size=BLOCK):
            w = codes * jnp.repeat(scales, block_size, axis=0)
            return x @ w
        key = jax.random.key(seed)
        ks = jax.random.split(key, 9)
        B, S, D = (2, 256, 256)
        feat = NUM_HEADS * HEAD_DIM
        x = jax.random.normal(ks[0], (B, S, D), dtype=jnp.float32)

        def make_w(k, din, dout):
            w = jax.random.normal(k, (din, dout), dtype=jnp.float32) * (1.0 / np.sqrt(din))
            return quantize_to_mxfp4(w, BLOCK)
        wq_codes, wq_scales = make_w(ks[1], D, feat)
        wk_codes, wk_scales = make_w(ks[2], D, feat)
        wv_codes, wv_scales = make_w(ks[3], D, feat)
        wo_codes, wo_scales = make_w(ks[4], feat, D)
        bq = jnp.zeros((feat,), jnp.float32)
        bk = jnp.zeros((feat,), jnp.float32)
        bv = jnp.zeros((feat,), jnp.float32)
        bo = jnp.zeros((D,), jnp.float32)
        return {'x': x, 'wq_codes': wq_codes, 'wq_scales': wq_scales, 'bq': bq, 'wk_codes': wk_codes, 'wk_scales': wk_scales, 'bk': bk, 'wv_codes': wv_codes, 'wv_scales': wv_scales, 'bv': bv, 'wo_codes': wo_codes, 'wo_scales': wo_scales, 'bo': bo}
    _L0_attn_all = _L0_attn_setup()
    _L0_attn_in = {k: v for k, v in _L0_attn_all.items() if k in ('wq_codes', 'wq_scales', 'bq', 'wk_codes', 'wk_scales', 'bk', 'wv_codes', 'wv_scales', 'bv', 'wo_codes', 'wo_scales', 'bo')}
    del _L0_attn_all

    def _L0_xattn_setup():
        import jax, jax.numpy as jnp
        import numpy as np
        HIDDEN = 256
        NUM_HEADS = 16
        NUM_KV_HEADS = 4
        HEAD_DIM = 128
        ROPE_THETA = 10000.0
        EPS = 1e-06

        def rms_norm(x, w, eps=EPS):
            var = jnp.mean(jnp.square(x), axis=-1, keepdims=True)
            return x * jax.lax.rsqrt(var + eps) * w

        def rope_cache(L, head_dim, theta, dtype):
            inv_freq = 1.0 / theta ** (jnp.arange(0, head_dim, 2, dtype=jnp.float32) / head_dim)
            t = jnp.arange(L, dtype=jnp.float32)
            freqs = jnp.outer(t, inv_freq)
            emb = jnp.concatenate([freqs, freqs], -1)
            cos = jnp.cos(emb).astype(dtype)[None, :, None, :]
            sin = jnp.sin(emb).astype(dtype)[None, :, None, :]
            return (cos, sin)

        def rotate_half(x):
            x1, x2 = jnp.split(x, 2, axis=-1)
            return jnp.concatenate([-x2, x1], axis=-1)
        key = jax.random.key(seed)
        ks = jax.random.split(key, 10)
        B, L, T = (2, 256, 64)
        q_out = NUM_HEADS * HEAD_DIM
        kv_out = NUM_KV_HEADS * HEAD_DIM
        s = lambda fan_in: 1.0 / np.sqrt(fan_in)
        return {'x': jax.random.normal(ks[0], (B, L, HIDDEN), jnp.float32), 'h_ctx_kv': jax.random.normal(ks[1], (B, T, HIDDEN), jnp.float32), 'wq': jax.random.normal(ks[2], (HIDDEN, q_out), jnp.float32) * s(HIDDEN), 'wk': jax.random.normal(ks[3], (HIDDEN, kv_out), jnp.float32) * s(HIDDEN), 'wv': jax.random.normal(ks[4], (HIDDEN, kv_out), jnp.float32) * s(HIDDEN), 'wo': jax.random.normal(ks[5], (q_out, HIDDEN), jnp.float32) * s(q_out), 'wk_ctx': jax.random.normal(ks[6], (HIDDEN, kv_out), jnp.float32) * s(HIDDEN), 'wv_ctx': jax.random.normal(ks[7], (HIDDEN, kv_out), jnp.float32) * s(HIDDEN), 'q_norm_w': jnp.ones((HEAD_DIM,), jnp.float32), 'k_norm_w': jnp.ones((HEAD_DIM,), jnp.float32)}
    _L0_xattn_all = _L0_xattn_setup()
    _L0_xattn_in = {k: v for k, v in _L0_xattn_all.items() if k in ('wq', 'wk', 'wv', 'wo', 'wk_ctx', 'wv_ctx', 'q_norm_w', 'k_norm_w')}
    del _L0_xattn_all

    def _L0_ffn_setup():
        import jax, jax.numpy as jnp
        import numpy as np

        def _sparsify_2to4(h):
            B, S, I = h.shape
            g = h.reshape(B, S, I // 4, 4)
            a = jnp.abs(g)
            _, idx = jax.lax.top_k(a, 2)
            pos = jnp.arange(4)
            mask = (pos == idx[..., 0:1]) | (pos == idx[..., 1:2])
            return (g * mask.astype(g.dtype)).reshape(B, S, I)
        key = jax.random.key(seed)
        k1, k2, k3, k4 = jax.random.split(key, 4)
        B, S, H, I = (4, 256, 256, 1024)
        x = jax.random.normal(k1, (B, S, H), dtype=jnp.float32)
        w_gate = jax.random.normal(k2, (H, I), dtype=jnp.float32) / np.sqrt(H)
        w_up = jax.random.normal(k3, (H, I), dtype=jnp.float32) / np.sqrt(H)
        w_down = jax.random.normal(k4, (I, H), dtype=jnp.float32) / np.sqrt(I)
        return {'x': x, 'w_gate': w_gate, 'w_up': w_up, 'w_down': w_down}
    _L0_ffn_all = _L0_ffn_setup()
    _L0_ffn_in = {k: v for k, v in _L0_ffn_all.items() if k in ('w_gate', 'w_up', 'w_down')}
    del _L0_ffn_all

    def _L1_attn_setup():
        import jax, jax.numpy as jnp
        import numpy as np
        import math
        N_EMBD = 256
        N_HEAD = 16
        RATIO_KV = 4
        N_HEAD_KV = N_HEAD // RATIO_KV
        HEAD_DIM = N_EMBD // N_HEAD

        def alibi_slopes(n_heads):

            def pow2_slopes(n):
                start = 2 ** (-2 ** (-(math.log2(n) - 3)))
                return [start * start ** i for i in range(n)]
            if math.log2(n_heads).is_integer():
                return jnp.array(pow2_slopes(n_heads), dtype=jnp.float32)
            cp2 = 2 ** math.floor(math.log2(n_heads))
            base = pow2_slopes(cp2)
            if n_heads <= 2 * cp2:
                s = base + base[0::2]
            else:
                s = base + base[0::2] + base[1::2]
            return jnp.array(s[:n_heads], dtype=jnp.float32)
        key = jax.random.key(seed)
        ks = jax.random.split(key, 5)
        B, T = (4, 256)
        scale = 1.0 / math.sqrt(N_EMBD)
        x = jax.random.normal(ks[0], (B, T, N_EMBD), dtype=jnp.float32)
        Wq = jax.random.normal(ks[1], (N_EMBD, N_EMBD), dtype=jnp.float32) * scale
        Wk = jax.random.normal(ks[2], (N_EMBD, N_HEAD_KV * HEAD_DIM), dtype=jnp.float32) * scale
        Wv = jax.random.normal(ks[3], (N_EMBD, N_HEAD_KV * HEAD_DIM), dtype=jnp.float32) * scale
        Wo = jax.random.normal(ks[4], (N_EMBD, N_EMBD), dtype=jnp.float32) * scale
        return {'x': x, 'Wq': Wq, 'Wk': Wk, 'Wv': Wv, 'Wo': Wo}
    _L1_attn_all = _L1_attn_setup()
    _L1_attn_in = {k: v for k, v in _L1_attn_all.items() if k in ('Wq', 'Wk', 'Wv', 'Wo')}
    del _L1_attn_all

    def _L1_xattn_setup():
        import math
        import jax, jax.numpy as jnp
        import numpy as np
        N_HEADS = 16
        key = jax.random.key(seed)
        k1, k2 = jax.random.split(key)
        qkv = jax.random.normal(k1, (2, 128, 256), dtype=jnp.float32)
        y = jax.random.normal(k2, (2, 128, 256), dtype=jnp.float32)
        return {'qkv': qkv, 'y': y}
    _L1_xattn_all = _L1_xattn_setup()
    _L1_xattn_in = {k: v for k, v in _L1_xattn_all.items() if k in ()}
    del _L1_xattn_all

    def _L1_ffn_setup():
        import jax, jax.numpy as jnp
        import numpy as np
        NUM_EXPERTS = 32
        TOP_K = 8
        SELECT_TOP_K = 4
        THRESHOLD = 0.5
        HIDDEN = 256
        D_FF = 96

        def _moe_forward(hidden_states, gate_weight, gate_up_proj, down_proj, similarity):
            B, S_len, H = hidden_states.shape
            E, K, Ssel = (NUM_EXPERTS, TOP_K, SELECT_TOP_K)
            x = hidden_states.reshape(-1, H)
            router_logits = x @ gate_weight.T
            router_probs = jax.nn.softmax(router_logits.astype(jnp.float32), axis=-1).astype(router_logits.dtype)
            router_top_value, router_indices = jax.lax.top_k(router_probs, K)
            routing_weights = router_top_value / jnp.clip(jnp.sum(router_top_value, axis=-1, keepdims=True), 1e-12, None)
            sim = similarity.astype(jnp.float32)
            sim = sim.at[jnp.arange(E), jnp.arange(E)].set(1.0)
            prim = router_indices[:, :Ssel]
            sec = router_indices[:, Ssel:]
            sim_cand = sim[sec[:, :, None], prim[:, None, :]]
            best_sim = jnp.max(sim_cand, axis=-1)
            best_i = jnp.argmax(sim_cand, axis=-1)
            prim_rep = jnp.broadcast_to(prim[:, None, :], sim_cand.shape)
            best_primary = jnp.take_along_axis(prim_rep, best_i[..., None], axis=-1)[..., 0]
            new_sec = jnp.where(best_sim < THRESHOLD, sec, best_primary) if THRESHOLD > 0.0 else best_primary
            rerouted_indices = jnp.concatenate([prim, new_sec], axis=1)
            combine = jnp.sum(jax.nn.one_hot(rerouted_indices, E, dtype=routing_weights.dtype) * routing_weights[..., None], axis=1)

            def expert_step(y, params):
                wgu, wd, cw = params
                gu = x @ wgu.T
                g, u = jnp.split(gu, 2, axis=-1)
                h = jax.nn.silu(g) * u
                y = y + h @ wd.T * cw[:, None]
                return (y, None)
            y0 = jnp.zeros_like(x)
            y, _ = jax.lax.scan(expert_step, y0, (gate_up_proj, down_proj, combine.T))
            return y.reshape(B, S_len, H)
        key = jax.random.key(seed)
        ks = jax.random.split(key, 5)
        hidden_states = jax.random.normal(ks[0], (4, 256, HIDDEN), dtype=jnp.float32)
        gate_weight = jax.random.normal(ks[1], (NUM_EXPERTS, HIDDEN), dtype=jnp.float32) * 0.02
        gate_up_proj = jax.random.normal(ks[2], (NUM_EXPERTS, 2 * D_FF, HIDDEN), dtype=jnp.float32) * 0.02
        down_proj = jax.random.normal(ks[3], (NUM_EXPERTS, HIDDEN, D_FF), dtype=jnp.float32) * 0.02
        similarity = jax.random.uniform(ks[4], (NUM_EXPERTS, NUM_EXPERTS), dtype=jnp.float32)
        return {'hidden_states': hidden_states, 'gate_weight': gate_weight, 'gate_up_proj': gate_up_proj, 'down_proj': down_proj, 'similarity': similarity}
    _L1_ffn_all = _L1_ffn_setup()
    _L1_ffn_in = {k: v for k, v in _L1_ffn_all.items() if k in ('gate_weight', 'gate_up_proj', 'down_proj', 'similarity')}
    del _L1_ffn_all
    return {'x': x, 'ctx_2048': ctx_2048, 'L0_attn_wq_codes': _L0_attn_in['wq_codes'], 'L0_attn_wq_scales': _L0_attn_in['wq_scales'], 'L0_attn_bq': _L0_attn_in['bq'], 'L0_attn_wk_codes': _L0_attn_in['wk_codes'], 'L0_attn_wk_scales': _L0_attn_in['wk_scales'], 'L0_attn_bk': _L0_attn_in['bk'], 'L0_attn_wv_codes': _L0_attn_in['wv_codes'], 'L0_attn_wv_scales': _L0_attn_in['wv_scales'], 'L0_attn_bv': _L0_attn_in['bv'], 'L0_attn_wo_codes': _L0_attn_in['wo_codes'], 'L0_attn_wo_scales': _L0_attn_in['wo_scales'], 'L0_attn_bo': _L0_attn_in['bo'], 'L0_xattn_wq': _L0_xattn_in['wq'], 'L0_xattn_wk': _L0_xattn_in['wk'], 'L0_xattn_wv': _L0_xattn_in['wv'], 'L0_xattn_wo': _L0_xattn_in['wo'], 'L0_xattn_wk_ctx': _L0_xattn_in['wk_ctx'], 'L0_xattn_wv_ctx': _L0_xattn_in['wv_ctx'], 'L0_xattn_q_norm_w': _L0_xattn_in['q_norm_w'], 'L0_xattn_k_norm_w': _L0_xattn_in['k_norm_w'], 'L0_ffn_w_gate': _L0_ffn_in['w_gate'], 'L0_ffn_w_up': _L0_ffn_in['w_up'], 'L0_ffn_w_down': _L0_ffn_in['w_down'], 'L1_attn_Wq': _L1_attn_in['Wq'], 'L1_attn_Wk': _L1_attn_in['Wk'], 'L1_attn_Wv': _L1_attn_in['Wv'], 'L1_attn_Wo': _L1_attn_in['Wo'], 'L1_ffn_gate_weight': _L1_ffn_in['gate_weight'], 'L1_ffn_gate_up_proj': _L1_ffn_in['gate_up_proj'], 'L1_ffn_down_proj': _L1_ffn_in['down_proj'], 'L1_ffn_similarity': _L1_ffn_in['similarity']}

def reference(x, ctx_2048, L0_attn_wq_codes, L0_attn_wq_scales, L0_attn_bq, L0_attn_wk_codes, L0_attn_wk_scales, L0_attn_bk, L0_attn_wv_codes, L0_attn_wv_scales, L0_attn_bv, L0_attn_wo_codes, L0_attn_wo_scales, L0_attn_bo, L0_xattn_wq, L0_xattn_wk, L0_xattn_wv, L0_xattn_wo, L0_xattn_wk_ctx, L0_xattn_wv_ctx, L0_xattn_q_norm_w, L0_xattn_k_norm_w, L0_ffn_w_gate, L0_ffn_w_up, L0_ffn_w_down, L1_attn_Wq, L1_attn_Wk, L1_attn_Wv, L1_attn_Wo, L1_ffn_gate_weight, L1_ffn_gate_up_proj, L1_ffn_down_proj, L1_ffn_similarity):
    import jax
    import jax.numpy as jnp

    def _L0_attn_ref(x, wq_codes, wq_scales, bq, wk_codes, wk_scales, bk, wv_codes, wv_scales, bv, wo_codes, wo_scales, bo):
        import jax, jax.numpy as jnp
        import numpy as np
        BLOCK = 32
        NUM_HEADS = 16
        HEAD_DIM = 128
        FP4_GRID = jnp.array([0.0, 0.5, 1.0, 1.5, 2.0, 3.0, 4.0, 6.0], dtype=jnp.float32)

        def quantize_to_mxfp4(w, block_size=BLOCK):
            D, F = w.shape
            blocks = w.reshape(D // block_size, block_size, F)
            amax = jnp.max(jnp.abs(blocks), axis=1)
            e = jnp.floor(jnp.log2(jnp.maximum(amax, 1e-12) / 6.0))
            scale = jnp.exp2(e)
            v = blocks / scale[:, None, :]
            idx = jnp.argmin(jnp.abs(jnp.abs(v)[..., None] - FP4_GRID), axis=-1)
            codes = jnp.sign(v) * FP4_GRID[idx]
            return (codes.reshape(D, F).astype(jnp.float32), scale.astype(jnp.float32))

        def _mxfp4_matmul(x, codes, scales, block_size=BLOCK):
            w = codes * jnp.repeat(scales, block_size, axis=0)
            return x @ w
        B, S, D = x.shape
        q = _mxfp4_matmul(x, wq_codes, wq_scales) + bq
        k = _mxfp4_matmul(x, wk_codes, wk_scales) + bk
        v = _mxfp4_matmul(x, wv_codes, wv_scales) + bv
        q = q.reshape(B, S, NUM_HEADS, HEAD_DIM)
        k = k.reshape(B, S, NUM_HEADS, HEAD_DIM)
        v = v.reshape(B, S, NUM_HEADS, HEAD_DIM)
        scores = jnp.einsum('bqhd,bkhd->bhqk', q, k) / jnp.sqrt(jnp.float32(HEAD_DIM))
        attn = jax.nn.softmax(scores, axis=-1)
        out = jnp.einsum('bhqk,bkhd->bqhd', attn, v).reshape(B, S, NUM_HEADS * HEAD_DIM)
        return _mxfp4_matmul(out, wo_codes, wo_scales) + bo

    def _L0_xattn_ref(x, h_ctx_kv, wq, wk, wv, wo, wk_ctx, wv_ctx, q_norm_w, k_norm_w):
        import jax, jax.numpy as jnp
        import numpy as np
        HIDDEN = 256
        NUM_HEADS = 16
        NUM_KV_HEADS = 4
        HEAD_DIM = 128
        ROPE_THETA = 10000.0
        EPS = 1e-06

        def rms_norm(x, w, eps=EPS):
            var = jnp.mean(jnp.square(x), axis=-1, keepdims=True)
            return x * jax.lax.rsqrt(var + eps) * w

        def rope_cache(L, head_dim, theta, dtype):
            inv_freq = 1.0 / theta ** (jnp.arange(0, head_dim, 2, dtype=jnp.float32) / head_dim)
            t = jnp.arange(L, dtype=jnp.float32)
            freqs = jnp.outer(t, inv_freq)
            emb = jnp.concatenate([freqs, freqs], -1)
            cos = jnp.cos(emb).astype(dtype)[None, :, None, :]
            sin = jnp.sin(emb).astype(dtype)[None, :, None, :]
            return (cos, sin)

        def rotate_half(x):
            x1, x2 = jnp.split(x, 2, axis=-1)
            return jnp.concatenate([-x2, x1], axis=-1)
        B, L, _ = x.shape
        T = h_ctx_kv.shape[1]
        rep = NUM_HEADS // NUM_KV_HEADS
        q = (x @ wq).reshape(B, L, NUM_HEADS, HEAD_DIM)
        k = (x @ wk).reshape(B, L, NUM_KV_HEADS, HEAD_DIM)
        v = (x @ wv).reshape(B, L, NUM_KV_HEADS, HEAD_DIM)
        q = rms_norm(q, q_norm_w)
        k = rms_norm(k, k_norm_w)
        k_ctx = (h_ctx_kv @ wk_ctx).reshape(B, T, NUM_KV_HEADS, HEAD_DIM)
        v_ctx = (h_ctx_kv @ wv_ctx).reshape(B, T, NUM_KV_HEADS, HEAD_DIM)
        k_ctx = rms_norm(k_ctx, k_norm_w)
        cos, sin = rope_cache(L, HEAD_DIM, ROPE_THETA, x.dtype)
        q = q * cos + rotate_half(q) * sin
        k = k * cos + rotate_half(k) * sin
        k_full = jnp.concatenate([k_ctx, k], axis=1)
        v_full = jnp.concatenate([v_ctx, v], axis=1)
        k_full = jnp.repeat(k_full, rep, axis=2)
        v_full = jnpp_repeat = jnp.repeat(v_full, rep, axis=2)
        i = jnp.arange(L)[:, None]
        j = jnp.arange(L)[None, :]
        causal = jnp.where(j > i, -jnp.inf, 0.0).astype(x.dtype)
        mask = jnp.concatenate([jnp.zeros((L, T), x.dtype), causal], axis=1)
        scale = 1.0 / np.sqrt(HEAD_DIM)
        scores = jnp.einsum('blhd,bmhd->bhlm', q, k_full) * scale + mask
        probs = jax.nn.softmax(scores, axis=-1)
        out = jnp.einsum('bhlm,bmhd->blhd', probs, v_full)
        out = out.reshape(B, L, NUM_HEADS * HEAD_DIM)
        return out @ wo

    def _L0_ffn_ref(x, w_gate, w_up, w_down):
        import jax, jax.numpy as jnp
        import numpy as np

        def _sparsify_2to4(h):
            B, S, I = h.shape
            g = h.reshape(B, S, I // 4, 4)
            a = jnp.abs(g)
            _, idx = jax.lax.top_k(a, 2)
            pos = jnp.arange(4)
            mask = (pos == idx[..., 0:1]) | (pos == idx[..., 1:2])
            return (g * mask.astype(g.dtype)).reshape(B, S, I)
        h = jax.nn.silu(jnp.einsum('bsh,hi->bsi', x, w_gate)) * jnp.einsum('bsh,hi->bsi', x, w_up)
        h_sparse = _sparsify_2to4(h)
        return jnp.einsum('bsi,ih->bsh', h_sparse, w_down)

    def _L1_attn_ref(x, Wq, Wk, Wv, Wo):
        import jax, jax.numpy as jnp
        import numpy as np
        import math
        N_EMBD = 256
        N_HEAD = 16
        RATIO_KV = 4
        N_HEAD_KV = N_HEAD // RATIO_KV
        HEAD_DIM = N_EMBD // N_HEAD

        def alibi_slopes(n_heads):

            def pow2_slopes(n):
                start = 2 ** (-2 ** (-(math.log2(n) - 3)))
                return [start * start ** i for i in range(n)]
            if math.log2(n_heads).is_integer():
                return jnp.array(pow2_slopes(n_heads), dtype=jnp.float32)
            cp2 = 2 ** math.floor(math.log2(n_heads))
            base = pow2_slopes(cp2)
            if n_heads <= 2 * cp2:
                s = base + base[0::2]
            else:
                s = base + base[0::2] + base[1::2]
            return jnp.array(s[:n_heads], dtype=jnp.float32)
        B, T, C = x.shape
        rep = N_HEAD // N_HEAD_KV
        q = (x @ Wq).reshape(B, T, N_HEAD, HEAD_DIM).transpose(0, 2, 1, 3)
        k = (x @ Wk).reshape(B, T, N_HEAD_KV, HEAD_DIM).transpose(0, 2, 1, 3)
        v = (x @ Wv).reshape(B, T, N_HEAD_KV, HEAD_DIM).transpose(0, 2, 1, 3)
        k = jnp.repeat(k, rep, axis=1)
        v = jnp.repeat(v, rep, axis=1)
        scale = 1.0 / math.sqrt(HEAD_DIM)
        att = jnp.einsum('bhqd,bhkd->bhqk', q, k) * scale
        slopes = alibi_slopes(N_HEAD)
        pos = jnp.arange(T)
        rel = pos[None, :] - pos[:, None]
        alibi = slopes[:, None, None] * rel[None, :, :].astype(jnp.float32)
        alibi = jnp.repeat(alibi, rep, axis=0)[:N_HEAD]
        att = att + alibi[None]
        causal = jnp.triu(jnp.full((T, T), -jnp.inf, dtype=jnp.float32), k=1)
        att = att + causal[None, None]
        att = jax.nn.softmax(att.astype(jnp.float32), axis=-1).astype(q.dtype)
        y = jnp.einsum('bhqk,bhkd->bhqd', att, v)
        y = y.transpose(0, 2, 1, 3).reshape(B, T, C)
        return y @ Wo

    def _L1_xattn_ref(qkv, y):
        import math
        import jax, jax.numpy as jnp
        import numpy as np
        N_HEADS = 16
        bs, width, length = qkv.shape
        ch = width // N_HEADS
        q = qkv.reshape(bs * N_HEADS, ch, length)
        k = v = y.reshape(bs * N_HEADS, ch, -1)
        scale = 1.0 / math.sqrt(math.sqrt(ch))
        weight = jnp.einsum('bct,bcs->bts', q * scale, k * scale)
        weight = jax.nn.softmax(weight.astype(jnp.float32), axis=-1).astype(weight.dtype)
        a = jnp.einsum('bts,bcs->bct', weight, v)
        return a.reshape(bs, -1, length)

    def _L1_ffn_ref(hidden_states, gate_weight, gate_up_proj, down_proj, similarity):
        import jax, jax.numpy as jnp
        import numpy as np
        NUM_EXPERTS = 32
        TOP_K = 8
        SELECT_TOP_K = 4
        THRESHOLD = 0.5
        HIDDEN = 256
        D_FF = 96

        def _moe_forward(hidden_states, gate_weight, gate_up_proj, down_proj, similarity):
            B, S_len, H = hidden_states.shape
            E, K, Ssel = (NUM_EXPERTS, TOP_K, SELECT_TOP_K)
            x = hidden_states.reshape(-1, H)
            router_logits = x @ gate_weight.T
            router_probs = jax.nn.softmax(router_logits.astype(jnp.float32), axis=-1).astype(router_logits.dtype)
            router_top_value, router_indices = jax.lax.top_k(router_probs, K)
            routing_weights = router_top_value / jnp.clip(jnp.sum(router_top_value, axis=-1, keepdims=True), 1e-12, None)
            sim = similarity.astype(jnp.float32)
            sim = sim.at[jnp.arange(E), jnp.arange(E)].set(1.0)
            prim = router_indices[:, :Ssel]
            sec = router_indices[:, Ssel:]
            sim_cand = sim[sec[:, :, None], prim[:, None, :]]
            best_sim = jnp.max(sim_cand, axis=-1)
            best_i = jnp.argmax(sim_cand, axis=-1)
            prim_rep = jnp.broadcast_to(prim[:, None, :], sim_cand.shape)
            best_primary = jnp.take_along_axis(prim_rep, best_i[..., None], axis=-1)[..., 0]
            new_sec = jnp.where(best_sim < THRESHOLD, sec, best_primary) if THRESHOLD > 0.0 else best_primary
            rerouted_indices = jnp.concatenate([prim, new_sec], axis=1)
            combine = jnp.sum(jax.nn.one_hot(rerouted_indices, E, dtype=routing_weights.dtype) * routing_weights[..., None], axis=1)

            def expert_step(y, params):
                wgu, wd, cw = params
                gu = x @ wgu.T
                g, u = jnp.split(gu, 2, axis=-1)
                h = jax.nn.silu(g) * u
                y = y + h @ wd.T * cw[:, None]
                return (y, None)
            y0 = jnp.zeros_like(x)
            y, _ = jax.lax.scan(expert_step, y0, (gate_up_proj, down_proj, combine.T))
            return y.reshape(B, S_len, H)
        return _moe_forward(hidden_states, gate_weight, gate_up_proj, down_proj, similarity)
    x = x + _L0_attn_ref(_layernorm(x, axis=-1), L0_attn_wq_codes, L0_attn_wq_scales, L0_attn_bq, L0_attn_wk_codes, L0_attn_wk_scales, L0_attn_bk, L0_attn_wv_codes, L0_attn_wv_scales, L0_attn_bv, L0_attn_wo_codes, L0_attn_wo_scales, L0_attn_bo)
    x = x + _L0_xattn_ref(_layernorm(x, axis=-1), ctx_2048, L0_xattn_wq, L0_xattn_wk, L0_xattn_wv, L0_xattn_wo, L0_xattn_wk_ctx, L0_xattn_wv_ctx, L0_xattn_q_norm_w, L0_xattn_k_norm_w)
    x = x + _L0_ffn_ref(_layernorm(x, axis=-1), L0_ffn_w_gate, L0_ffn_w_up, L0_ffn_w_down)
    x = x + _L1_attn_ref(_layernorm(x, axis=-1), L1_attn_Wq, L1_attn_Wk, L1_attn_Wv, L1_attn_Wo)
    x = x + _L1_xattn_ref(_layernorm(x, axis=-1), ctx_2048)
    x = x + _L1_ffn_ref(_layernorm(x, axis=-1), L1_ffn_gate_weight, L1_ffn_gate_up_proj, L1_ffn_down_proj, L1_ffn_similarity)
    return x

_drawn_inputs = setup_inputs


def setup_inputs(seed=0):
    import zlib

    import numpy as np

    out = dict(_drawn_inputs(seed))
    spreads = {'L0_attn_bq': (0.0, 0.33),
     'L0_attn_bk': (0.0, 0.8),
     'L0_attn_bv': (0.0, 0.1),
     'L0_attn_bo': (0.0, 0.1),
     'L0_xattn_q_norm_w': (1.0, 0.2),
     'L0_xattn_k_norm_w': (1.0, 0.2)}
    factors = {'L1_ffn_gate_weight': 8.0,
     'L1_ffn_gate_up_proj': 8.0,
     'L1_ffn_down_proj': 8.0,
     'L1_ffn_similarity': 8.0}
    for name, (base, spread) in spreads.items():
        noise = np.random.default_rng([zlib.crc32(name.encode()), seed]).standard_normal(out[name].shape)
        drawn = base * np.exp(spread * noise) if base else spread * noise
        out[name] = jnp.asarray(drawn.astype(out[name].dtype))
    for name, factor in factors.items():
        out[name] = (out[name] * factor).astype(out[name].dtype)
    return out
```

```python
import numpy as np
from contextlib import ExitStack, contextmanager
import concourse.bass as bass
from concourse import mybir

F32 = mybir.dt.float32
F16 = mybir.dt.float16
I32 = mybir.dt.int32
BF16 = mybir.dt.bfloat16
ALU = mybir.AluOpType
ACT = mybir.ActivationFunctionType
AX = mybir.AxisListType

P = 128
B, S, D = 32, 64, 256
TOKENS = B * S
KD = D // P
TILES = TOKENS // P
SUBS = 4
STEPS = TILES // SUBS
TOK = SUBS * P
LN_EPS = 1e-5


class Tally:

    def __init__(self, core, name, per):
        self.sem = core.sem(name)
        self.per = per

    def at(self, i, k):
        return i * self.per + (self.per + k)

    def before(self, i, k):
        return i * self.per + k


KB = 1024
AT_BASE = (0, 26 * KB)
AT_ATTN_W, AT_CROSS_W, AT_FFN_W, AT_MOE_W = (125 * KB, 157 * KB), (157 * KB, 205 * KB), (26 * KB, 56 * KB), (125 * KB, 205 * KB)
AT_ATTN, AT_CROSS, AT_FFN, AT_MOE = (26 * KB, 125 * KB), (56 * KB, 157 * KB), (56 * KB, 125 * KB), (26 * KB, 125 * KB)
AT_CHANNEL = (26 * KB, 125 * KB)
CHUNK = 1024


class Region:

    def __init__(self, core, at):
        self.arena, (self.next, self.end) = core.arena, at

    def take(self, shape, dt):
        size = int(np.prod(shape[1:])) * (4 if dt in (F32, I32) else 2)
        size = (size + 31) // 32 * 32
        assert self.next + size <= self.end, (self.next, size, self.end)
        view = self.arena[:, self.next // 4:(self.next + size) // 4]
        if dt != F32:
            view = view.bitcast(dt)
        self.next += size
        view = view[:, 0:int(np.prod(shape[1:]))]
        if len(shape) > 2:
            names = "abcde"[:len(shape) - 1]
            view = view.rearrange(f"p ({' '.join(names)}) -> p {' '.join(names)}", **dict(zip(names, shape[1:])))
        return view[0:shape[0]]


class Core:

    def __init__(self, nc, ctx, ins, out):
        self.nc, self.ctx, self.ins, self.out = nc, ctx, ins, out
        self.sems = []
        self.arena = ctx.enter_context(nc.sbuf_tensor("arena", [P, 205 * KB // 4], F32))
        self.ps = ctx.enter_context(nc.psum_tensor("ps", [P, 8, 512], F32))
        base = Region(self, AT_BASE)
        self.x = base.take([P, TILES, D], F32)
        self.staging = base.take([P, 2, CHUNK], F32)
        self.ident = base.take([P, P], F32)
        self.headmask = base.take([P, 8], F32)
        self.apart = base.take([P, 8], F32)
        self.s_staged = [self.sem("staged0"), self.sem("staged1")]
        self.s_split = self.sem("split")
        self.own = self.sem("split_hi")
        self.passed = self.sem("passed")

    def sem(self, name):
        handle = self.nc.alloc_semaphore(name)
        self.sems.append(handle)
        return handle

    @contextmanager
    def stage(self):
        kept, self.sems = self.sems, []
        yield
        self.nc.clear_and_free_semaphores(self.sems)
        self.sems = kept
        self.nc.all_engine_barrier()


def chunks(src, parts):
    step = min(CHUNK, src.shape[1])
    return [(src[:, c:c + step], *(p[:, c:c + step] for p in parts)) for c in range(0, src.shape[1], step)]


def stage_weights(core, sp, jobs, first):
    for j, (src, hi, lo) in enumerate(jobs, first):
        if j >= 2:
            sp.wait_ge(core.s_split, j - 1)
        core.nc.sync.dma_start(core.staging[0:src.shape[0], j % 2, 0:src.shape[1]], src).then_inc(core.s_staged[j % 2], 16)


def split_weights(core, pool, jobs, first, own):
    nc = core.nc
    for j, (src, hi, lo) in enumerate(jobs, first):
        raw = core.staging[0:src.shape[0], j % 2, 0:src.shape[1]]
        pool.wait_ge(core.s_staged[j % 2], 16 * (j // 2 + 1))
        nc.gpsimd.tensor_copy(hi, raw).then_inc(own, 1)
        pool.wait_ge(own, j + 1)
        nc.gpsimd.tensor_tensor(lo, raw, hi, ALU.subtract).then_inc(core.s_split, 1)
        pool.wait_ge(core.s_split, j + 1)


RSQRT_STEPS = 12


def rsqrt(core, dve, tally, i, k, var, eps, out, tmp):
    nc = core.nc
    v, t, u = (tmp[:, j, 0:out.shape[1]] for j in range(3))
    def step(instruction):
        nonlocal k
        instruction.then_inc(tally.sem, 1)
        k += 1
        dve.wait_ge(tally.sem, tally.at(i, k))
    dve.wait_ge(tally.sem, tally.at(i, k))
    step(nc.vector.tensor_scalar(v, var, eps, None, ALU.add))
    step(nc.vector.tensor_scalar(t.bitcast(I32), v.bitcast(I32), 1, None, ALU.logical_shift_right))
    step(nc.vector.tensor_scalar(out.bitcast(I32), t.bitcast(I32), -1.0, float(0x5F3759DF), ALU.mult, ALU.add))
    for _ in range(3):
        step(nc.vector.scalar_tensor_tensor(out=t, in0=out, scalar=-0.5, in1=v, op0=ALU.mult, op1=ALU.mult))
        step(nc.vector.tensor_tensor(u, t, out, ALU.mult))
        step(nc.vector.scalar_tensor_tensor(out=out, in0=u, scalar=1.5, in1=out, op0=ALU.add, op1=ALU.mult))


def norm_tile(core, dve, stat, i, s, tile, st, mv, rstd, root):
    nc = core.nc
    n = (2 + RSQRT_STEPS) * s
    nc.vector.bn_stats(st[:, :], core.x[:, tile, :]).then_inc(stat.sem, 1)
    dve.wait_ge(stat.sem, stat.at(i, n + 1))
    dve.sem_inc(core.passed, 1)
    nc.vector.bn_aggr(mv[:, :], st[:, :]).then_inc(stat.sem, 1)
    rsqrt(core, dve, stat, i, n + 2, mv[:, 1:2], LN_EPS, rstd[:, :], root)


class Norm:

    def __init__(self, core, name, region):
        self.xn = region.take([P, SUBS, D], F32)
        self.stats = region.take([P, SUBS, 6], F32)
        self.meanvar = region.take([P, SUBS, 2], F32)
        self.rstd = region.take([P, SUBS], F32)
        self.root = region.take([P, 3, SUBS], F32)
        self.xT_hi = region.take([P, KD, TOK], F16)
        self.xT_lo = region.take([P, KD, TOK], F16)
        self.stat = Tally(core, name + "_stat", 2 * SUBS + RSQRT_STEPS)
        self.normed = Tally(core, name + "_xn", SUBS)
        self.turned = Tally(core, name + "_turned", KD)
        self.hi = Tally(core, name + "_hi", KD)
        self.lo = Tally(core, name + "_lo", KD)


def norm_vector(core, n, i, dve):
    nc = core.nc
    for s in range(SUBS):
        nc.vector.bn_stats(n.stats[:, s, :], core.x[:, i * SUBS + s, :]).then_inc(n.stat.sem, 1)
    for s in range(SUBS):
        dve.wait_ge(n.stat.sem, n.stat.at(i, s + 1))
        dve.sem_inc(core.passed, 1)
        nc.vector.bn_aggr(n.meanvar[:, s, :], n.stats[:, s, :]).then_inc(n.stat.sem, 1)
    rsqrt(core, dve, n.stat, i, 2 * SUBS, n.meanvar[:, :, 1], LN_EPS, n.rstd[:, :], n.root)
    dve.wait_ge(n.turned.sem, n.turned.before(i, KD))
    for s in range(SUBS):
        nc.vector.tensor_scalar(n.xn[:, s, :], core.x[:, i * SUBS + s, :], n.meanvar[:, s, 0:1],
                                n.rstd[:, s:s + 1], ALU.subtract, ALU.mult).then_inc(n.normed.sem, 1)


def norm_tensor(core, n, i, pe, banks, free):
    nc = core.nc
    pe.wait_ge(n.normed.sem, n.normed.at(i, SUBS))
    free()
    for k in range(KD):
        for s in range(SUBS):
            last = nc.tensor.transpose(core.ps[:, banks[k], s * P:(s + 1) * P], n.xn[:, s, k * P:(k + 1) * P],
                                       core.ident[:, :])
        last.then_inc(n.turned.sem, 1)


def norm_scalar(core, n, i, act, banks):
    for k in range(KD):
        act.wait_ge(n.turned.sem, n.turned.at(i, k + 1))
        core.nc.scalar.activation(n.xT_hi[:, k, :], core.ps[:, banks[k], :], ACT.Copy).then_inc(n.hi.sem, 1)


def norm_vector_low(core, n, i, dve, banks):
    for k in range(KD):
        dve.wait_ge(n.hi.sem, n.hi.at(i, k + 1))
        core.nc.vector.tensor_tensor(n.xT_lo[:, k, :], core.ps[:, banks[k], :], n.xT_hi[:, k, :],
                                     ALU.subtract).then_inc(n.lo.sem, 1)


def spread(ap, n):
    return ap.unsqueeze(len(ap.shape)).broadcast_to([*ap.shape, n])


def credit(eng, *tallies):
    for t in tallies:
        eng.sem_inc(t.sem, t.per)


def product(nc, out, stationary, moving, start, stop, group=True):
    pairs = [(a, b) for x, a in enumerate(stationary) for y, b in enumerate(moving) if x + y < 2]
    for n, (a, b) in enumerate(pairs):
        last = nc.tensor.matmul(out, a, b, start=start and n == 0, stop=stop and n == len(pairs) - 1,
                                skip_group_check=not group)
    return last



ATTN_HEADS, ATTN_HD = 16, 128
ATTN_FEAT = ATTN_HEADS * ATTN_HD
ATTN_SCALE = 1.0 / float(np.sqrt(ATTN_HD))
ATTN_GROUP = 4
ATTN_BLOCK = 32


class AttnWeights:

    def __init__(self, region):
        self.qkv = region.take([P, 3, KD, ATTN_FEAT], BF16)
        self.out = region.take([P, ATTN_HEADS, D], BF16)


def attn_load(core, w):
    nc = core.nc
    slots = 4
    region = Region(core, AT_ATTN)
    core.bias = region.take([P, 3, ATTN_HEADS], F32)
    core.bo = region.take([P, D], F32)
    codes = region.take([P, slots, CHUNK], F32)
    scales = region.take([P, slots, CHUNK], F32)
    s_small = core.sem("small_loaded")
    s_product = core.sem("weights_made")
    s_raw = [core.sem(f"raw{j}") for j in range(slots)]
    jobs = []
    for c in range(0, ATTN_FEAT, CHUNK):
        for n, name in enumerate("qkv"):
            for k in range(KD):
                jobs.append((core.ins[f"L0_attn_w{name}_codes"][k * P:(k + 1) * P, c:c + CHUNK],
                             core.ins[f"L0_attn_w{name}_scales"][k * 4:(k + 1) * 4, c:c + CHUNK], w.qkv[:, n, k, c:c + CHUNK]))
    per = CHUNK // D
    for t in range(0, ATTN_HEADS, per):
        jobs.append((core.ins["L0_attn_wo_codes"].rearrange("(t p) d -> p t d", p=P)[:, t:t + per, :],
                     core.ins["L0_attn_wo_scales"].rearrange("(t b) d -> b t d", b=4)[:, t:t + per, :],
                     w.out[:, t:t + per, :]))
    with nc.Block() as block:
        @block.sync
        def _(sp):
            sp.dma_start(core.x[:, :, :], core.ins["x"].rearrange("(t p) d -> p t d", p=P)).then_inc(s_small, 16)
            sp.dma_start(core.ident[:, :], core.ins["ident"]).then_inc(s_small, 16)
            sp.dma_start(core.headmask, core.ins["headmask"]).then_inc(s_small, 16)
            for n, name in enumerate("qkv"):
                sp.dma_start(core.bias[:, n, :], core.ins[f"L0_attn_b{name}"]).then_inc(s_small, 16)
            sp.dma_start(core.bo[:, :], core.ins["L0_attn_bo"]).then_inc(s_small, 16)
            for j, (src, sc, dst) in enumerate(jobs):
                if j >= slots:
                    sp.wait_ge(s_product, j - slots + 1)
                to, ts = codes[:, j % slots, :], scales[:, j % slots, :]
                if len(src.shape) == 3:
                    to, ts = (q.rearrange("p (t d) -> p t d", d=D) for q in (to, ts))
                sp.dma_start(to, src).then_inc(s_raw[j % slots], 16)
                for b in range(4):
                    sp.dma_start(ts[b * ATTN_BLOCK:(b + 1) * ATTN_BLOCK], sc[b].partition_broadcast(ATTN_BLOCK)).then_inc(s_raw[j % slots], 16)
            sp.wait_ge(s_small, 16 * 7)

        @block.vector
        def _(dve):
            for j, (src, sc, dst) in enumerate(jobs):
                dve.wait_ge(s_raw[j % slots], 80 * (j // slots + 1))
                a, b = codes[:, j % slots, :], scales[:, j % slots, :]
                if len(src.shape) == 3:
                    a, b = (t.rearrange("p (t d) -> p t d", d=D) for t in (a, b))
                nc.vector.tensor_tensor(dst, a, b, ALU.mult).then_inc(s_product, 1)


def attn_stage(core, w, jobs=(), first=0):
    nc, ps = core.nc, core.ps
    Q, K, V, SC, T, O, A = 0, 1, 2, 3, 4, 5, (6, 7)
    LN = (SC, T)
    region = Region(core, AT_ATTN)
    region.take([P, 3, ATTN_HEADS], F32), region.take([P, D], F32)
    n = Norm(core, "attn", region)
    tally = lambda name, per: Tally(core, "attn_" + name, per)
    q_ready, k_ready, v_ready = (tally(f"{c}_ready", ATTN_HEADS) for c in "qkv")
    q_kept, v_kept = tally("q_kept", ATTN_HEADS), tally("v_kept", ATTN_HEADS)
    k_kept = tally("k_kept", ATTN_HEADS)
    scored = tally("scored", ATTN_HEADS)
    maxed, shifted, summed, inverse = (tally(c, ATTN_HEADS) for c in ("maxed", "shifted", "summed", "inverse"))
    exped = tally("exped", ATTN_HEADS)
    probs = tally("probs", 2 * ATTN_HEADS)
    turned = tally("probs_turned", ATTN_HEADS)
    pT_kept = tally("pT_kept", ATTN_HEADS)
    mixed = tally("mixed", ATTN_HEADS)
    o_hi = tally("o_hi", ATTN_HEADS)
    o_lo = tally("o_lo", ATTN_HEADS)
    projected = tally("projected", ATTN_HEADS)
    added = tally("added", 2 * SUBS)
    cleared = core.sem("attn_cleared")
    with ExitStack() as own:
        def sb(name, shape, dt):
            return region.take(shape, dt)
        qT = sb("qT", [P, 2, TOK], F32)
        kT = sb("kT", [P, 2, TOK], F32)
        v = sb("v", [P, 3, SUBS, ATTN_GROUP * ATTN_HD], F32)
        top = sb("top", [P, 2, SUBS], F32)
        total = sb("total", [P, 2, SUBS], F32)
        inv = sb("inv", [P, 2, SUBS], F32)
        shift = sb("shift", [P, 2, SUBS, S], F32)
        e = sb("e", [P, 2, SUBS, S], F32)
        prob = sb("prob", [P, 2, SUBS, P], F32)
        pT = sb("pT", [P, 2, TOK], F32)
        oT = [sb(f"oT{p}", [P, 2, TOK], F16) for p in range(2)]
        scores = ps[:, SC, :].rearrange("p (b s k) -> p b s k", b=2, k=S)
        block = own.enter_context(nc.Block())

        @block.sync
        def _(sp):
            stage_weights(core, sp, jobs, first)

        @block.tensor
        def _(pe):
            credit(pe, n.turned, q_ready, k_ready, v_ready, scored, turned, mixed, projected)

            def free():
                pe.wait_ge(shifted.sem, shifted.at(i, 0))
                pe.wait_ge(pT_kept.sem, pT_kept.at(i, 0))

            def values(g, s):
                c = g * ATTN_GROUP + s + 1
                pe.wait_ge(v_kept.sem, v_kept.at(i, c - 1))
                for k in range(KD):
                    last = product(nc, ps[:, V, :], [t[:, k, s * P:(s + 1) * P] for t in (n.xT_hi, n.xT_lo)],
                                   [w.qkv[:, 2, k, g * ATTN_GROUP * ATTN_HD:(g + 1) * ATTN_GROUP * ATTN_HD]], k == 0, k == KD - 1)
                last.then_inc(v_ready.sem, 1)

            def project(h):
                for c, bank, kept, ready in ((0, Q, q_kept, q_ready), (1, K, k_kept, k_ready)):
                    pe.wait_ge(kept.sem, kept.at(i, h))
                    for k in range(KD):
                        last = product(nc, ps[:, bank, :], [w.qkv[:, c, k, h * ATTN_HD:(h + 1) * ATTN_HD]],
                                       [n.xT_hi[:, k, :], n.xT_lo[:, k, :]], k == 0, k == KD - 1)
                    last.then_inc(ready.sem, 1)

            def score(h):
                pe.wait_ge(q_kept.sem, q_kept.at(i, h + 1))
                pe.wait_ge(k_kept.sem, k_kept.at(i, h + 1))
                pe.wait_ge(shifted.sem, shifted.at(i, h))
                for s in range(SUBS):
                    for b in range(2):
                        c = s * P + b * S
                        last = nc.tensor.matmul(scores[b * S:(b + 1) * S, h % 2, s, :], qT[:, h % 2, c:c + S],
                                                kT[:, h % 2, c:c + S], start=True, stop=True)
                last.then_inc(scored.sem, 1)

            def turn(h):
                pe.wait_ge(probs.sem, probs.at(i, 2 * h + 2))
                pe.wait_ge(pT_kept.sem, pT_kept.at(i, h))
                for s in range(SUBS):
                    last = nc.tensor.transpose(ps[:, T, s * P:(s + 1) * P], prob[:, h % 2, s, :], core.ident[:, :])
                last.then_inc(turned.sem, 1)

            def mix(h):
                pe.wait_ge(pT_kept.sem, pT_kept.at(i, h + 1))
                pe.wait_ge(v_kept.sem, v_kept.at(i, (h // ATTN_GROUP + 1) * ATTN_GROUP))
                pe.wait_ge(o_lo.sem, o_lo.at(i, h))
                for s in range(SUBS):
                    last = nc.tensor.matmul(ps[:, O, s * P:(s + 1) * P], v[:, h // ATTN_GROUP % 3, s, h % ATTN_GROUP * ATTN_HD:(h % ATTN_GROUP + 1) * ATTN_HD],
                                            pT[:, h % 2, s * P:(s + 1) * P], start=True, stop=True)
                last.then_inc(mixed.sem, 1)

            def out(h):
                pe.wait_ge(o_hi.sem, o_hi.at(i, h + 1))
                pe.wait_ge(o_lo.sem, o_lo.at(i, h + 1))
                if h == 0:
                    pe.wait_ge(added.sem, added.at(i, 0))
                for s in range(SUBS):
                    last = product(nc, ps[:, A[s // 2], s % 2 * D:(s % 2 + 1) * D], [t[:, h % 2, s * P:(s + 1) * P] for t in oT],
                                   [w.out[:, h, :]], h == 0 and s % 2 == 0, h == ATTN_HEADS - 1, group=False)
                last.then_inc(projected.sem, 1)

            with pe.Fori(0, STEPS) as i:
                norm_tensor(core, n, i, pe, LN, free)
                pe.wait_ge(n.hi.sem, n.hi.at(i, KD))
                pe.wait_ge(n.lo.sem, n.lo.at(i, KD))
                for s in range(SUBS):
                    values(0, s)
                for t in range(ATTN_HEADS + 4):
                    if t < ATTN_HEADS:
                        project(t)
                    if 1 <= t < ATTN_HEADS + 1:
                        score(t - 1)
                    if t < ATTN_HEADS - ATTN_GROUP:
                        values(t // ATTN_GROUP + 1, t % ATTN_GROUP)
                    if 3 <= t < ATTN_HEADS + 3:
                        mix(t - 3)
                    if 2 <= t < ATTN_HEADS + 2:
                        turn(t - 2)
                    if t >= 4:
                        out(t - 4)

        @block.scalar
        def _(act):
            credit(act, n.hi, q_kept, v_kept, exped, pT_kept, o_hi)
            with act.Fori(0, STEPS) as i:
                norm_scalar(core, n, i, act, LN)

                def keep_v(g, s):
                    c = g * ATTN_GROUP + s + 1
                    act.wait_ge(v_ready.sem, v_ready.at(i, c))
                    act.wait_ge(mixed.sem, mixed.at(i, max(g - 2, 0) * ATTN_GROUP))
                    nc.scalar.activation(v[:, g % 3, s, :], ps[:, V, :], ACT.Copy).then_inc(v_kept.sem, 1)

                for s in range(SUBS):
                    keep_v(0, s)
                for t in range(ATTN_HEADS + 4):
                    if t < ATTN_HEADS:
                        h = t
                        act.wait_ge(q_ready.sem, q_ready.at(i, h + 1))
                        act.wait_ge(scored.sem, scored.at(i, h - 1))
                        nc.scalar.activation(qT[:, h % 2, :], ps[:, Q, :], ACT.Identity, bias=core.bias[:, 0, h:h + 1]).then_inc(q_kept.sem, 1)
                    if 3 <= t < ATTN_HEADS + 3:
                        h = t - 3
                        act.wait_ge(mixed.sem, mixed.at(i, h + 1))
                        act.wait_ge(projected.sem, projected.at(i, h - 1))
                        nc.scalar.activation(oT[0][:, h % 2, :], ps[:, O, :], ACT.Identity, bias=core.bias[:, 2, h:h + 1]).then_inc(o_hi.sem, 1)
                    if 2 <= t < ATTN_HEADS + 2:
                        h = t - 2
                        act.wait_ge(turned.sem, turned.at(i, h + 1))
                        act.wait_ge(mixed.sem, mixed.at(i, h - 1))
                        nc.scalar.activation(pT[:, h % 2, :], ps[:, T, :], ACT.Copy).then_inc(pT_kept.sem, 1)
                    if 1 <= t < ATTN_HEADS + 1:
                        h = t - 1
                        act.wait_ge(shifted.sem, shifted.at(i, h + 1))
                        act.wait_ge(probs.sem, probs.at(i, 2 * h - 2))
                        nc.scalar.activation(e[:, h % 2], shift[:, h % 2], ACT.Exp, scale=ATTN_SCALE).then_inc(exped.sem, 1)
                    if t < ATTN_HEADS - ATTN_GROUP:
                        keep_v(t // ATTN_GROUP + 1, t % ATTN_GROUP)

        @block.vector
        def _(dve):
            credit(dve, n.stat, n.normed, n.lo, k_kept, maxed, shifted, summed, inverse, o_lo, added)
            with dve.Fori(0, STEPS) as i:
                norm_vector(core, n, i, dve)
                norm_vector_low(core, n, i, dve, LN)
                for t in range(ATTN_HEADS + 4):
                    if t < ATTN_HEADS:
                        h = t
                        dve.wait_ge(k_ready.sem, k_ready.at(i, h + 1))
                        dve.wait_ge(scored.sem, scored.at(i, h - 1))
                        nc.vector.tensor_scalar(kT[:, h % 2, :], ps[:, K, :], core.bias[:, 1, h:h + 1], None, ALU.add).then_inc(k_kept.sem, 1)
                    if 1 <= t < ATTN_HEADS + 1:
                        h = t - 1
                        dve.wait_ge(scored.sem, scored.at(i, h + 1))
                        nc.vector.tensor_reduce(top[:, h % 2, :], scores[:, h % 2], AX.X, ALU.max).then_inc(maxed.sem, 1)
                        dve.wait_ge(maxed.sem, maxed.at(i, h + 1))
                        dve.wait_ge(exped.sem, exped.at(i, h - 1))
                        nc.vector.tensor_tensor(shift[:, h % 2], scores[:, h % 2], spread(top[:, h % 2, :], S), ALU.subtract).then_inc(shifted.sem, 1)
                    if 3 <= t < ATTN_HEADS + 3:
                        h = t - 3
                        dve.wait_ge(o_hi.sem, o_hi.at(i, h + 1))
                        nc.vector.scalar_tensor_tensor(out=oT[1][:, h % 2, :], in0=ps[:, O, :], scalar=core.bias[:, 2, h:h + 1],
                                                       in1=oT[0][:, h % 2, :], op0=ALU.add, op1=ALU.subtract).then_inc(o_lo.sem, 1)
                    if 1 <= t < ATTN_HEADS + 1:
                        h = t - 1
                        dve.wait_ge(exped.sem, exped.at(i, h + 1))
                        dve.wait_ge(probs.sem, probs.at(i, 2 * h - 2))
                        nc.vector.tensor_reduce(total[:, h % 2, :], e[:, h % 2], AX.X, ALU.add).then_inc(summed.sem, 1)
                        dve.wait_ge(summed.sem, summed.at(i, h + 1))
                        nc.vector.reciprocal(inv[:, h % 2, :], total[:, h % 2, :]).then_inc(inverse.sem, 1)
                dve.wait_ge(projected.sem, projected.at(i, ATTN_HEADS))
                for s in range(SUBS):
                    xs = core.x[:, i * SUBS + s, :]
                    nc.vector.tensor_tensor(xs, ps[:, A[s // 2], s % 2 * D:(s % 2 + 1) * D], xs, ALU.add).then_inc(added.sem, 1)
                for s in range(SUBS):
                    dve.wait_ge(added.sem, added.at(i, s + 1))
                    xs = core.x[:, i * SUBS + s, :]
                    nc.vector.tensor_tensor(xs, xs, core.bo[:, :], ALU.add).then_inc(added.sem, 1)
                dve.wait_ge(added.sem, added.at(i, 2 * SUBS))

        @block.gpsimd
        def _(pool):
            credit(pool, probs)
            nc.gpsimd.memset(prob[:, :, :, :], 0.0).then_inc(cleared, 1)
            pool.wait_ge(cleared, 1)
            for i in range(STEPS):
                for h in range(ATTN_HEADS):
                    pool.wait_ge(inverse.sem, inverse.at(i, h + 1))
                    pool.wait_ge(turned.sem, turned.at(i, h - 1))
                    for b in range(2):
                        r = slice(b * S, (b + 1) * S)
                        nc.gpsimd.tensor_tensor(prob[r, h % 2, :, b * S:(b + 1) * S], e[r, h % 2], spread(inv[r, h % 2, :], S),
                                                ALU.mult).then_inc(probs.sem, 1)
                a, b = len(jobs) * i // STEPS, len(jobs) * (i + 1) // STEPS
                pool.wait_ge(probs.sem, probs.at(i, 2 * ATTN_HEADS))
                split_weights(core, pool, jobs[a:b], first + a, core.own)



CROSS_HEADS, CROSS_KVH, CROSS_HD = 16, 4, 128
CROSS_REP = CROSS_HEADS // CROSS_KVH
CROSS_GW = CROSS_REP * CROSS_HD
CROSS_SCALE = 1.0 / float(np.sqrt(CROSS_HD))
CROSS_RMS_EPS = 1e-6
CROSS_UNITS = SUBS * CROSS_KVH
CROSS_TURNS = 2 + CROSS_KVH
CROSS_NORMS = 2 * CROSS_KVH + CROSS_HEADS
CROSS_KEYS = 2 * S


class CrossWeights:
    def __init__(self, region):
        self.q = [region.take([P, KD, CROSS_HEADS * CROSS_HD], F16) for p in range(2)]
        self.kv = [region.take([P, 4, KD, CROSS_KVH * CROSS_HD], F16) for p in range(2)]
        self.out = [region.take([P, CROSS_HEADS, D], F16) for p in range(2)]

    def jobs(self, core):
        out = []
        for k in range(KD):
            out += chunks(core.ins["L0_xattn_wq"][k * P:(k + 1) * P, :], [q[:, k, :] for q in self.q])
        for n, name in enumerate(("wk_ctx", "wk", "wv_ctx", "wv")):
            for k in range(KD):
                out += chunks(core.ins["L0_xattn_" + name][k * P:(k + 1) * P, :], [q[:, n, k, :] for q in self.kv])
        for t in range(CROSS_HEADS):
            out += chunks(core.ins["L0_xattn_wo"][t * P:(t + 1) * P, :], [q[:, t, :] for q in self.out])
        return out


def steps(engine, body):
    body(0, lambda k: k >= 0)
    with engine.Fori(1, STEPS) as i:
        body(i, lambda k: True)
    body(STEPS, lambda k: k < 0)


def cross_stage(core, w, jobs=(), first=0):
    nc, ps = core.nc, core.ps
    QP, KVP, TQ, SC, PT, O, ACC, LNB = range(8)
    tally = lambda name, per: Tally(core, "x_" + name, per)
    stat = tally("stat", SUBS * (2 + RSQRT_STEPS))
    xn = tally("xn", SUBS)
    xn_turned = tally("xn_turned", SUBS)
    x_hi = tally("x_hi", SUBS)
    x_lo = tally("x_lo", SUBS)
    c_hi, c_lo = tally("c_hi", SUBS), tally("c_lo", SUBS)
    kv_ready, q_ready = tally("kv_ready", CROSS_UNITS), tally("q_ready", CROSS_UNITS)
    kv_kept, q_kept = tally("kv_kept", CROSS_UNITS), tally("q_kept", CROSS_UNITS)
    squared = tally("squared", SUBS * CROSS_TURNS)
    summed = tally("summed", SUBS * CROSS_TURNS)
    rooted = tally("rooted", SUBS * RSQRT_STEPS)
    roped = tally("roped", SUBS * CROSS_TURNS)
    joined = tally("joined", SUBS * CROSS_TURNS)
    scaled = tally("scaled", SUBS * CROSS_TURNS)
    turned, turn_kept = tally("turned", SUBS * CROSS_TURNS), tally("turn_kept", SUBS * CROSS_TURNS)
    scored = tally("scored", CROSS_UNITS)
    maxed, shifted, totalled, inverse = (tally(c, CROSS_UNITS) for c in ("maxed", "shifted", "totalled", "inverse"))
    exped = tally("exped", CROSS_UNITS)
    probs = tally("probs", CROSS_UNITS)
    p_turned, pT_kept = tally("p_turned", CROSS_UNITS), tally("pT_kept", CROSS_UNITS)
    mixed, o_hi, o_lo = tally("mixed", CROSS_UNITS), tally("o_hi", CROSS_UNITS), tally("o_lo", CROSS_UNITS)
    projected = tally("projected", CROSS_UNITS)
    added = tally("added", SUBS)
    s_ctx = [core.sem("x_ctx0"), core.sem("x_ctx1")]
    s_const, s_tables = core.sem("x_const"), core.sem("x_tables")
    L_TURN, L_PROJ, L_ROPE, L_FLIP, L_SCORE, L_PROB, L_PTURN, L_MIX, L_OUT = 1, 4, 8, 9, 10, 11, 12, 13, 14
    region = Region(core, AT_CROSS)
    with ExitStack() as own:
        def sb(name, shape, dt):
            return region.take(shape, dt)
        xT = [sb(f"xT{p}", [P, 2, KD, P], F16) for p in range(2)]
        cT = [sb(f"cT{p}", [P, 2, KD, P], F16) for p in range(2)]
        xnorm = sb("xnorm", [P, 2, D], F32)
        st, mv, rstd, root = sb("st", [P, 6], F32), sb("mv", [P, 2], F32), sb("rstd", [P, 1], F32), sb("root", [P, 3, CROSS_NORMS], F32)
        qs = sb("qs", [P, CROSS_KVH, CROSS_GW], F32)
        ks = sb("ks", [P, 2, CROSS_KVH * CROSS_HD], F32)
        cRaw = sb("cRaw", [P, 2, KD, P], F32)
        v = sb("v", [P, SUBS, 2, CROSS_KVH * CROSS_HD], F32)
        square = sb("square", [P, 2, CROSS_GW], F32)
        sums, rms = sb("sums", [P, 2, CROSS_NORMS], F32), sb("rms", [P, 2, CROSS_NORMS], F32)
        ropeA, ropeB = sb("ropeA", [P, 4, CROSS_GW], F32), sb("ropeB", [P, 2, CROSS_GW], F32)
        kT = sb("kT", [P, 2, CROSS_KVH, 2, CROSS_KEYS], F32)
        qT = sb("qT", [P, 2, 2, CROSS_REP * S], F32)
        top, total, inv = (sb(c, [P, 2, 4], F32) for c in ("top", "total", "inv"))
        shift, prob = (sb(c, [P, 2, 4, CROSS_KEYS], F32) for c in ("shift", "prob"))
        e = shift
        pT = sb("pT", [P, 2, 2, CROSS_REP * S], F32)
        oT = [sb(f"oT{p}", [P, 2, CROSS_REP, P], F16) for p in range(2)]
        raw = sb("raw", [P, 4, CROSS_HD], F32)
        table = sb("table", [P, 2, 2, CROSS_HD], F32)
        mask = sb("mask", [P, 4, CROSS_KEYS], BF16)
        maskf = sb("maskf", [P, CROSS_KEYS], F32)
        ident = sb("ident", [P, P], BF16)
        block = own.enter_context(nc.Block())

        def turns_at(g):
            return [0, 1, 2] if g == 0 else [g + 2]

        def unit(t, lag):
            k = t - lag
            return k, k // CROSS_KVH, k % CROSS_KVH

        @block.sync
        def _(sp):
            for n, name in enumerate(("cos", "sin", "L0_xattn_q_norm_w", "L0_xattn_k_norm_w")):
                sp.dma_start(raw[:, n, :], core.ins[name]).then_inc(s_const, 16)
            sp.dma_start(maskf[:, :], core.ins["mask"]).then_inc(s_const, 16)
            stage_weights(core, sp, jobs, first)

        @block.tensor
        def _(pe):
            credit(pe, xn_turned, kv_ready, q_ready, turned, scored, p_turned, mixed, projected)

            def body(i, alive):
                for t in range(CROSS_UNITS):
                    k, s, g = unit(t, L_TURN)
                    if alive(k) and g == 0:
                        pe.wait_ge(xn.sem, xn.at(i, s + 1))
                        pe.wait_ge(x_lo.sem, x_lo.at(i, s))
                        for c in range(KD):
                            last = nc.tensor.transpose(ps[:, LNB, c * P:(c + 1) * P], xnorm[:, s % 2, c * P:(c + 1) * P], core.ident[:, :])
                        last.then_inc(xn_turned.sem, 1)
                    k, s, g = unit(t, L_PROJ)
                    if alive(k):
                        src = cT if g % 2 == 0 else xT
                        if g == 0:
                            pe.wait_ge(c_lo.sem, c_lo.at(i, s + 1))
                            pe.wait_ge(x_lo.sem, x_lo.at(i, s + 1))
                        pe.wait_ge(kv_kept.sem, kv_kept.at(i, k))
                        for c in range(KD):
                            last = product(nc, ps[:, KVP, :], [q[:, s % 2, c, :] for q in src], [q[:, g, c, :] for q in w.kv], c == 0, c == KD - 1)
                        last.then_inc(kv_ready.sem, 1)
                        pe.wait_ge(q_kept.sem, q_kept.at(i, k))
                        pe.wait_ge(squared.sem, squared.at(i, CROSS_TURNS * s + min(g, 2) + g))
                        for c in range(KD):
                            last = product(nc, ps[:, QP, :], [q[:, s % 2, c, :] for q in xT], [q[:, c, g * CROSS_GW:(g + 1) * CROSS_GW] for q in w.q], c == 0, c == KD - 1)
                        last.then_inc(q_ready.sem, 1)
                    k, s, g = unit(t, L_SCORE)
                    if alive(k):
                        pe.wait_ge(turn_kept.sem, turn_kept.at(i, CROSS_TURNS * s + g + 3))
                        pe.wait_ge(shifted.sem, shifted.at(i, k))
                        nc.tensor.matmul(ps[:, SC, :], ident[:, :], mask[:, :, :].rearrange("p a b -> p (a b)"), start=True, stop=False, skip_group_check=True)
                        for b in range(2):
                            for r in range(2):
                                c = b * 2 + r
                                last = nc.tensor.matmul(ps[:, SC, c * CROSS_KEYS:(c + 1) * CROSS_KEYS], qT[:, k % 2, b, r * P:(r + 1) * P],
                                                        kT[:, s % 2, g, b, :], start=False, stop=True, skip_group_check=True)
                        last.then_inc(scored.sem, 1)
                    k, s, g = unit(t, L_MIX)
                    if alive(k):
                        pe.wait_ge(pT_kept.sem, pT_kept.at(i, k + 1))
                        pe.wait_ge(o_lo.sem, o_lo.at(i, k))
                        for b in range(2):
                            last = nc.tensor.matmul(ps[:, O, b * CROSS_REP * S:(b + 1) * CROSS_REP * S], v[:, s % SUBS, b, g * CROSS_HD:(g + 1) * CROSS_HD],
                                                    pT[:, k % 2, b, :], start=True, stop=True)
                        last.then_inc(mixed.sem, 1)
                    k, s, g = unit(t, L_PTURN)
                    if alive(k):
                        pe.wait_ge(probs.sem, probs.at(i, k + 1))
                        pe.wait_ge(pT_kept.sem, pT_kept.at(i, k))
                        for c in range(4):
                            last = nc.tensor.transpose(ps[:, PT, c * P:(c + 1) * P], prob[:, k % 2, c, :], core.ident[:, :])
                        last.then_inc(p_turned.sem, 1)
                    k, s, g = unit(t, L_FLIP)
                    if alive(k):
                        for u in turns_at(g):
                            n = CROSS_TURNS * s + u
                            pe.wait_ge(scaled.sem, scaled.at(i, n + 1))
                            pe.wait_ge(turn_kept.sem, turn_kept.at(i, n))
                            for r in range(CROSS_REP):
                                last = nc.tensor.transpose(ps[:, TQ, r * P:(r + 1) * P], ropeA[:, n % 4, r * CROSS_HD:(r + 1) * CROSS_HD], core.ident[:, :])
                            last.then_inc(turned.sem, 1)
                    k, s, g = unit(t, L_OUT)
                    if alive(k):
                        pe.wait_ge(o_lo.sem, o_lo.at(i, k + 1))
                        if g == 0:
                            pe.wait_ge(added.sem, added.at(i, s))
                        for r in range(CROSS_REP):
                            last = product(nc, ps[:, ACC, 0:D], [q[:, k % 2, r, :] for q in oT], [q[:, g * CROSS_REP + r, :] for q in w.out],
                                           g == 0 and r == 0, g == CROSS_KVH - 1 and r == CROSS_REP - 1)
                        last.then_inc(projected.sem, 1)

            pe.wait_ge(s_tables, 1)
            steps(pe, body)

        @block.scalar
        def _(act):
            credit(act, x_hi, kv_kept, q_kept, squared, turn_kept, exped, pT_kept, o_hi)


            def body(i, alive):
                for t in range(CROSS_UNITS):
                    k, s, g = unit(t, L_TURN)
                    if alive(k) and g == 0:
                        act.wait_ge(xn_turned.sem, xn_turned.at(i, s + 1))
                        act.wait_ge(q_ready.sem, q_ready.at(i, CROSS_KVH * (s - 1)))
                        nc.scalar.activation(xT[0][:, s % 2], ps[:, LNB, 0:D].rearrange("p (c q) -> p c q", c=KD), ACT.Copy).then_inc(x_hi.sem, 1)
                    k, s, g = unit(t, L_PROJ)
                    if alive(k):
                        act.wait_ge(kv_ready.sem, kv_ready.at(i, k + 1))
                        if g < 2:
                            n = CROSS_TURNS * s + 2 * g
                            act.wait_ge(roped.sem, roped.at(i, CROSS_TURNS * (s - 1) + g + 1))
                            nc.scalar.activation(ks[:, g, :], ps[:, KVP, :], ACT.Copy)
                            act.wait_ge(summed.sem, summed.at(i, n - 1))
                            nc.scalar.activation(square[:, n % 2, :], ps[:, KVP, :], ACT.Square, scale=CROSS_SCALE).then_inc(squared.sem, 1)
                            act.wait_ge(squared.sem, squared.at(i, n + 1))
                            act.sem_inc(kv_kept.sem, 1)
                        else:
                            half = g - 2
                            act.wait_ge(mixed.sem, mixed.at(i, CROSS_KVH * (s - 3)))
                            nc.scalar.activation(v[half * S:(half + 1) * S, s % SUBS, 0, :], ps[0:S, KVP, :], ACT.Copy)
                            nc.scalar.activation(v[half * S:(half + 1) * S, s % SUBS, 1, :], ps[S:P, KVP, :], ACT.Copy).then_inc(kv_kept.sem, 1)
                        act.wait_ge(q_ready.sem, q_ready.at(i, k + 1))
                        n = CROSS_TURNS * s + min(g + 1, 2) + g
                        act.wait_ge(roped.sem, roped.at(i, CROSS_TURNS * (s - 1) + g + 3))
                        nc.scalar.activation(qs[:, g, :], ps[:, QP, :], ACT.Copy).then_inc(q_kept.sem, 1)
                        act.wait_ge(summed.sem, summed.at(i, n - 1))
                        nc.scalar.activation(square[:, n % 2, :], ps[:, QP, :], ACT.Square, scale=CROSS_SCALE).then_inc(squared.sem, 1)
                    k, s, g = unit(t, L_SCORE)
                    if alive(k):
                        act.wait_ge(shifted.sem, shifted.at(i, k + 1))
                        act.wait_ge(probs.sem, probs.at(i, k - 1))
                        nc.scalar.activation(e[:, k % 2], shift[:, k % 2], ACT.Exp, scale=CROSS_SCALE).then_inc(exped.sem, 1)
                    k, s, g = unit(t, L_MIX)
                    if alive(k):
                        act.wait_ge(mixed.sem, mixed.at(i, k + 1))
                        act.wait_ge(projected.sem, projected.at(i, k - 1))
                        nc.scalar.activation(oT[0][:, k % 2].rearrange("p r (b q) -> p b r q", b=2),
                                             ps[:, O, :].rearrange("p (b r q) -> p b r q", b=2, r=CROSS_REP), ACT.Copy).then_inc(o_hi.sem, 1)
                    k, s, g = unit(t, L_PTURN)
                    if alive(k):
                        act.wait_ge(p_turned.sem, p_turned.at(i, k + 1))
                        act.wait_ge(mixed.sem, mixed.at(i, k - 1))
                        nc.scalar.activation(pT[:, k % 2], ps[:, PT, :].rearrange("p (b n) -> p b n", b=2), ACT.Copy).then_inc(pT_kept.sem, 1)
                    k, s, g = unit(t, L_FLIP)
                    if alive(k):
                        for u in turns_at(g):
                            n = CROSS_TURNS * s + u
                            act.wait_ge(turned.sem, turned.at(i, n + 1))
                            if u < 2:
                                act.wait_ge(scored.sem, scored.at(i, CROSS_KVH * (s - 1)))
                                nc.scalar.activation(kT[:, s % 2, :, :, u * S:(u + 1) * S],
                                                     ps[:, TQ, :].rearrange("p (g b m) -> p g b m", g=CROSS_KVH, b=2), ACT.Copy).then_inc(turn_kept.sem, 1)
                            else:
                                act.wait_ge(scored.sem, scored.at(i, k - 1))
                                nc.scalar.activation(qT[:, k % 2].rearrange("p b (r q) -> p r b q", r=CROSS_REP),
                                                     ps[:, TQ, :].rearrange("p (r b q) -> p r b q", r=CROSS_REP, b=2), ACT.Copy).then_inc(turn_kept.sem, 1)

            steps(act, body)

        @block.vector
        def _(dve):
            credit(dve, stat, xn, x_lo, summed, rooted, roped, maxed, shifted, totalled, inverse, o_lo, added)
            dve.wait_ge(s_const, 80)
            half = CROSS_HD // 2
            for n in range(2):
                nc.vector.tensor_tensor(table[:, n, 0, :], raw[:, 0, :], raw[:, 2 + n, :], ALU.mult)
                for a, b in ((0, half), (half, 0)):
                    nc.vector.tensor_tensor(table[:, n, 1, a:a + half], raw[:, 1, a:a + half], raw[:, 2 + n, b:b + half], ALU.mult)
            nc.vector.tensor_copy(ident[:, :], core.ident[:, :])
            nc.vector.tensor_copy(mask[:, :, :], maskf[:, :].unsqueeze(1).broadcast_to([P, 4, CROSS_KEYS]))
            dve.drain().then_inc(s_tables, 1)
            dve.wait_ge(s_tables, 1)

            def body(i, alive):
                for t in range(CROSS_UNITS):
                    k, s, g = unit(t, 0)
                    if alive(k) and g == 0:
                        n = (2 + RSQRT_STEPS) * s
                        tile = i * SUBS + s
                        nc.vector.bn_stats(st[:, :], core.x[:, tile, :]).then_inc(stat.sem, 1)
                        dve.wait_ge(stat.sem, stat.at(i, n + 1))
                        dve.sem_inc(core.passed, 1)
                        nc.vector.bn_aggr(mv[:, :], st[:, :]).then_inc(stat.sem, 1)
                        rsqrt(core, dve, stat, i, n + 2, mv[:, 1:2], LN_EPS, rstd[:, :], root)
                        dve.wait_ge(xn_turned.sem, xn_turned.at(i, s - 1))
                        nc.vector.tensor_scalar(xnorm[:, s % 2, :], core.x[:, tile, :], mv[:, 0:1], rstd[:, 0:1],
                                                ALU.subtract, ALU.mult).then_inc(xn.sem, 1)
                    k, s, g = unit(t, L_SCORE)
                    if alive(k):
                        sc = ps[:, SC, :].rearrange("p (c m) -> p c m", c=4)
                        dve.wait_ge(scored.sem, scored.at(i, k + 1))
                        nc.vector.tensor_reduce(top[:, k % 2, :], sc, AX.X, ALU.max).then_inc(maxed.sem, 1)
                        dve.wait_ge(maxed.sem, maxed.at(i, k + 1))
                        dve.wait_ge(probs.sem, probs.at(i, k - 1))
                        nc.vector.tensor_tensor(shift[:, k % 2], sc, spread(top[:, k % 2, :], CROSS_KEYS), ALU.subtract).then_inc(shifted.sem, 1)
                    k, s, g = unit(t, L_ROPE)
                    if alive(k):
                        for u in turns_at(g):
                            n = CROSS_TURNS * s + u
                            src = ks[:, u, :] if u < 2 else qs[:, u - 2, :]
                            tab = table[:, 1 if u < 2 else 0]
                            dve.wait_ge(turned.sem, turned.at(i, n - 3))
                            dve.wait_ge(joined.sem, joined.at(i, n - 1))
                            a4, b4, s4 = (q.rearrange("p (r d) -> p r d", d=CROSS_HD) for q in (ropeA[:, n % 4, :], ropeB[:, n % 2, :], src))
                            if u == 0:
                                last = nc.vector.tensor_tensor(a4, s4, raw[:, 3, :].unsqueeze(1).broadcast_to([P, CROSS_REP, CROSS_HD]), ALU.mult)
                            else:
                                nc.vector.tensor_tensor(a4, s4, tab[:, 0, :].unsqueeze(1).broadcast_to([P, CROSS_REP, CROSS_HD]), ALU.mult)
                                for a, b in ((0, half), (half, 0)):
                                    last = nc.vector.tensor_tensor(b4[:, :, a:a + half], s4[:, :, b:b + half],
                                                                   tab[:, 1, a:a + half].unsqueeze(1).broadcast_to([P, CROSS_REP, half]), ALU.mult)
                            last.then_inc(roped.sem, 1)
                    k, s, g = unit(t, 1)
                    if alive(k) and g == 0:
                        dve.wait_ge(x_hi.sem, x_hi.at(i, s + 1))
                        nc.vector.tensor_tensor(xT[1][:, s % 2], ps[:, LNB, 0:D].rearrange("p (c q) -> p c q", c=KD),
                                                xT[0][:, s % 2], ALU.subtract).then_inc(x_lo.sem, 1)
                    k, s, g = unit(t, L_PROJ)
                    if alive(k):
                        for n, row in {0: [(0, 0), (1, 2)], 1: [(2, 1), (3, 3)], 2: [(4, 4)], 3: [(5, 5)]}[g]:
                            dve.wait_ge(squared.sem, squared.at(i, CROSS_TURNS * s + n + 1))
                            if n == 0:
                                dve.wait_ge(rooted.sem, rooted.at(i, RSQRT_STEPS * (s - 1)))
                            nc.vector.tensor_reduce(sums[:, s % 2, row * CROSS_KVH:(row + 1) * CROSS_KVH],
                                                    square[:, n % 2, :].rearrange("p (r d) -> p r d", d=CROSS_HD), AX.X, ALU.add).then_inc(summed.sem, 1)
                        if g == CROSS_KVH - 1:
                            dve.wait_ge(summed.sem, summed.at(i, CROSS_TURNS * (s + 1)))
                            dve.wait_ge(scaled.sem, scaled.at(i, CROSS_TURNS * (s - 1)))
                            rsqrt(core, dve, rooted, i, RSQRT_STEPS * s, sums[:, s % 2, :], CROSS_RMS_EPS, rms[:, s % 2, :], root)
                    k, s, g = unit(t, L_MIX)
                    if alive(k):
                        dve.wait_ge(o_hi.sem, o_hi.at(i, k + 1))
                        nc.vector.tensor_tensor(oT[1][:, k % 2].rearrange("p r (b q) -> p b r q", b=2),
                                                ps[:, O, :].rearrange("p (b r q) -> p b r q", b=2, r=CROSS_REP),
                                                oT[0][:, k % 2].rearrange("p r (b q) -> p b r q", b=2), ALU.subtract).then_inc(o_lo.sem, 1)
                    k, s, g = unit(t, L_SCORE)
                    if alive(k):
                        dve.wait_ge(exped.sem, exped.at(i, k + 1))
                        dve.wait_ge(probs.sem, probs.at(i, k - 1))
                        nc.vector.tensor_reduce(total[:, k % 2, :], e[:, k % 2], AX.X, ALU.add).then_inc(totalled.sem, 1)
                        dve.wait_ge(totalled.sem, totalled.at(i, k + 1))
                        nc.vector.reciprocal(inv[:, k % 2, :], total[:, k % 2, :]).then_inc(inverse.sem, 1)
                    k, s, g = unit(t, L_OUT)
                    if alive(k) and g == CROSS_KVH - 1:
                        dve.wait_ge(projected.sem, projected.at(i, k + 1))
                        tile = core.x[:, i * SUBS + s, :]
                        nc.vector.tensor_tensor(tile, ps[:, ACC, 0:D], tile, ALU.add).then_inc(added.sem, 1)

            steps(dve, body)

        @block.gpsimd
        def _(pool):
            credit(pool, c_hi, c_lo, joined, scaled, probs)
            ctx = core.ins["ctxT"].rearrange("(k p) n -> p k n", p=P)

            def load_context(tile):
                pool.dma_start(cRaw[:, tile % 2], ctx[:, :, tile * P:(tile + 1) * P]).then_inc(s_ctx[tile % 2], 16)

            load_context(0)
            load_context(1)
            for i in range(STEPS + 1):
                alive = (lambda k: k >= 0) if i == 0 else (lambda k: k < 0) if i == STEPS else (lambda k: True)
                for t in range(CROSS_UNITS):
                    k, s, g = unit(t, 0)
                    if alive(k) and g == 0:
                        tile = i * SUBS + s
                        src = cRaw[:, s % 2]
                        pool.wait_ge(s_ctx[s % 2], 16 * (tile // 2 + 1))
                        pool.wait_ge(kv_ready.sem, kv_ready.at(i, CROSS_KVH * (s - 1)))
                        pool.sem_inc(core.passed, 1)
                        nc.gpsimd.tensor_copy(cT[0][:, s % 2], src).then_inc(c_hi.sem, 1)
                        pool.wait_ge(c_hi.sem, c_hi.at(i, s + 1))
                        nc.gpsimd.tensor_tensor(cT[1][:, s % 2], src, cT[0][:, s % 2], ALU.subtract).then_inc(c_lo.sem, 1)
                        if tile + 2 < TILES:
                            pool.wait_ge(c_lo.sem, c_lo.at(i, s + 1))
                            load_context(tile + 2)
                    k, s, g = unit(t, L_ROPE)
                    if alive(k):
                        if g == 0:
                            pool.wait_ge(rooted.sem, rooted.at(i, RSQRT_STEPS * (s + 1)))
                        for u in turns_at(g):
                            n = CROSS_TURNS * s + u
                            pool.wait_ge(roped.sem, roped.at(i, n + 1))
                            a = ropeA[:, n % 4, :]
                            if u > 0:
                                nc.gpsimd.tensor_tensor(a, a, ropeB[:, n % 2, :], ALU.add).then_inc(joined.sem, 1)
                                pool.wait_ge(joined.sem, joined.at(i, n + 1))
                            else:
                                pool.sem_inc(joined.sem, 1)
                            a4 = a.rearrange("p (r d) -> p r d", d=CROSS_HD)
                            nc.gpsimd.tensor_tensor(a4, a4, spread(rms[:, s % 2, u * CROSS_KVH:(u + 1) * CROSS_KVH], CROSS_HD), ALU.mult).then_inc(scaled.sem, 1)
                    k, s, g = unit(t, L_PROB)
                    if alive(k):
                        pool.wait_ge(inverse.sem, inverse.at(i, k + 1))
                        pool.wait_ge(p_turned.sem, p_turned.at(i, k - 1))
                        nc.gpsimd.tensor_tensor(prob[:, k % 2], e[:, k % 2], spread(inv[:, k % 2, :], CROSS_KEYS), ALU.mult).then_inc(probs.sem, 1)
                if i < STEPS:
                    a, b = len(jobs) * i // STEPS, len(jobs) * (i + 1) // STEPS
                    split_weights(core, pool, jobs[a:b], first + a, core.own)



FFN_FF = 1024
FFN_FFT = FFN_FF // P
FFN_HALF = 512


class FfnWeights:
    def __init__(self, region):
        self.gate = [region.take([P, KD, FFN_FF], F16) for p in range(2)]
        self.up = [region.take([P, KD, FFN_FF], F16) for p in range(2)]
        self.down = [region.take([P, FFN_FFT, D], F16) for p in range(2)]

    def jobs(self, core):
        out = []
        for name, w in (("L0_ffn_w_gate", self.gate), ("L0_ffn_w_up", self.up)):
            for k in range(KD):
                out += chunks(core.ins[name][k * P:(k + 1) * P, :], [q[:, k, :] for q in w])
        for t in range(FFN_FFT):
            out += chunks(core.ins["L0_ffn_w_down"][t * P:(t + 1) * P, :], [q[:, t, :] for q in self.down])
        return out


def ffn_stage(core, w, jobs=(), first=0):
    nc, ps = core.nc, core.ps
    G, U, T, O = (0, 1), (2, 3), (4, 5), 6
    region = Region(core, AT_FFN)
    n = Norm(core, "ffn", region)
    gate_ready = Tally(core, "ffn_gate", 2 * SUBS)
    up_ready = Tally(core, "ffn_up", 2 * SUBS)
    silu_ready = Tally(core, "ffn_silu", 2 * SUBS)
    h_ready = Tally(core, "ffn_h", 2 * SUBS)
    step = Tally(core, "ffn_step", 12 * SUBS)
    kept_ready = Tally(core, "ffn_kept", 4 * SUBS)
    hT_ready = Tally(core, "ffn_hT", 2 * SUBS)
    hT_hi = Tally(core, "ffn_hT_hi", 2 * SUBS)
    hT_lo = Tally(core, "ffn_hT_lo", 2 * SUBS)
    out_ready = Tally(core, "ffn_out", SUBS)
    added = Tally(core, "ffn_added", SUBS)
    with ExitStack() as own:
        def sb(name, shape, dt):
            return region.take(shape, dt)
        silu = sb("silu", [P, 2, FFN_HALF], F32)
        h = sb("h", [P, 2, FFN_FF], F32)
        mag = sb("mag", [P, FFN_FF], F32)
        beats = sb("beats", [P, 3, FFN_HALF], F32)
        wins = sb("wins", [P, 2, FFN_HALF], F32)
        votes = sb("votes", [P, FFN_FF], F32)
        kept = sb("kept", [P, 2, FFN_FF], F32)
        hT = [sb(f"hT{p}", [P, FFN_FFT, P], F16) for p in range(2)]
        block = own.enter_context(nc.Block())

        @block.sync
        def _(sp):
            stage_weights(core, sp, jobs, first)

        @block.gpsimd
        def _(pool):
            split_weights(core, pool, jobs, first, core.own)

        @block.vector
        def _(dve):
            credit(dve, n.stat, n.normed, n.lo, h_ready, step, kept_ready, hT_lo, added)

            def choose(i, s):
                k = s * 12
                hv = h[:, s % 2, :]
                nc.vector.scalar_tensor_tensor(out=mag[:, :], in0=hv, scalar=-1.0, in1=hv, op0=ALU.mult, op1=ALU.max).then_inc(step.sem, 1)
                dve.wait_ge(step.sem, step.at(i, k + 1))
                m = mag[:, :].rearrange("p (g a b) -> p g a b", a=2, b=2)
                m4 = mag[:, :].rearrange("p (g f) -> p g f", f=4)
                b0 = beats[:, 0, :].rearrange("p (g a) -> p g a", a=2)
                b1 = beats[:, 1, :].rearrange("p (g a) -> p g a", a=2)
                b2 = beats[:, 2, :].rearrange("p (g a) -> p g a", a=2)
                nc.vector.tensor_tensor(b0, m[:, :, :, 0], m[:, :, :, 1], ALU.is_ge).then_inc(step.sem, 1)
                nc.vector.tensor_tensor(b1, m[:, :, 0, :], m[:, :, 1, :], ALU.is_ge).then_inc(step.sem, 1)
                nc.vector.tensor_tensor(b2[:, :, 0], m4[:, :, 0], m4[:, :, 3], ALU.is_ge).then_inc(step.sem, 1)
                nc.vector.tensor_tensor(b2[:, :, 1], m4[:, :, 1], m4[:, :, 2], ALU.is_ge).then_inc(step.sem, 1)
                dve.wait_ge(step.sem, step.at(i, k + 5))
                w0 = wins[:, 0, :].rearrange("p (g a) -> p g a", a=2)
                w1 = wins[:, 1, :].rearrange("p (g a) -> p g a", a=2)
                nc.vector.tensor_tensor(wins[:, 0, :], beats[:, 1, :], beats[:, 2, :], ALU.add).then_inc(step.sem, 1)
                nc.vector.tensor_tensor(w1[:, :, 0], b1[:, :, 0], b2[:, :, 1], ALU.add).then_inc(step.sem, 1)
                nc.vector.tensor_tensor(w1[:, :, 1], b1[:, :, 1], b2[:, :, 0], ALU.add).then_inc(step.sem, 1)
                dve.wait_ge(step.sem, step.at(i, k + 8))
                v = votes[:, :].rearrange("p (g f) -> p g f", f=4)
                nc.vector.tensor_tensor(v[:, :, 0], b0[:, :, 0], w0[:, :, 0], ALU.add).then_inc(step.sem, 1)
                nc.vector.tensor_tensor(v[:, :, 1], w0[:, :, 1], b0[:, :, 0], ALU.subtract).then_inc(step.sem, 1)
                nc.vector.tensor_tensor(v[:, :, 2], b0[:, :, 1], w1[:, :, 0], ALU.subtract).then_inc(step.sem, 1)
                nc.vector.tensor_tensor(v[:, :, 3], b0[:, :, 1], w1[:, :, 1], ALU.add).then_inc(step.sem, 1)
                dve.wait_ge(step.sem, step.at(i, k + 12))
                h4 = hv.rearrange("p (g f) -> p g f", f=4)
                kv = kept[:, s % 2, :].rearrange("p (g f) -> p g f", f=4)
                dve.wait_ge(hT_ready.sem, hT_ready.at(i, 2 * s - 2) if s >= 2 else hT_ready.before(i, 2 * (SUBS + s) - 2))
                for f, (least, op) in enumerate(((2.0, ALU.is_ge), (1.0, ALU.is_ge), (0.0, ALU.is_ge), (1.0, ALU.is_le))):
                    nc.vector.scalar_tensor_tensor(out=kv[:, :, f], in0=v[:, :, f], scalar=least, in1=h4[:, :, f], op0=op,
                                                   op1=ALU.mult).then_inc(kept_ready.sem, 1)

            def low_and_add(i, s):
                for a in range(2):
                    dve.wait_ge(hT_hi.sem, hT_hi.at(i, 2 * s + a + 1))
                    nc.vector.tensor_tensor(hT[1][:, 4 * a:4 * a + 4, :], ps[:, T[a], :].rearrange("p (t q) -> p t q", q=P),
                                            hT[0][:, 4 * a:4 * a + 4, :], ALU.subtract).then_inc(hT_lo.sem, 1)
                dve.wait_ge(out_ready.sem, out_ready.at(i, s + 1))
                xs = core.x[:, i * SUBS + s, :]
                nc.vector.tensor_tensor(xs, ps[:, O, 0:D], xs, ALU.add).then_inc(added.sem, 1)

            with dve.Fori(0, STEPS) as i:
                norm_vector(core, n, i, dve)
                norm_vector_low(core, n, i, dve, T)
                for s in range(SUBS):
                    for a in range(2):
                        dve.wait_ge(silu_ready.sem, silu_ready.at(i, 2 * s + a + 1))
                        dve.wait_ge(up_ready.sem, up_ready.at(i, 2 * s + a + 1))
                        nc.vector.tensor_tensor(h[:, s % 2, a * FFN_HALF:(a + 1) * FFN_HALF], ps[:, U[a], :], silu[:, a, :],
                                                ALU.mult).then_inc(h_ready.sem, 1)
                    dve.wait_ge(h_ready.sem, h_ready.at(i, 2 * s + 2))
                    if s >= 1:
                        low_and_add(i, s - 1)
                    choose(i, s)
                low_and_add(i, SUBS - 1)

        @block.tensor
        def _(pe):
            credit(pe, n.turned, gate_ready, up_ready, hT_ready, out_ready)

            def free():
                pe.wait_ge(hT_lo.sem, hT_lo.before(i, 2 * SUBS))

            def project(i, s):
                for a in range(2):
                    for bank, ww, ready in ((G[a], w.gate, gate_ready), (U[a], w.up, up_ready)):
                        pe.wait_ge(h_ready.sem, h_ready.before(i, 2 * SUBS + 2 * (s - 1) + a + 1) if s == 0
                                   else h_ready.at(i, 2 * (s - 1) + a + 1))
                        for k in range(KD):
                            last = product(nc, ps[:, bank, :], [t[:, k, s * P:(s + 1) * P] for t in (n.xT_hi, n.xT_lo)],
                                           [t[:, k, a * FFN_HALF:(a + 1) * FFN_HALF] for t in ww], k == 0, k == KD - 1)
                        last.then_inc(ready.sem, 1)

            def turn_and_down(i, s):
                pe.wait_ge(kept_ready.sem, kept_ready.at(i, 4 * s + 4))
                for a in range(2):
                    if s == 0:
                        pe.wait_ge(n.lo.sem, n.lo.at(i, a + 1))
                    else:
                        pe.wait_ge(hT_lo.sem, hT_lo.at(i, 2 * (s - 1) + a + 1))
                    for t in range(4 * a, 4 * a + 4):
                        last = nc.tensor.transpose(ps[:, T[a], (t % 4) * P:(t % 4 + 1) * P], kept[:, s % 2, t * P:(t + 1) * P],
                                                   core.ident[:, :])
                    last.then_inc(hT_ready.sem, 1)
                pe.wait_ge(added.sem, added.before(i, SUBS) if s == 0 else added.at(i, s))
                for t in range(FFN_FFT):
                    if t % 4 == 0:
                        pe.wait_ge(hT_lo.sem, hT_lo.at(i, 2 * s + t // 4 + 1))
                    last = product(nc, ps[:, O, 0:D], [q[:, t, :] for q in hT], [q[:, t, :] for q in w.down], t == 0, t == FFN_FFT - 1)
                last.then_inc(out_ready.sem, 1)

            with pe.Fori(0, STEPS) as i:
                norm_tensor(core, n, i, pe, T, free)
                pe.wait_ge(n.hi.sem, n.hi.at(i, KD))
                pe.wait_ge(n.lo.sem, n.lo.at(i, KD))
                for s in range(SUBS):
                    project(i, s)
                    if s >= 1:
                        turn_and_down(i, s - 1)
                turn_and_down(i, SUBS - 1)

        @block.scalar
        def _(act):
            credit(act, n.hi, silu_ready, hT_hi)

            def high(i, s):
                for a in range(2):
                    act.wait_ge(hT_ready.sem, hT_ready.at(i, 2 * s + a + 1))
                    act.wait_ge(out_ready.sem, out_ready.before(i, SUBS) if s == 0 else out_ready.at(i, s))
                    nc.scalar.activation(hT[0][:, 4 * a:4 * a + 4, :], ps[:, T[a], :].rearrange("p (t q) -> p t q", q=P),
                                         ACT.Copy).then_inc(hT_hi.sem, 1)

            with act.Fori(0, STEPS) as i:
                norm_scalar(core, n, i, act, T)
                for s in range(SUBS):
                    for a in range(2):
                        act.wait_ge(gate_ready.sem, gate_ready.at(i, 2 * s + a + 1))
                        act.wait_ge(h_ready.sem, h_ready.before(i, 2 * SUBS - 2 + a + 1) if s == 0 else h_ready.at(i, 2 * (s - 1) + a + 1))
                        nc.scalar.activation(silu[:, a, :], ps[:, G[a], :], ACT.Silu).then_inc(silu_ready.sem, 1)
                    if s >= 1:
                        high(i, s - 1)
                high(i, SUBS - 1)



ALIBI_HEADS, ALIBI_KVH, ALIBI_HD = 16, 4, 16
ALIBI_PAIRS = 2
ALIBI_UNITS = SUBS * ALIBI_PAIRS
ALIBI_SCALE = 0.25
ALIBI_KV = ALIBI_KVH * ALIBI_HD


class AlibiWeights:

    def __init__(self, region):
        self.q = [region.take([P, KD, D], F16) for p in range(2)]
        self.k = [region.take([P, KD, 2 * ALIBI_KV], F16) for p in range(2)]
        self.v = [region.take([P, KD, ALIBI_KV], F16) for p in range(2)]
        self.out = [region.take([P, KD, D], F16) for p in range(2)]

    def jobs(self, core):
        out = []
        for name, w in (("L1_attn_Wq", self.q), ("L1_attn_Wk", self.k), ("L1_attn_Wv", self.v), ("L1_attn_Wo", self.out)):
            for k in range(KD):
                out += chunks(core.ins[name][k * P:(k + 1) * P, :], [q[:, k, :] for q in w])
        return out


def alibi_stage(core, w, jobs=(), first=0):
    nc, ps = core.nc, core.ps
    LNB, QB, KB_, VB, SC, PT, O, ACC = range(8)
    tally = lambda name, per: Tally(core, "al_" + name, per)
    stat = tally("stat", SUBS * (2 + RSQRT_STEPS))
    normed, x_lo = tally("normed", SUBS), tally("x_lo", SUBS)
    xn_turned, x_hi = tally("xn_turned", SUBS), tally("x_hi", SUBS)
    q_ready, k_ready, v_ready = (tally(c, SUBS) for c in ("q_ready", "k_ready", "v_ready"))
    q_kept, k_kept, v_kept = (tally(c, SUBS) for c in ("q_kept", "k_kept", "v_kept"))
    scored = tally("scored", ALIBI_UNITS)
    biased, maxed, shifted, totalled, inverse = (tally(c, ALIBI_UNITS) for c in ("biased", "maxed", "shifted", "totalled", "inverse"))
    exped, probs = tally("exped", ALIBI_UNITS), tally("probs", ALIBI_UNITS)
    p_turned, pT_kept = tally("p_turned", ALIBI_UNITS), tally("pT_kept", ALIBI_UNITS)
    mixed, o_hi, o_lo = tally("mixed", ALIBI_UNITS), tally("o_hi", ALIBI_UNITS), tally("o_lo", ALIBI_UNITS)
    projected, added = tally("projected", SUBS), tally("added", SUBS)
    s_const, s_zero = core.sem("al_const"), core.sem("al_zero")
    L_TURN, L_PROJ, L_SCORE, L_PROB, L_PTURN, L_MIX, L_OUT = 1, 2, 4, 5, 6, 7, 8
    region = Region(core, AT_FFN)
    sb = lambda name, shape, dt: region.take(shape, dt)
    xT = [sb(f"xT{p}", [P, 2, KD, P], F16) for p in range(2)]
    xnorm = sb("xnorm", [P, 2, D], F32)
    st, mv, rstd, root = sb("st", [P, 6], F32), sb("mv", [P, 2], F32), sb("rstd", [P, 1], F32), sb("root", [P, 3, 1], F32)
    qT = sb("qT", [P, 2, ALIBI_PAIRS, P], F32)
    kT = sb("kT", [P, 2, 2, 8, S], F32)
    v = sb("v", [P, SUBS, 2, 2, 2 * ALIBI_HD], F32)
    bias = sb("bias", [P, ALIBI_KVH, S], F32)
    logits, e, prob = (sb(c, [P, 2, 8, S], F32) for c in ("logits", "e", "prob"))
    top, total, inv = (sb(c, [P, 2, 8], F32) for c in ("top", "total", "inv"))
    pT = sb("pT", [P, 2, 4, P], F32)
    oT = [sb(f"oT{p}", [P, 2, ALIBI_PAIRS, P], F16) for p in range(2)]

    def unit(t, lag):
        k = t - lag
        return k, k // ALIBI_PAIRS, k % ALIBI_PAIRS

    with nc.Block() as block:
        @block.sync
        def _(sp):
            sp.dma_start(bias, core.ins["alibi"]).then_inc(s_const, 16)
            stage_weights(core, sp, jobs, first)

        @block.tensor
        def _(pe):
            credit(pe, xn_turned, q_ready, k_ready, v_ready, scored, p_turned, mixed, projected)

            def body(i, alive):
                for t in range(ALIBI_UNITS):
                    k, s, a = unit(t, L_TURN)
                    if alive(k) and a == 0:
                        pe.wait_ge(normed.sem, normed.at(i, s + 1))
                        pe.wait_ge(x_lo.sem, x_lo.at(i, s))
                        for c in range(KD):
                            last = nc.tensor.transpose(ps[:, LNB, c * P:(c + 1) * P], xnorm[:, s % 2, c * P:(c + 1) * P], core.ident)
                        last.then_inc(xn_turned.sem, 1)
                    k, s, a = unit(t, L_PROJ)
                    if alive(k) and a == 0:
                        x = [q[:, s % 2] for q in xT]
                        pe.wait_ge(x_lo.sem, x_lo.at(i, s + 1))
                        pe.wait_ge(q_kept.sem, q_kept.at(i, s))
                        for a in range(ALIBI_PAIRS):
                            for c in range(KD):
                                last = product(nc, ps[:, QB, a * P:(a + 1) * P], [q[:, c, a * P:(a + 1) * P] for q in w.q],
                                               [q[:, c, :] for q in x], c == 0, c == KD - 1)
                        last.then_inc(q_ready.sem, 1)
                        pe.wait_ge(k_kept.sem, k_kept.at(i, s))
                        for c in range(KD):
                            last = product(nc, ps[:, KB_, 0:P], [q[:, c, :] for q in w.k], [q[:, c, :] for q in x], c == 0, c == KD - 1)
                        last.then_inc(k_ready.sem, 1)
                        pe.wait_ge(v_kept.sem, v_kept.at(i, s))
                        for c in range(KD):
                            last = product(nc, ps[:, VB, 0:ALIBI_KV], [q[:, c, :] for q in x], [q[:, c, :] for q in w.v], c == 0, c == KD - 1)
                        last.then_inc(v_ready.sem, 1)
                    k, s, a = unit(t, L_SCORE)
                    if alive(k):
                        pe.wait_ge(k_kept.sem, k_kept.at(i, s + 1))
                        pe.wait_ge(q_kept.sem, q_kept.at(i, s + 1))
                        pe.wait_ge(biased.sem, biased.at(i, k))
                        for b in range(2):
                            last = nc.tensor.matmul(ps[b * S:(b + 1) * S, SC, :], qT[:, s % 2, a, b * S:(b + 1) * S],
                                                    kT[:, s % 2, b].rearrange("p h k -> p (h k)"), start=True, stop=True)
                        last.then_inc(scored.sem, 1)
                    k, s, a = unit(t, L_MIX)
                    if alive(k):
                        pe.wait_ge(pT_kept.sem, pT_kept.at(i, k + 1))
                        pe.wait_ge(v_kept.sem, v_kept.at(i, s + 1))
                        pe.wait_ge(o_lo.sem, o_lo.at(i, k))
                        for b in range(2):
                            for c in range(4):
                                last = nc.tensor.matmul(ps[c * 32:(c + 1) * 32, O, b * S:(b + 1) * S], v[:, s % SUBS, b, c % 2, :],
                                                        pT[:, k % 2, c, b * S:(b + 1) * S], start=True, stop=True,
                                                        tile_position=(0, c * 32))
                        last.then_inc(mixed.sem, 1)
                    k, s, a = unit(t, L_PTURN)
                    if alive(k):
                        pe.wait_ge(probs.sem, probs.at(i, k + 1))
                        pe.wait_ge(pT_kept.sem, pT_kept.at(i, k))
                        for c in range(4):
                            last = nc.tensor.transpose(ps[:, PT, c * P:(c + 1) * P], prob[:, k % 2, 2 * c:2 * c + 2, :].rearrange("p h k -> p (h k)"), core.ident)
                        last.then_inc(p_turned.sem, 1)
                    k, s, a = unit(t, L_OUT)
                    if alive(k) and a == ALIBI_PAIRS - 1:
                        pe.wait_ge(o_lo.sem, o_lo.at(i, k + 1))
                        pe.wait_ge(added.sem, added.at(i, s))
                        for a in range(ALIBI_PAIRS):
                            last = product(nc, ps[:, ACC, 0:D], [q[:, s % 2, a, :] for q in oT], [q[:, a, :] for q in w.out], a == 0, a == ALIBI_PAIRS - 1)
                        last.then_inc(projected.sem, 1)

            steps(pe, body)

        @block.scalar
        def _(act):
            credit(act, x_hi, q_kept, k_kept, v_kept, exped, pT_kept, o_hi)
            act.wait_ge(s_zero, 2)

            def body(i, alive):
                for t in range(ALIBI_UNITS):
                    k, s, a = unit(t, L_TURN)
                    if alive(k) and a == 0:
                        act.wait_ge(xn_turned.sem, xn_turned.at(i, s + 1))
                        act.wait_ge(v_ready.sem, v_ready.at(i, s - 1))
                        nc.scalar.activation(xT[0][:, s % 2], ps[:, LNB, 0:D].rearrange("p (c q) -> p c q", c=KD), ACT.Copy).then_inc(x_hi.sem, 1)
                    k, s, a = unit(t, L_PROJ)
                    if alive(k) and a == 0:
                        act.wait_ge(q_ready.sem, q_ready.at(i, s + 1))
                        act.wait_ge(scored.sem, scored.at(i, ALIBI_PAIRS * (s - 1)))
                        nc.scalar.activation(qT[:, s % 2], ps[:, QB, 0:D].rearrange("p (a q) -> p a q", a=ALIBI_PAIRS), ACT.Copy).then_inc(q_kept.sem, 1)
                        act.wait_ge(v_ready.sem, v_ready.at(i, s + 1))
                        act.wait_ge(mixed.sem, mixed.at(i, ALIBI_PAIRS * (s - 3)))
                        for b in range(2):
                            for c in range(2):
                                last = nc.scalar.activation(v[c * S:(c + 1) * S, s % SUBS, b, :, c * ALIBI_HD:(c + 1) * ALIBI_HD],
                                                            ps[b * S:(b + 1) * S, VB, 0:ALIBI_KV].rearrange("p (g c d) -> p g c d", c=2, d=ALIBI_HD)[:, :, c, :], ACT.Copy)
                        last.then_inc(v_kept.sem, 1)
                        act.wait_ge(k_ready.sem, k_ready.at(i, s + 1))
                        for j in range(8):
                            last = nc.scalar.activation(kT[:, s % 2, :, j, :], ps[:, KB_, 0:P].rearrange("p (b k) -> p b k", b=2), ACT.Copy,
                                                        scale=core.headmask[:, j:j + 1])
                        last.then_inc(k_kept.sem, 1)
                    k, s, a = unit(t, L_SCORE)
                    if alive(k):
                        act.wait_ge(shifted.sem, shifted.at(i, k + 1))
                        act.wait_ge(probs.sem, probs.at(i, k - 1))
                        nc.scalar.activation(e[:, k % 2], logits[:, k % 2], ACT.Exp).then_inc(exped.sem, 1)
                    k, s, a = unit(t, L_MIX)
                    if alive(k):
                        act.wait_ge(mixed.sem, mixed.at(i, k + 1))
                        act.wait_ge(projected.sem, projected.at(i, s - 1))
                        nc.scalar.activation(oT[0][:, s % 2, a, :], ps[:, O, 0:P], ACT.Copy).then_inc(o_hi.sem, 1)
                    k, s, a = unit(t, L_PTURN)
                    if alive(k):
                        act.wait_ge(p_turned.sem, p_turned.at(i, k + 1))
                        act.wait_ge(mixed.sem, mixed.at(i, k - 1))
                        nc.scalar.activation(pT[:, k % 2], ps[:, PT, :].rearrange("p (c q) -> p c q", c=4), ACT.Copy).then_inc(pT_kept.sem, 1)

            steps(act, body)

        @block.vector
        def _(dve):
            credit(dve, stat, normed, x_lo, biased, maxed, shifted, totalled, inverse, o_lo, added)
            nc.vector.memset(v, 0.0).then_inc(s_zero, 1)
            dve.wait_ge(s_zero, 1)
            dve.wait_ge(s_const, 16)
            dve.sem_inc(s_zero, 1)

            def body(i, alive):
                for t in range(ALIBI_UNITS):
                    k, s, a = unit(t, 0)
                    if alive(k) and a == 0:
                        norm_tile(core, dve, stat, i, s, i * SUBS + s, st, mv, rstd, root)
                        dve.wait_ge(xn_turned.sem, xn_turned.at(i, s - 1))
                        nc.vector.tensor_scalar(xnorm[:, s % 2, :], core.x[:, i * SUBS + s, :], mv[:, 0:1], rstd[:, 0:1],
                                                ALU.subtract, ALU.mult).then_inc(normed.sem, 1)
                    k, s, a = unit(t, L_SCORE)
                    if alive(k):
                        lg = logits[:, k % 2]
                        dve.wait_ge(scored.sem, scored.at(i, k + 1))
                        dve.wait_ge(exped.sem, exped.at(i, k - 1))
                        nc.vector.scalar_tensor_tensor(out=lg.rearrange("p (r g) k -> p r (g k)", r=2), in0=ps[:, SC, :].rearrange("p (r n) -> p r n", r=2),
                                                       scalar=ALIBI_SCALE, in1=bias.rearrange("p g k -> p (g k)").unsqueeze(1).broadcast_to([P, 2, ALIBI_KVH * S]),
                                                       op0=ALU.mult, op1=ALU.add).then_inc(biased.sem, 1)
                        dve.wait_ge(biased.sem, biased.at(i, k + 1))
                        nc.vector.tensor_reduce(top[:, k % 2, :], lg, AX.X, ALU.max).then_inc(maxed.sem, 1)
                        dve.wait_ge(maxed.sem, maxed.at(i, k + 1))
                        nc.vector.tensor_tensor(lg, lg, spread(top[:, k % 2, :], S), ALU.subtract).then_inc(shifted.sem, 1)
                    k, s, a = unit(t, L_TURN)
                    if alive(k) and a == 0:
                        dve.wait_ge(x_hi.sem, x_hi.at(i, s + 1))
                        nc.vector.tensor_tensor(xT[1][:, s % 2], ps[:, LNB, 0:D].rearrange("p (c q) -> p c q", c=KD),
                                                xT[0][:, s % 2], ALU.subtract).then_inc(x_lo.sem, 1)
                    k, s, a = unit(t, L_SCORE)
                    if alive(k):
                        dve.wait_ge(exped.sem, exped.at(i, k + 1))
                        dve.wait_ge(probs.sem, probs.at(i, k - 1))
                        nc.vector.tensor_reduce(total[:, k % 2, :], e[:, k % 2], AX.X, ALU.add).then_inc(totalled.sem, 1)
                        dve.wait_ge(totalled.sem, totalled.at(i, k + 1))
                        nc.vector.reciprocal(inv[:, k % 2, :], total[:, k % 2, :]).then_inc(inverse.sem, 1)
                    k, s, a = unit(t, L_MIX)
                    if alive(k):
                        dve.wait_ge(o_hi.sem, o_hi.at(i, k + 1))
                        nc.vector.tensor_tensor(oT[1][:, s % 2, a, :], ps[:, O, 0:P], oT[0][:, s % 2, a, :], ALU.subtract).then_inc(o_lo.sem, 1)
                    k, s, a = unit(t, L_OUT)
                    if alive(k) and a == ALIBI_PAIRS - 1:
                        dve.wait_ge(projected.sem, projected.at(i, s + 1))
                        tile = core.x[:, i * SUBS + s, :]
                        nc.vector.tensor_tensor(tile, ps[:, ACC, 0:D], tile, ALU.add).then_inc(added.sem, 1)

            steps(dve, body)

        @block.gpsimd
        def _(pool):
            credit(pool, probs)
            for i in range(STEPS + 1):
                alive = (lambda k: k >= 0) if i == 0 else (lambda k: k < 0) if i == STEPS else (lambda k: True)
                for t in range(ALIBI_UNITS):
                    k, s, a = unit(t, L_PROB)
                    if alive(k):
                        pool.wait_ge(inverse.sem, inverse.at(i, k + 1))
                        pool.wait_ge(p_turned.sem, p_turned.at(i, k - 1))
                        nc.gpsimd.tensor_tensor(prob[:, k % 2], e[:, k % 2], spread(inv[:, k % 2, :], S), ALU.mult).then_inc(probs.sem, 1)
                    if t % 2 and i < STEPS:
                        a, b = (len(jobs) * (i * ALIBI_UNITS + t + n) // (STEPS * ALIBI_UNITS) for n in (-1, 1))
                        split_weights(core, pool, jobs[a:b], first + a, core.own)



CH_CH = 4
CH_GROUPS, CH_IN_GROUP = 2, 8
CH_QUADS, CH_UNITS_B = 4, 4
CH_GT = CH_IN_GROUP * CH_CH
CH_BT = CH_GROUPS * CH_GT
CH_ROWS = 3 * CH_GT
CH_ONES = CH_ROWS + CH_IN_GROUP
CH_STEP_TILES = 2
CH_BLOCKS = CH_STEP_TILES * 2
CH_SLOTS = CH_BLOCKS * CH_UNITS_B
CH_STEPS5 = TILES // CH_STEP_TILES
CH_SCALE = 0.5


def steps5(engine, body):
    body(0, lambda k: k >= 0)
    with engine.Fori(1, CH_STEPS5) as i:
        body(i, lambda k: True)
    body(CH_STEPS5, lambda k: k < 0)


def channel_stage(core, jobs=(), first=0):
    nc, ps = core.nc, core.ps
    A, T, O, M = (0, 1), (2, 4), 6, 7
    tally = lambda name, per: Tally(core, "ch_" + name, per)
    stat = tally("stat", CH_STEP_TILES * (2 + RSQRT_STEPS))
    normed = tally("normed", CH_STEP_TILES)
    ctx_in = [tally(f"ctx_in{n}", 64 * CH_BLOCKS // 2) for n in range(2)]
    q_in = [tally(f"q_in{n}", 96 * CH_BLOCKS // 2) for n in range(2)]
    k_hi, k_lo, q_hi, q_lo = (tally(c, CH_BLOCKS) for c in ("k_hi", "k_lo", "q_hi", "q_lo"))
    k_apart = tally("k_apart", CH_BLOCKS)
    k_apart2 = tally("k_apart2", CH_BLOCKS)
    v_set = tally("v_set", CH_BLOCKS)
    scored = tally("scored", CH_BLOCKS * 16)
    maxed = tally("maxed", CH_BLOCKS * 16)
    m_turned, m_set = tally("m_turned", CH_BLOCKS), tally("m_set", CH_BLOCKS)
    scoredT = tally("scoredT", CH_BLOCKS * 8)
    exped = tally("exped", CH_BLOCKS * 8)
    mixed = tally("mixed", CH_SLOTS)
    o_kept = tally("o_kept", CH_BLOCKS)
    o_moved = [tally(f"o_moved{n}", 128 * CH_BLOCKS // 2) for n in range(2)]
    finished = tally("finished", 3 * CH_STEP_TILES)
    s_const, s_zero = core.sem("ch_const"), core.sem("ch_zero")
    region = Region(core, AT_CHANNEL)
    sb = lambda shape, dt=F32: region.take(shape, dt)
    xnorm = sb([P, 2, D])
    st, mv, rstd, root = sb([P, 6]), sb([P, 2]), sb([P, 1]), sb([P, 3, 1])
    kraw, qraw = sb([P, 2, CH_GROUPS, D]), sb([P, 2, CH_GROUPS, D])
    vraw = sb([P, 2, KD, CH_BT])
    kg = sb([P, CH_GROUPS, D], F16)
    ka = sb([P, CH_BLOCKS, CH_GROUPS, CH_IN_GROUP, D], F16)
    qg = sb([P, CH_BLOCKS, CH_GROUPS, D], F16)
    vz = sb([P, 2, KD, CH_QUADS, CH_UNITS_B, 32])
    m = sb([P, 2, CH_GROUPS, KD, CH_IN_GROUP])
    pT = sb([P, 2, 2, 2, KD, D])
    osb = sb([P, 2, D])
    oo, ss = sb([P, D]), sb([P, D])

    def block_of(t, lag):
        k = t - lag * CH_UNITS_B
        return k, k // CH_UNITS_B, k % CH_UNITS_B

    with nc.Block() as block:
        @block.sync
        def _(sp):
            credit(sp, *ctx_in, *q_in, *o_moved)
            sp.dma_start(core.apart, core.ins["apart"]).then_inc(s_const, 16)
            rows = core.ins["ctx_2048"].rearrange("(n g p) d -> n p g d", g=CH_GROUPS, p=CH_GT)
            cols = core.ins["ctxT"].rearrange("(k p) n -> p k n", p=P)

            def body(i, alive):
                for b in range(CH_BLOCKS):
                    n = i * CH_BLOCKS + b
                    if alive(b):
                        sp.wait_ge(k_lo.sem, k_lo.at(i, b - 1))
                        sp.wait_ge(v_set.sem, v_set.at(i, b - 1))
                        for r in range(3):
                            sp.dma_start(kraw[r * CH_GT:(r + 1) * CH_GT, b % 2], rows[n]).then_inc(ctx_in[b % 2].sem, 16)
                        sp.dma_start(vraw[:, b % 2], cols[:, :, bass.ts(n, CH_BT)]).then_inc(ctx_in[b % 2].sem, 16)
                        sp.wait_ge(normed.sem, normed.at(i, b // 2 + 1))
                        sp.wait_ge(q_lo.sem, q_lo.at(i, b - 1))
                        for g in range(CH_GROUPS):
                            r0 = (b % 2 * CH_GROUPS + g) * CH_GT
                            for r in range(3):
                                sp.dma_start(qraw[r * CH_GT:(r + 1) * CH_GT, b % 2, g], xnorm[r0:r0 + CH_GT, b // 2 % 2]).then_inc(q_in[b % 2].sem, 16)
                    k, b, j = block_of(b * CH_UNITS_B, 4)
                    if alive(k):
                        sp.wait_ge(o_kept.sem, o_kept.at(i, b + 1))
                        sp.sem_inc(core.passed, 1)
                        sp.wait_ge(finished.sem, finished.at(i, 3 * (b // 2)))
                        for q in range(CH_QUADS):
                            to = slice(b % 2 * CH_BT + q * 16, b % 2 * CH_BT + (q + 1) * 16)
                            sp.dma_start(oo[to], osb[q * 32:q * 32 + 16, b % 2]).then_inc(o_moved[b % 2].sem, 16)
                            sp.dma_start(ss[to], osb[q * 32 + 16:(q + 1) * 32, b % 2]).then_inc(o_moved[b % 2].sem, 16)

            steps5(sp, body)
            stage_weights(core, sp, jobs, first)

        @block.tensor
        def _(pe):
            credit(pe, scored, m_turned, scoredT, mixed)
            pe.wait_ge(s_zero, 4)

            def body(i, alive):
                for t in range(CH_SLOTS):
                    k, b, j = block_of(t, 2)
                    k2, b2, j2 = block_of(t, 3)
                    for q in range(CH_QUADS):
                        if alive(k):
                            if q == 0 and j == 0:
                                pe.wait_ge(k_apart.sem, k_apart.at(i, b + 1))
                                pe.wait_ge(k_apart2.sem, k_apart2.at(i, b + 1))
                                pe.wait_ge(q_lo.sem, q_lo.at(i, b + 1))
                            n = k * CH_QUADS + q
                            g, hd = q // 2, q % 2 * 4 + j
                            pe.wait_ge(maxed.sem, maxed.at(i, n - 1))
                            for u in range(KD):
                                last = nc.tensor.matmul(ps[:, A[q % 2], u * D:(u + 1) * D], qg[0:CH_ROWS, b % CH_BLOCKS, g, u * P:(u + 1) * P],
                                                        ka[0:CH_ROWS, b % CH_BLOCKS, g, hd, :], start=True, stop=True)
                            last.then_inc(scored.sem, 1)
                        if alive(k2):
                            if q == 0 and j2 == 0:
                                pe.wait_ge(m_set.sem, m_set.at(i, b2 + 1))
                            g, hd = q // 2, q % 2 * 4 + j2
                            if q % 2 == 0:
                                pe.wait_ge(exped.sem, exped.at(i, 2 * k2 + q // 2 - 1))
                            for u in range(KD):
                                last = nc.tensor.matmul(ps[:, T[q // 2] + q % 2, u * D:(u + 1) * D], ka[0:CH_ONES, b2 % CH_BLOCKS, g, hd, u * P:(u + 1) * P],
                                                        qg[0:CH_ONES, b2 % CH_BLOCKS, g, :], start=True, stop=True)
                            if q % 2 == 1:
                                last.then_inc(scoredT.sem, 1)
                    if alive(k) and j == CH_UNITS_B - 1:
                        pe.wait_ge(maxed.sem, maxed.at(i, (b + 1) * 16))
                        pe.wait_ge(m_set.sem, m_set.at(i, b))
                        for g in range(CH_GROUPS):
                            for u in range(KD):
                                last = nc.tensor.transpose(ps[0:CH_IN_GROUP, M, (g * KD + u) * P:(g * KD + u + 1) * P], m[:, b % 2, g, u, :], core.ident)
                        last.then_inc(m_turned.sem, 1)
                    k3 = t - 3 * CH_UNITS_B - 1
                    if alive(k3):
                        b3, j3 = k3 // CH_UNITS_B, k3 % CH_UNITS_B
                        pe.wait_ge(exped.sem, exped.at(i, 2 * k3 + 2))
                        if j3 == 0:
                            pe.wait_ge(o_kept.sem, o_kept.at(i, b3))
                            pe.wait_ge(v_set.sem, v_set.at(i, b3 + 1))
                        for u in range(KD):
                            for q in range(CH_QUADS):
                                last = nc.tensor.matmul(ps[q * 32:(q + 1) * 32, O, 0:D], vz[:, b3 % 2, u, q, j3, :], pT[:, k3 % 2, q // 2, q % 2, u, :],
                                                        start=j3 == 0 and u == 0, stop=j3 == CH_UNITS_B - 1 and u == KD - 1,
                                                        tile_position=(0, q * 32), skip_group_check=True)
                        last.then_inc(mixed.sem, 1)

            steps5(pe, body)

        @block.scalar
        def _(act):
            credit(act, v_set, m_set, exped, o_kept)
            act.wait_ge(s_zero, 4)

            def body(i, alive):
                for t in range(CH_SLOTS):
                    k, b, j = block_of(t, 2)
                    if alive(k) and j == 1:
                        act.wait_ge(ctx_in[b % 2].sem, ctx_in[b % 2].at(i, 64 * (b // 2 + 1)))
                        act.wait_ge(mixed.sem, mixed.at(i, CH_UNITS_B * (b - 1)))
                        src = vraw[:, b % 2].rearrange("p u (q j c) -> p u q j c", q=CH_QUADS, c=CH_CH)
                        for jj in range(CH_UNITS_B):
                            last = nc.scalar.activation(vz[:, b % 2, :, :, jj, CH_CH * jj:CH_CH * (jj + 1)], src[:, :, :, jj, :], ACT.Copy)
                        last.then_inc(v_set.sem, 1)
                    k, b, j = block_of(t, 3)
                    if alive(k):
                        if j == 0:
                            act.wait_ge(m_turned.sem, m_turned.at(i, b + 1))
                            nc.scalar.activation(qg[CH_ROWS:CH_ONES, b % CH_BLOCKS], ps[0:CH_IN_GROUP, M, :].rearrange("p (g t) -> p g t", g=CH_GROUPS),
                                                 ACT.Copy, scale=-1.0).then_inc(m_set.sem, 1)
                        for a in range(2):
                            act.wait_ge(scoredT.sem, scoredT.at(i, 2 * k + a + 1))
                            act.wait_ge(mixed.sem, mixed.at(i, k - 1))
                            nc.scalar.activation(pT[:, k % 2, a], ps[:, T[a]:T[a] + 2, :].rearrange("p h (u t) -> p h u t", u=KD), ACT.Exp,
                                                 scale=CH_SCALE).then_inc(exped.sem, 1)
                    k, b, j = block_of(t, 4)
                    if alive(k) and j == 0:
                        act.wait_ge(mixed.sem, mixed.at(i, k + CH_UNITS_B))
                        act.wait_ge(o_moved[b % 2].sem, o_moved[b % 2].at(i, 128 * (b // 2)))
                        nc.scalar.activation(osb[:, b % 2], ps[:, O, 0:D], ACT.Copy).then_inc(o_kept.sem, 1)

            steps5(act, body)

        @block.vector
        def _(dve):
            credit(dve, stat, normed, k_apart2, maxed, finished)
            nc.vector.memset(vz, 0.0).then_inc(s_zero, 1)
            dve.wait_ge(s_zero, 1)
            dve.wait_ge(s_const, 16)
            for j in range(CH_UNITS_B):
                for n in range(2):
                    nc.vector.memset(vz[:, n, :, :, j, 16 + CH_CH * j:16 + CH_CH * (j + 1)].rearrange("p u q c -> p (u q) c"), 1.0)
            for n in range(CH_BLOCKS):
                for g in range(CH_GROUPS):
                    nc.vector.tensor_copy(ka[CH_ROWS:CH_ONES, n, g], spread(core.apart[CH_ROWS:CH_ONES, :], D))
            dve.drain().then_inc(s_zero, 3)
            dve.wait_ge(s_zero, 4)

            def body(i, alive):
                for t in range(CH_SLOTS):
                    if alive(t) and t % 8 == 0:
                        s = t // 8
                        norm_tile(core, dve, stat, i, s, i * CH_STEP_TILES + s, st, mv, rstd, root)
                        for n in range(2):
                            dve.wait_ge(q_in[n].sem, q_in[n].at(i, 96 * (s - 1)))
                        nc.vector.tensor_scalar(xnorm[:, s % 2, :], core.x[:, i * CH_STEP_TILES + s, :], mv[:, 0:1], rstd[:, 0:1],
                                                ALU.subtract, ALU.mult).then_inc(normed.sem, 1)
                    k, b, j = block_of(t, 1)
                    if alive(k) and j == 2:
                        dve.wait_ge(k_lo.sem, k_lo.at(i, b + 1))
                        dve.wait_ge(scoredT.sem, scoredT.at(i, 8 * (b - 3)))
                        for hd in range(CH_IN_GROUP):
                            last = nc.vector.tensor_scalar(ka[0:CH_ROWS, b % CH_BLOCKS, 1, hd, :], kg[0:CH_ROWS, 1, :], core.apart[0:CH_ROWS, hd:hd + 1], None, ALU.mult)
                        last.then_inc(k_apart2.sem, 1)
                    k, b, j = block_of(t, 2)
                    if alive(k):
                        for q in range(CH_QUADS):
                            n = k * CH_QUADS + q
                            dve.wait_ge(scored.sem, scored.at(i, n + 1))
                            if j == 0 and q == 0:
                                dve.wait_ge(m_turned.sem, m_turned.at(i, b - 1))
                            nc.vector.tensor_reduce(m[:, b % 2, q // 2, :, q % 2 * 4 + j], ps[:, A[q % 2], :].rearrange("p (u s) -> p u s", u=KD),
                                                    AX.X, ALU.max).then_inc(maxed.sem, 1)
                    k, b, j = block_of(t, 4)
                    if alive(k) and b % 2 == 1 and j == 3:
                        s = b // 2
                        tile = core.x[:, i * CH_STEP_TILES + s, :]
                        for n in range(2):
                            dve.wait_ge(o_moved[n].sem, o_moved[n].at(i, 128 * (s + 1)))
                        nc.vector.reciprocal(ss, ss).then_inc(finished.sem, 1)
                        dve.wait_ge(finished.sem, finished.at(i, 3 * s + 1))
                        nc.vector.tensor_tensor(oo, oo, ss, ALU.mult).then_inc(finished.sem, 1)
                        dve.wait_ge(finished.sem, finished.at(i, 3 * s + 2))
                        nc.vector.tensor_tensor(tile, tile, oo, ALU.add).then_inc(finished.sem, 1)

            steps5(dve, body)

        @block.gpsimd
        def _(pool):
            credit(pool, k_hi, k_lo, q_hi, q_lo, k_apart)

            def body(i, alive):
                for b in range(CH_BLOCKS):
                    k, b, j = block_of(b * CH_UNITS_B, 1)
                    if alive(k):
                        lo = slice(CH_GT, 2 * CH_GT)
                        pool.wait_ge(ctx_in[b % 2].sem, ctx_in[b % 2].at(i, 64 * (b // 2 + 1)))
                        pool.wait_ge(k_apart2.sem, k_apart2.at(i, b))
                        pool.wait_ge(k_apart.sem, k_apart.at(i, b))
                        pool.sem_inc(core.passed, 1)
                        nc.gpsimd.tensor_copy(kg[0:CH_ROWS], kraw[0:CH_ROWS, b % 2]).then_inc(k_hi.sem, 1)
                        pool.wait_ge(k_hi.sem, k_hi.at(i, b + 1))
                        nc.gpsimd.tensor_tensor(kg[lo], kraw[lo, b % 2], kg[lo], ALU.subtract).then_inc(k_lo.sem, 1)
                        pool.wait_ge(q_in[b % 2].sem, q_in[b % 2].at(i, 96 * (b // 2 + 1)))
                        pool.wait_ge(scoredT.sem, scoredT.at(i, 8 * (b - 3)))
                        pool.wait_ge(k_lo.sem, k_lo.at(i, b + 1))
                        pool.sem_inc(core.passed, 1)
                        nc.gpsimd.tensor_copy(qg[0:CH_ROWS, b % CH_BLOCKS], qraw[0:CH_ROWS, b % 2]).then_inc(q_hi.sem, 1)
                        pool.wait_ge(q_hi.sem, q_hi.at(i, b + 1))
                        lo = slice(2 * CH_GT, 3 * CH_GT)
                        nc.gpsimd.tensor_tensor(qg[lo, b % CH_BLOCKS], qraw[lo, b % 2], qg[lo, b % CH_BLOCKS], ALU.subtract).then_inc(q_lo.sem, 1)
                        pool.wait_ge(q_lo.sem, q_lo.at(i, b + 1))
                        nc.gpsimd.tensor_tensor(ka[0:CH_ROWS, b % CH_BLOCKS, 0], kg[0:CH_ROWS, 0, :].unsqueeze(1).broadcast_to([CH_ROWS, CH_IN_GROUP, D]),
                                                spread(core.apart[0:CH_ROWS, :], D), ALU.mult).then_inc(k_apart.sem, 1)

            pool.wait_ge(s_zero, 4)
            steps5(pool, body)
            split_weights(core, pool, jobs, first, core.own)



MOE_EXPERTS, MOE_TOPK, MOE_PRIMARY, MOE_FF = 32, 8, 4, 96
MOE_SECOND = MOE_TOPK - MOE_PRIMARY
MOE_THRESHOLD = 0.5
MOE_FRONT = 16


class MoeWeights:
    def __init__(self, region):
        self.up = [region.take([P, KD, MOE_EXPERTS * 2 * MOE_FF], F16) for p in range(2)]
        self.down = [region.take([P, MOE_EXPERTS, D], F16) for p in range(2)]

    def jobs(self, core):
        out = []
        for k in range(KD):
            out += chunks(core.ins["L1_ffn_gate_up_proj"][k * P:(k + 1) * P, :], [q[:, k, :] for q in self.up])
        src = core.ins["L1_ffn_down_proj"].rearrange("f e d -> f (e d)")
        out += chunks(src, [q[0:MOE_FF].rearrange("f e d -> f (e d)") for q in self.down])
        return out


def moe_stage(core, w):
    nc, ps = core.nc, core.ps
    G, U, CW, ACC, R = (0, 1), (2, 3), 4, (5, 6), 7
    tally = lambda name, per: Tally(core, "moe_" + name, per)
    ROUTE = 15 + 4 * SUBS
    stat = tally("stat", SUBS * (2 + RSQRT_STEPS))
    normed = tally("normed", SUBS)
    xn_turned, next_hi, next_lo = tally("xn_turned", KD), tally("next_hi", KD), tally("next_lo", KD)
    routed = tally("routed", 1)
    rexp = tally("rexp", 1)
    route = tally("route", 44)
    sec_turned, sec_kept, similar = tally("sec_turned", 1), tally("sec_kept", 1), tally("similar", 1)
    cw_turned, cw_hi, cw_lo = tally("cw_turned", 1), tally("cw_hi", 1), tally("cw_lo", 1)
    moved = tally("moved", 3)
    gate_ready, up_ready, cw_ready = (tally(c, MOE_EXPERTS) for c in ("gate_ready", "up_ready", "cw_ready"))
    silu_ready = tally("silu_ready", MOE_EXPERTS)
    gated, weighed = tally("gated", MOE_EXPERTS), tally("weighed", MOE_EXPERTS)
    h_hi, h_lo = tally("h_hi", MOE_EXPERTS), tally("h_lo", MOE_EXPERTS)
    down = tally("down", MOE_EXPERTS)
    added = tally("added", SUBS)
    s_const, s_out, s_setup = core.sem("moe_const"), core.sem("out"), core.sem("moe_setup")
    region = Region(core, AT_MOE)
    sb = lambda shape, dt=F32: region.take(shape, dt)
    xnorm = sb([P, SUBS, D])
    st, mv, rstd, root = sb([P, 6]), sb([P, SUBS, 2]), sb([P, SUBS]), sb([P, 3, SUBS])
    nextT = [sb([P, KD, TOK], F16) for p in range(2)]
    xT = [sb([P, KD, TOK], F16) for p in range(2)]
    router = [sb([P, KD, MOE_EXPERTS], F16) for p in range(2)]
    router_raw = sb([P, KD, MOE_EXPERTS])
    pr = sb([P, SUBS, MOE_EXPERTS])
    s4 = sb([P, SUBS])
    best8 = sb([P, SUBS, MOE_TOPK])
    at8 = sb([P, SUBS, MOE_TOPK], I32)
    at8f = sb([P, SUBS * MOE_TOPK])
    iota = sb([P, MOE_EXPERTS])
    hot = sb([P, SUBS * MOE_TOPK, MOE_EXPERTS])
    picked = sb([P, SUBS * MOE_TOPK, MOE_EXPERTS])
    hotT = sb([P, SUBS, P])
    simdiag = sb([P, P])
    unit_diag = sb([P, P])
    cand = sb([P, SUBS * MOE_SECOND, MOE_PRIMARY])
    prod = sb([P, MOE_SECOND, MOE_PRIMARY * MOE_EXPERTS])
    take = sb([P, SUBS * MOE_SECOND, MOE_PRIMARY])
    best = sb([P, SUBS * MOE_SECOND])
    keep = sb([P, SUBS * MOE_SECOND])
    rest = sb([P, SUBS * MOE_SECOND])
    coef = sb([P, SUBS, MOE_TOPK])
    extra = sb([P, SUBS, MOE_PRIMARY])
    comb = sb([P, SUBS, MOE_EXPERTS])
    cwn = sb([P, TOK], F16)
    cwT = sb([P, TOK], F16)
    select = sb([P, MOE_EXPERTS, MOE_FF], F16)
    silu = sb([P, 2, TOK])
    h = sb([P, 2, TOK])
    hT = [sb([P, 2, TOK], F16) for p in range(2)]

    def unit(t, lag):
        return t - lag

    with nc.Block() as block:
        @block.sync
        def _(sp):
            sp.dma_start(router_raw, core.ins["L1_ffn_gate_weight"].rearrange("(k p) e -> p k e", p=P)).then_inc(s_const, 16)
            sp.dma_start(iota, core.ins["iota"]).then_inc(s_const, 16)
            sp.dma_start(select, core.ins["select"]).then_inc(s_const, 16)
            sp.wait_ge(s_setup, 1)
            for m in range(MOE_SECOND):
                r = slice(m * MOE_EXPERTS, (m + 1) * MOE_EXPERTS)
                sp.dma_start(simdiag[r, r], core.ins["L1_ffn_similarity"]).then_inc(s_const, 16)
            out = core.out.rearrange("(t p) d -> p t d", p=P)
            for i in range(STEPS):
                sp.wait_ge(added.sem, added.at(i, SUBS))
                sp.dma_start(out[:, i * SUBS:(i + 1) * SUBS, :], core.x[:, i * SUBS:(i + 1) * SUBS, :]).then_inc(s_out, 16)
            sp.wait_ge(s_out, 16 * STEPS)

        @block.tensor
        def _(pe):
            credit(pe, xn_turned, routed, sec_turned, similar, cw_turned, gate_ready, up_ready, cw_ready, down)
            pe.wait_ge(s_setup, 6)

            def body(i, alive):
                for t in range(MOE_EXPERTS):
                    if alive(t) and t in (1, 2):
                        c = t - 1
                        pe.wait_ge(normed.sem, normed.at(i, SUBS))
                        pe.wait_ge(next_lo.sem, next_lo.at(i, c))
                        pe.wait_ge(cw_lo.sem, cw_lo.at(i, 0))
                        for s in range(SUBS):
                            last = nc.tensor.transpose(ps[:, R, s * P:(s + 1) * P], xnorm[:, s, c * P:(c + 1) * P], core.ident)
                        last.then_inc(xn_turned.sem, 1)
                    if alive(t) and t == 4:
                        pe.wait_ge(next_lo.sem, next_lo.at(i, KD))
                        for s in range(SUBS):
                            for c in range(KD):
                                last = product(nc, ps[:, R, s * MOE_EXPERTS:(s + 1) * MOE_EXPERTS], [q[:, c, s * P:(s + 1) * P] for q in nextT],
                                               [q[:, c, :] for q in router], c == 0, c == KD - 1)
                        last.then_inc(routed.sem, 1)
                    if alive(t) and t == 8:
                        pe.wait_ge(route.sem, route.at(i, MOE_R_HOT))
                        for s in range(SUBS):
                            last = nc.tensor.transpose(ps[:, R, s * P:(s + 1) * P], hot[:, s * MOE_TOPK + MOE_PRIMARY:(s + 1) * MOE_TOPK, :].rearrange("p m e -> p (m e)"), core.ident)
                        last.then_inc(sec_turned.sem, 1)
                    if alive(t) and t == 9:
                        pe.wait_ge(sec_kept.sem, sec_kept.at(i, 1))
                        for s in range(SUBS):
                            last = nc.tensor.matmul(ps[:, R, s * P:(s + 1) * P], hotT[:, s, :], simdiag, start=True, stop=True)
                        last.then_inc(similar.sem, 1)
                    if alive(t) and t == 14:
                        pe.wait_ge(route.sem, route.at(i, route.per))
                        for s in range(SUBS):
                            last = nc.tensor.transpose(ps[0:MOE_EXPERTS, R, s * P:(s + 1) * P], comb[:, s, :], core.ident)
                        last.then_inc(cw_turned.sem, 1)
                    e = unit(t, MOE_FRONT)
                    if alive(e):
                        if e % MOE_EXPERTS == 0:
                            pe.wait_ge(moved.sem, moved.at(i if e == 0 else i, 3))
                        x = MOE_EXPERTS * 0
                        pe.wait_ge(silu_ready.sem, silu_ready.at(i, e - 1))
                        pe.wait_ge(gated.sem, gated.at(i, e - 1))
                        ee = e % MOE_EXPERTS
                        for off, bank, ready in ((0, G, gate_ready), (MOE_FF, U, up_ready)):
                            for c in range(KD):
                                col = ee * 2 * MOE_FF + off
                                last = product(nc, ps[0:MOE_FF, bank[e % 2], :], [q[:, c, col:col + MOE_FF] for q in w.up], [q[:, c, :] for q in xT],
                                               c == 0, c == KD - 1)
                            last.then_inc(ready.sem, 1)
                        pe.wait_ge(weighed.sem, weighed.at(i, e))
                        nc.tensor.matmul(ps[0:MOE_FF, CW, :], select[0:2 * MOE_EXPERTS, ee, :], cwT[0:2 * MOE_EXPERTS, :], start=True, stop=True).then_inc(cw_ready.sem, 1)
                    e = unit(t, MOE_FRONT + 2)
                    if alive(e) or (e >= 0 and False):
                        ee = e % MOE_EXPERTS
                        pe.wait_ge(h_lo.sem, h_lo.at(i, e + 1))
                        if ee == 0:
                            pe.wait_ge(added.sem, added.at(i, 0))
                        for s in range(SUBS):
                            last = product(nc, ps[:, ACC[s // 2], s % 2 * D:(s % 2 + 1) * D], [q[0:MOE_FF, e % 2, s * P:(s + 1) * P] for q in hT],
                                           [q[0:MOE_FF, ee, :] for q in w.down], ee == 0 and s % 2 == 0, ee == MOE_EXPERTS - 1, group=False)
                        last.then_inc(down.sem, 1)

            steps(pe, body)

        @block.scalar
        def _(act):
            credit(act, next_hi, rexp, sec_kept, cw_hi, silu_ready, h_hi)

            def body(i, alive):
                for t in range(MOE_EXPERTS):
                    if alive(t) and t in (1, 2):
                        c = t - 1
                        act.wait_ge(xn_turned.sem, xn_turned.at(i, c + 1))
                        act.wait_ge(moved.sem, moved.at(i, 0))
                        nc.scalar.activation(nextT[0][:, c, :], ps[:, R, :], ACT.Copy).then_inc(next_hi.sem, 1)
                    if alive(t) and t == 5:
                        act.wait_ge(route.sem, route.at(i, MOE_R_SHIFT))
                        nc.scalar.activation(pr, pr, ACT.Exp).then_inc(rexp.sem, 1)
                    if alive(t) and t == 8:
                        act.wait_ge(sec_turned.sem, sec_turned.at(i, 1))
                        nc.scalar.activation(hotT, ps[:, R, :].rearrange("p (s q) -> p s q", s=SUBS), ACT.Copy).then_inc(sec_kept.sem, 1)
                    if alive(t) and t == 14:
                        act.wait_ge(cw_turned.sem, cw_turned.at(i, 1))
                        nc.scalar.activation(cwn[0:MOE_EXPERTS, :], ps[0:MOE_EXPERTS, R, :], ACT.Copy).then_inc(cw_hi.sem, 1)
                    e = unit(t, MOE_FRONT + 1)
                    if alive(e):
                        act.wait_ge(weighed.sem, weighed.at(i, e + 1))
                        act.wait_ge(down.sem, down.at(i, e - 1))
                        nc.scalar.activation(hT[0][0:MOE_FF, e % 2, :], h[0:MOE_FF, e % 2, :], ACT.Copy).then_inc(h_hi.sem, 1)
                    e = unit(t, MOE_FRONT)
                    if alive(e):
                        act.wait_ge(gate_ready.sem, gate_ready.at(i, e + 1))
                        act.wait_ge(gated.sem, gated.at(i, e - 1))
                        nc.scalar.activation(silu[0:MOE_FF, e % 2, :], ps[0:MOE_FF, G[e % 2], :], ACT.Silu).then_inc(silu_ready.sem, 1)

            steps(act, body)

        @block.vector
        def _(dve):
            credit(dve, stat, normed, next_lo, route, cw_lo, moved, gated, weighed, h_lo, added)
            nc.vector.memset(simdiag, 0.0).then_inc(s_setup, 1)
            dve.wait_ge(s_const, 16 * 7)
            nc.vector.tensor_copy(router[0], router_raw).then_inc(s_setup, 1)
            dve.wait_ge(s_setup, 2)
            nc.vector.tensor_tensor(router[1], router_raw, router[0], ALU.subtract).then_inc(s_setup, 1)
            nc.vector.tensor_scalar(unit_diag, core.ident, -1.0, 1.0, ALU.mult, ALU.add).then_inc(s_setup, 1)
            dve.wait_ge(s_setup, 4)
            nc.vector.tensor_tensor(simdiag, simdiag, unit_diag, ALU.mult).then_inc(s_setup, 1)
            dve.wait_ge(s_setup, 5)
            nc.vector.tensor_tensor(simdiag, simdiag, core.ident, ALU.add).then_inc(s_setup, 1)
            dve.wait_ge(s_setup, 6)

            def router_first(i, step):
                lg = ps[:, R, 0:SUBS * MOE_EXPERTS].rearrange("p (s e) -> p s e", s=SUBS)
                step(nc.vector.tensor_reduce(s4, lg, AX.X, ALU.max))
                step(nc.vector.tensor_tensor(pr, lg, spread(s4, MOE_EXPERTS), ALU.subtract))

            def router_choose(i, step):
                step(nc.vector.tensor_reduce(s4, pr, AX.X, ALU.add))
                step(nc.vector.reciprocal(s4, s4))
                step(nc.vector.tensor_tensor(pr, pr, spread(s4, MOE_EXPERTS), ALU.mult))
                for s in range(SUBS):
                    dve.sem_inc(core.passed, 1)
                    step(nc.vector.max(best8[:, s, :], pr[:, s, :]))
                    dve.sem_inc(core.passed, 1)
                    step(nc.vector.max_index(at8[:, s, :].bitcast(mybir.dt.uint32), best8[:, s, :], pr[:, s, :]))
                step(nc.vector.tensor_copy(at8f, at8.rearrange("p s k -> p (s k)").bitcast(mybir.dt.uint32)))
                step(nc.vector.tensor_tensor(hot, iota.unsqueeze(1).broadcast_to([P, SUBS * MOE_TOPK, MOE_EXPERTS]), spread(at8f, MOE_EXPERTS), ALU.is_equal))

            def router_weights(i, step):
                step(nc.vector.tensor_reduce(s4, best8, AX.X, ALU.add))
                step(nc.vector.tensor_scalar(s4, s4, 1e-12, None, ALU.max))
                step(nc.vector.reciprocal(s4, s4))
                step(nc.vector.tensor_tensor(best8, best8, spread(s4, MOE_TOPK), ALU.mult))

            def router_similar(i, s, step):
                sim = ps[:, R, s * P:(s + 1) * P].rearrange("p (m e) -> p m e", m=MOE_SECOND)
                pv = prod.rearrange("p m (j e) -> p m j e", j=MOE_PRIMARY)
                step(nc.vector.tensor_tensor(pv, sim.unsqueeze(2).broadcast_to([P, MOE_SECOND, MOE_PRIMARY, MOE_EXPERTS]),
                                             hot[:, s * MOE_TOPK:s * MOE_TOPK + MOE_PRIMARY, :].unsqueeze(1).broadcast_to([P, MOE_SECOND, MOE_PRIMARY, MOE_EXPERTS]), ALU.mult))
                step(nc.vector.tensor_reduce(cand[:, s * MOE_SECOND:(s + 1) * MOE_SECOND, :], pv, AX.X, ALU.add))

            def router_combine(i, step):
                step(nc.vector.tensor_reduce(best, cand, AX.X, ALU.max))
                step(nc.vector.tensor_scalar(keep, best, MOE_THRESHOLD, None, ALU.is_lt))
                step(nc.vector.tensor_scalar(rest, keep, -1.0, 1.0, ALU.mult, ALU.add))
                step(nc.vector.tensor_tensor(take, cand, spread(best, MOE_PRIMARY), ALU.is_ge))
                for j in range(MOE_PRIMARY):
                    step(nc.vector.tensor_tensor(take[:, :, j], take[:, :, j], rest, ALU.mult))
                    if j < MOE_PRIMARY - 1:
                        step(nc.vector.tensor_tensor(rest, rest, take[:, :, j], ALU.subtract))
                second = best8[:, :, MOE_PRIMARY:MOE_TOPK]
                t4 = take.rearrange("p (s m) j -> p s m j", s=SUBS)
                step(nc.vector.tensor_tensor(t4, t4, spread(second, MOE_PRIMARY), ALU.mult))
                step(nc.vector.tensor_reduce(extra, take.rearrange("p (s m) j -> p s j m", s=SUBS), AX.X, ALU.add))
                step(nc.vector.tensor_tensor(coef[:, :, 0:MOE_PRIMARY], best8[:, :, 0:MOE_PRIMARY], extra, ALU.add))
                step(nc.vector.tensor_tensor(coef[:, :, MOE_PRIMARY:MOE_TOPK], second, keep.rearrange("p (s m) -> p s m", s=SUBS), ALU.mult))
                step(nc.vector.tensor_tensor(picked, hot, spread(coef.rearrange("p s k -> p (s k)"), MOE_EXPERTS), ALU.mult))
                step(nc.vector.tensor_reduce(comb, picked.rearrange("p (s k) e -> p s e k", s=SUBS), AX.X, ALU.add))

            def body(i, alive):
                done = 0

                def step(instruction):
                    nonlocal done
                    done += 1
                    instruction.then_inc(route.sem, 1)
                    dve.wait_ge(route.sem, route.at(i, done))

                for t in range(MOE_EXPERTS):
                    if alive(t) and t == 0:
                        for s in range(SUBS):
                            norm_tile(core, dve, stat, i, s, i * SUBS + s, st, mv[:, s, :], rstd[:, s:s + 1], root)
                            if s == 0:
                                dve.wait_ge(xn_turned.sem, xn_turned.at(i, 0))
                            nc.vector.tensor_scalar(xnorm[:, s, :], core.x[:, i * SUBS + s, :], mv[:, s, 0:1], rstd[:, s:s + 1],
                                                    ALU.subtract, ALU.mult).then_inc(normed.sem, 1)
                    if alive(t) and t in (1, 2):
                        c = t - 1
                        dve.wait_ge(next_hi.sem, next_hi.at(i, c + 1))
                        nc.vector.tensor_tensor(nextT[1][:, c, :], ps[:, R, :], nextT[0][:, c, :], ALU.subtract).then_inc(next_lo.sem, 1)
                    if alive(t) and t == 4:
                        dve.wait_ge(routed.sem, routed.at(i, 1))
                        router_first(i, step)
                        assert done == MOE_R_SHIFT
                    if alive(t) and t == 6:
                        dve.wait_ge(rexp.sem, rexp.at(i, 1))
                        router_choose(i, step)
                        assert done == MOE_R_HOT
                    if alive(t) and t == 7:
                        router_weights(i, step)
                    if alive(t) and t in (10, 11):
                        dve.wait_ge(similar.sem, similar.at(i, 1))
                        for s in range(2 * (t - 10), 2 * (t - 9)):
                            router_similar(i, s, step)
                    if alive(t) and t == 12:
                        router_combine(i, step)
                        assert done == route.per, done
                    if alive(t) and t == 14:
                        dve.wait_ge(cw_hi.sem, cw_hi.at(i, 1))
                        nc.vector.tensor_tensor(cwn[MOE_EXPERTS:2 * MOE_EXPERTS, :], ps[0:MOE_EXPERTS, R, :], cwn[0:MOE_EXPERTS, :], ALU.subtract).then_inc(cw_lo.sem, 1)
                    if alive(t) and t == MOE_FRONT:
                        dve.wait_ge(cw_ready.sem, cw_ready.at(i, 0))
                        dve.wait_ge(cw_lo.sem, cw_lo.at(i, 1))
                        for q in range(2):
                            nc.vector.tensor_copy(xT[q], nextT[q]).then_inc(moved.sem, 1)
                        nc.vector.tensor_copy(cwT[0:2 * MOE_EXPERTS, :], cwn[0:2 * MOE_EXPERTS, :]).then_inc(moved.sem, 1)
                    e = unit(t, MOE_FRONT)
                    if alive(e):
                        hv = h[0:MOE_FF, e % 2, :]
                        dve.wait_ge(silu_ready.sem, silu_ready.at(i, e + 1))
                        dve.wait_ge(up_ready.sem, up_ready.at(i, e + 1))
                        dve.wait_ge(h_hi.sem, h_hi.at(i, e - 1))
                        nc.vector.tensor_tensor(hv, ps[0:MOE_FF, U[e % 2], :], silu[0:MOE_FF, e % 2, :], ALU.mult).then_inc(gated.sem, 1)
                    e = unit(t, MOE_FRONT + 1)
                    if alive(e):
                        dve.wait_ge(h_hi.sem, h_hi.at(i, e + 1))
                        nc.vector.tensor_tensor(hT[1][0:MOE_FF, e % 2, :], h[0:MOE_FF, e % 2, :], hT[0][0:MOE_FF, e % 2, :], ALU.subtract).then_inc(h_lo.sem, 1)
                    e = unit(t, MOE_FRONT)
                    if alive(e):
                        hv = h[0:MOE_FF, e % 2, :]
                        dve.wait_ge(gated.sem, gated.at(i, e + 1))
                        dve.wait_ge(cw_ready.sem, cw_ready.at(i, e + 1))
                        nc.vector.tensor_tensor(hv, ps[0:MOE_FF, CW, :], hv, ALU.mult).then_inc(weighed.sem, 1)
                    e = unit(t, MOE_FRONT + 2)
                    if alive(e) and e % MOE_EXPERTS == MOE_EXPERTS - 1:
                        dve.wait_ge(down.sem, down.at(i, e + 1))
                        for s in range(SUBS):
                            tile = core.x[:, (i - 1) * SUBS + s, :]
                            nc.vector.tensor_tensor(tile, ps[:, ACC[s // 2], s % 2 * D:(s % 2 + 1) * D], tile, ALU.add).then_inc(added.sem, 1)

            steps(dve, body)


MOE_R_SHIFT, MOE_R_HOT = 2, 15


def build(nc, ins, out):
    with ExitStack() as ctx:
        core = Core(nc, ctx, ins, out)
        attn = AttnWeights(Region(core, AT_ATTN_W))
        cross = CrossWeights(Region(core, AT_CROSS_W))
        ffn_region = Region(core, AT_FFN_W)
        ffn, alibi = FfnWeights(ffn_region), AlibiWeights(ffn_region)
        moe = MoeWeights(Region(core, AT_MOE_W))
        later = [cross.jobs(core), ffn.jobs(core) + alibi.jobs(core), moe.jobs(core)]
        first = [sum(len(j) for j in later[:n]) for n in range(3)]
        with core.stage():
            attn_load(core, attn)
            attn_stage(core, attn, later[0], first[0])
        with core.stage():
            cross_stage(core, cross, later[1], first[1])
        with core.stage():
            ffn_stage(core, ffn, later[2], first[2])
        with core.stage():
            alibi_stage(core, alibi)
        with core.stage():
            channel_stage(core)
        with core.stage():
            moe_stage(core, moe)


def constants():
    half = CROSS_HD // 2
    inv = (1.0 / 10000.0 ** (np.arange(0, CROSS_HD, 2, dtype=np.float32) / CROSS_HD)).astype(np.float32)
    angle = np.outer(np.arange(S, dtype=np.float32), inv).astype(np.float32)
    angle = np.concatenate([angle, angle], -1)
    sine = np.sin(angle)
    sine[:, :half] *= -1
    query, key = np.arange(P) % S, np.arange(S)
    future = key[None, :] > query[:, None]
    mask = np.concatenate([np.zeros((P, S)), np.where(future, -1e9, 0.0)], 1)
    start = 2.0 ** (-2.0 ** (-(np.log2(ALIBI_HEADS) - 3)))
    slopes = np.array([start * start ** n for n in range(ALIBI_KVH)], np.float32)
    rel = (key[None, :] - query[:, None]).astype(np.float32)
    alibi = np.where(future[:, None, :], np.float32(-1e30), slopes[None, :, None] * rel[:, None, :])
    row = np.arange(P)
    apart = (row[:, None] % CH_GT // CH_CH == np.arange(CH_IN_GROUP)[None]) & (row[:, None] < CH_ROWS)
    apart |= row[:, None] == CH_ROWS + np.arange(CH_IN_GROUP)[None]
    select = row[:, None] % MOE_EXPERTS == np.arange(MOE_EXPERTS)[None]
    select &= row[:, None] < 2 * MOE_EXPERTS
    f32 = lambda a: np.ascontiguousarray(a, dtype=np.float32)
    return {
        "ident": np.eye(P, dtype=np.float32),
        "headmask": f32(row[:, None] // ALIBI_HD == np.arange(8)[None]),
        "cos": f32(np.tile(np.cos(angle), (2, 1))),
        "sin": f32(np.tile(sine, (2, 1))),
        "mask": f32(mask),
        "alibi": f32(alibi),
        "apart": f32(apart),
        "iota": f32(np.tile(np.arange(MOE_EXPERTS), (P, 1))),
        "select": np.ascontiguousarray(np.repeat(select[:, :, None], MOE_FF, 2), dtype=np.float16),
    }


def kernel(**inputs):
    import concourse.bacc as bacc
    from concourse.bass_utils import run_bass_kernel_spmd

    a = {name: np.asarray(value) for name, value in inputs.items()}
    a["x"] = a["x"].reshape(TOKENS, D)
    a["ctx_2048"] = a["ctx_2048"].reshape(TOKENS, D)
    a["ctxT"] = a["ctx_2048"].T
    for n in "qkv":
        a[f"L0_attn_b{n}"] = a[f"L0_attn_b{n}"].reshape(ATTN_HEADS, ATTN_HD).T
    a["L0_attn_bo"] = np.broadcast_to(a["L0_attn_bo"], (P, D))
    for n in "qk":
        a[f"L0_xattn_{n}_norm_w"] = np.broadcast_to(a[f"L0_xattn_{n}_norm_w"], (P, CROSS_HD))
    a["L1_attn_Wq"] = a["L1_attn_Wq"].reshape(D, ALIBI_KVH, 2, 2, ALIBI_HD).transpose(0, 2, 3, 1, 4).reshape(D, D)
    a["L1_attn_Wo"] = a["L1_attn_Wo"].reshape(ALIBI_KVH, 2, 2, ALIBI_HD, D).transpose(1, 2, 0, 3, 4).reshape(D, D)
    a["L1_attn_Wk"] = np.tile(a["L1_attn_Wk"], (1, 2))
    a["L1_ffn_gate_weight"] = a["L1_ffn_gate_weight"].T
    a["L1_ffn_gate_up_proj"] = a["L1_ffn_gate_up_proj"].reshape(MOE_EXPERTS * 2 * MOE_FF, D).T
    a["L1_ffn_down_proj"] = a["L1_ffn_down_proj"].transpose(2, 0, 1)
    a.update(constants())
    nc = bacc.Bacc("TRN2", target_bir_lowering=False, num_devices=1)
    arrays = {f"in_{name}": np.ascontiguousarray(value) for name, value in a.items()}
    ins = {name: nc.dram_tensor(f"in_{name}", arrays[f"in_{name}"].shape, mybir.dt.from_np(arrays[f"in_{name}"].dtype),
                                kind="ExternalInput").ap() for name in a}
    out = nc.dram_tensor("out", (TOKENS, D), F32, kind="ExternalOutput").ap()
    build(nc, ins, out)
    result = run_bass_kernel_spmd(nc, [arrays], core_ids=[0])
    return result.results[0]["out"].reshape(B, S, D)
```

```python
import numpy as np
from contextlib import ExitStack, contextmanager
import concourse.bass as bass
from concourse import mybir

F32 = mybir.dt.float32
F16 = mybir.dt.float16
I32 = mybir.dt.int32
BF16 = mybir.dt.bfloat16
ALU = mybir.AluOpType
ACT = mybir.ActivationFunctionType
AX = mybir.AxisListType

P = 128
B, S, D = 32, 64, 256
TOKENS = B * S
KD = D // P
TILES = TOKENS // P
SUBS = 4
STEPS = TILES // SUBS
TOK = SUBS * P
LN_EPS = 1e-5


class Tally:

    def __init__(self, core, name, per):
        self.sem = core.sem(name)
        self.per = per

    def at(self, i, k):
        return i * self.per + (self.per + k)

    def before(self, i, k):
        return i * self.per + k


KB = 1024
AT_BASE = (0, 26 * KB)
AT_ATTN_W, AT_CROSS_W, AT_FFN_W, AT_MOE_W = (125 * KB, 157 * KB), (157 * KB, 205 * KB), (26 * KB, 56 * KB), (125 * KB, 205 * KB)
AT_ATTN, AT_CROSS, AT_FFN, AT_MOE = (26 * KB, 125 * KB), (56 * KB, 157 * KB), (56 * KB, 125 * KB), (26 * KB, 125 * KB)
AT_CHANNEL = (26 * KB, 125 * KB)
CHUNK = 1024


class Region:

    def __init__(self, core, at):
        self.arena, (self.next, self.end) = core.arena, at

    def take(self, shape, dt):
        size = int(np.prod(shape[1:])) * (4 if dt in (F32, I32) else 2)
        size = (size + 31) // 32 * 32
        assert self.next + size <= self.end, (self.next, size, self.end)
        view = self.arena[:, self.next // 4:(self.next + size) // 4]
        if dt != F32:
            view = view.bitcast(dt)
        self.next += size
        view = view[:, 0:int(np.prod(shape[1:]))]
        if len(shape) > 2:
            names = "abcde"[:len(shape) - 1]
            view = view.rearrange(f"p ({' '.join(names)}) -> p {' '.join(names)}", **dict(zip(names, shape[1:])))
        return view[0:shape[0]]


class Core:

    def __init__(self, nc, ctx, ins, out):
        self.nc, self.ctx, self.ins, self.out = nc, ctx, ins, out
        self.sems = []
        self.arena = ctx.enter_context(nc.sbuf_tensor("arena", [P, 205 * KB // 4], F32))
        self.ps = ctx.enter_context(nc.psum_tensor("ps", [P, 8, 512], F32))
        base = Region(self, AT_BASE)
        self.x = base.take([P, TILES, D], F32)
        self.staging = base.take([P, 2, CHUNK], F32)
        self.ident = base.take([P, P], F32)
        self.headmask = base.take([P, 8], F32)
        self.apart = base.take([P, 8], F32)
        self.stats = base.take([P, TILES, 6], F32)
        self.meanvar = base.take([P, TILES, 2], F32)
        self.rstd = base.take([P, TILES, 1], F32)
        self.root = base.take([P, 3, TILES], F32)
        self.s_staged = [self.sem("staged0"), self.sem("staged1")]
        self.s_split = self.sem("split")
        self.own = self.sem("split_hi")
        self.passed = self.sem("passed")

    def sem(self, name):
        handle = self.nc.alloc_semaphore(name)
        self.sems.append(handle)
        return handle

    @contextmanager
    def stage(self):
        kept, self.sems = self.sems, []
        yield
        self.nc.clear_and_free_semaphores(self.sems)
        self.sems = kept
        self.nc.all_engine_barrier()


def chunks(src, parts):
    step = min(CHUNK, src.shape[1])
    return [(src[:, c:c + step], *(p[:, c:c + step] for p in parts)) for c in range(0, src.shape[1], step)]


def stage_weights(core, sp, jobs, first):
    for j, (src, hi, lo) in enumerate(jobs, first):
        if j >= 2:
            sp.wait_ge(core.s_split, j - 1)
        core.nc.sync.dma_start(core.staging[0:src.shape[0], j % 2, 0:src.shape[1]], src).then_inc(core.s_staged[j % 2], 16)


def split_weights(core, pool, jobs, first, own):
    nc = core.nc
    for j, (src, hi, lo) in enumerate(jobs, first):
        raw = core.staging[0:src.shape[0], j % 2, 0:src.shape[1]]
        pool.wait_ge(core.s_staged[j % 2], 16 * (j // 2 + 1))
        nc.gpsimd.tensor_copy(hi, raw).then_inc(own, 1)
        pool.wait_ge(own, j + 1)
        nc.gpsimd.tensor_tensor(lo, raw, hi, ALU.subtract).then_inc(core.s_split, 1)
        pool.wait_ge(core.s_split, j + 1)


RSQRT_STEPS = 12


def rsqrt(core, dve, tally, i, k, var, eps, out, tmp):
    nc = core.nc
    v, t, u = (tmp[:, j, 0:out.shape[1]] for j in range(3))
    def step(instruction):
        nonlocal k
        instruction.then_inc(tally.sem, 1)
        k += 1
        dve.wait_ge(tally.sem, tally.at(i, k))
    dve.wait_ge(tally.sem, tally.at(i, k))
    step(nc.vector.tensor_scalar(v, var, eps, None, ALU.add))
    step(nc.vector.tensor_scalar(t.bitcast(I32), v.bitcast(I32), 1, None, ALU.logical_shift_right))
    step(nc.vector.tensor_scalar(out.bitcast(I32), t.bitcast(I32), -1.0, float(0x5F3759DF), ALU.mult, ALU.add))
    for _ in range(3):
        step(nc.vector.scalar_tensor_tensor(out=t, in0=out, scalar=-0.5, in1=v, op0=ALU.mult, op1=ALU.mult))
        step(nc.vector.tensor_tensor(u, t, out, ALU.mult))
        step(nc.vector.scalar_tensor_tensor(out=out, in0=u, scalar=1.5, in1=out, op0=ALU.add, op1=ALU.mult))


def measure(core, dve, tile):
    dve.sem_inc(core.passed, 1)
    core.nc.vector.bn_stats(core.stats[:, tile, :], core.x[:, tile, :])


def settle(core, dve, name):
    nc = core.nc
    settled = Tally(core, name + "_settled", 0)
    for t in range(TILES):
        nc.vector.bn_aggr(core.meanvar[:, t, :], core.stats[:, t, :]).then_inc(settled.sem, 1)
    rsqrt(core, dve, settled, 0, TILES, core.meanvar[:, :, 1], LN_EPS, core.rstd[:, :, 0], core.root)


def normalise(core, dve, out, tile):
    return core.nc.vector.tensor_scalar(out, core.x[:, tile, :], core.meanvar[:, tile, 0:1], core.rstd[:, tile, :],
                                        ALU.subtract, ALU.mult)


def spread(ap, n):
    return ap.unsqueeze(len(ap.shape)).broadcast_to([*ap.shape, n])


def steps(engine, body):
    body(0, lambda k: k >= 0)
    with engine.Fori(1, STEPS) as i:
        body(i, lambda k: True)
    body(STEPS, lambda k: k < 0)


def credit(eng, *tallies):
    for t in tallies:
        eng.sem_inc(t.sem, t.per)


def product(nc, out, stationary, moving, start, stop, group=True):
    pairs = [(a, b) for x, a in enumerate(stationary) for y, b in enumerate(moving) if x + y < 2]
    for n, (a, b) in enumerate(pairs):
        last = nc.tensor.matmul(out, a, b, start=start and n == 0, stop=stop and n == len(pairs) - 1,
                                skip_group_check=not group)
    return last



ATTN_HEADS, ATTN_HD = 16, 128
ATTN_FEAT = ATTN_HEADS * ATTN_HD
ATTN_SCALE = 1.0 / float(np.sqrt(ATTN_HD))
ATTN_GROUP = 4
ATTN_RING = 4
ATTN_RAWS = 4
ATTN_SMALL = 6 * 16
ATTN_PER_GROUP = 3 * KD + 1
ATTN_BLOCK = 32


class AttnWeights:

    def __init__(self, region):
        self.qkv = region.take([P, 3, KD, ATTN_FEAT], BF16)
        self.out = region.take([P, ATTN_HEADS, D], BF16)

    def raw(self, core):
        out = []
        for g in range(ATTN_HEADS // ATTN_GROUP):
            cols = slice(g * ATTN_GROUP * ATTN_HD, (g + 1) * ATTN_GROUP * ATTN_HD)
            for n, name in enumerate("qkv"):
                for k in range(KD):
                    out.append((core.ins[f"L0_attn_w{name}_codes"][k * P:(k + 1) * P, cols],
                                core.ins[f"L0_attn_w{name}_scales"][k * 4:(k + 1) * 4, cols], self.qkv[:, n, k, cols]))
            rows = slice(g * ATTN_GROUP, (g + 1) * ATTN_GROUP)
            out.append((core.ins["L0_attn_wo_codes"].rearrange("(t p) d -> p t d", p=P)[:, rows, :],
                        core.ins["L0_attn_wo_scales"].rearrange("(t b) d -> b t d", b=4)[:, rows, :], self.out[:, rows, :]))
        return out


def attn_stage(core, w, jobs=(), first=0):
    nc, ps = core.nc, core.ps
    Q, K, V, SC, T, O, A = 0, 1, 2, 3, 4, 5, (6, 7)
    region = Region(core, AT_ATTN)
    sb = lambda shape, dt=F32: region.take(shape, dt)
    bias, bo = sb([P, 3, ATTN_HEADS]), sb([P, D])
    x_all = [sb([P, STEPS, KD, TOK], F16) for p in range(2)]
    xT = [sb([P, KD, TOK], F16) for p in range(2)]
    xnorm = sb([P, ATTN_RING, D])
    codes, scales = (sb([P, ATTN_RAWS, CHUNK]) for _ in range(2))
    qT, kT = (sb([P, 2, TOK]) for _ in range(2))
    v = sb([P, 2, SUBS, ATTN_GROUP * ATTN_HD])
    top, total, inv = (sb([P, 2, SUBS]) for _ in range(3))
    shift, e = (sb([P, 2, SUBS, S]) for _ in range(2))
    prob = sb([P, 2, SUBS, P])
    pT = sb([P, 2, TOK])
    oT = [sb([P, 2, TOK], F16) for p in range(2)]
    scores = ps[:, SC, :].rearrange("p (b s k) -> p b s k", b=2, k=S)
    sem = lambda name: core.sem("attn_" + name)
    x_in = [sem(f"x_in{j}") for j in range(STEPS)]
    s_small, s_cleared = sem("small_in"), sem("cleared")
    s_raw = [sem(f"raw{j}") for j in range(ATTN_RAWS)]
    s_made = sem("made")
    s_normed, s_turned, s_hi, s_lo, s_biased = (sem(c) for c in ("normed", "x_turned", "x_hi", "x_lo", "biased"))
    tally = lambda name, per: Tally(core, "attn_" + name, per)
    x_set = tally("x_set", 2)
    q_ready, k_ready, v_ready = (tally(f"{c}_ready", ATTN_HEADS) for c in "qkv")
    q_kept, v_kept = tally("q_kept", ATTN_HEADS), tally("v_kept", ATTN_HEADS)
    k_kept = tally("k_kept", ATTN_HEADS)
    scored = tally("scored", ATTN_HEADS)
    maxed, shifted, summed, inverse = (tally(c, ATTN_HEADS) for c in ("maxed", "shifted", "summed", "inverse"))
    exped = tally("exped", ATTN_HEADS)
    probs = tally("probs", 2 * ATTN_HEADS)
    turned = tally("probs_turned", ATTN_HEADS)
    pT_kept = tally("pT_kept", ATTN_HEADS)
    mixed = tally("mixed", ATTN_HEADS)
    o_hi = tally("o_hi", ATTN_HEADS)
    o_lo = tally("o_lo", ATTN_HEADS)
    projected = tally("projected", ATTN_HEADS)
    added = tally("added", SUBS)
    raw = w.raw(core)

    with nc.Block() as block:
        @block.sync
        def _(sp):
            x = core.ins["x"].rearrange("(t p) d -> p t d", p=P)
            for j in range(STEPS):
                part = slice(j * SUBS, (j + 1) * SUBS)
                sp.dma_start(core.x[:, part, :], x[:, part, :]).then_inc(x_in[j], 16)
            sp.dma_start(core.ident[:, :], core.ins["ident"]).then_inc(s_small, 16)
            sp.dma_start(core.headmask, core.ins["headmask"]).then_inc(s_small, 16)
            for n, name in enumerate("qkv"):
                sp.dma_start(bias[:, n, :], core.ins[f"L0_attn_b{name}"]).then_inc(s_small, 16)
            sp.dma_start(bo[:, :], core.ins["L0_attn_bo"]).then_inc(s_small, 16)
            for j, (src, sc, dst) in enumerate(raw):
                if j >= ATTN_RAWS:
                    sp.wait_ge(s_made, j - ATTN_RAWS + 1)
                to, ts = (q[:, j % ATTN_RAWS, 0:int(np.prod(src.shape[1:]))] for q in (codes, scales))
                if len(src.shape) == 3:
                    to, ts = (q.rearrange("p (t d) -> p t d", d=D) for q in (to, ts))
                sp.dma_start(to, src).then_inc(s_raw[j % ATTN_RAWS], 16)
                for b in range(P // ATTN_BLOCK):
                    sp.dma_start(ts[b * ATTN_BLOCK:(b + 1) * ATTN_BLOCK], sc[b].partition_broadcast(ATTN_BLOCK)).then_inc(s_raw[j % ATTN_RAWS], 16)
            stage_weights(core, sp, jobs, first)

        @block.tensor
        def _(pe):
            credit(pe, q_ready, k_ready, v_ready, scored, turned, mixed, projected)
            pe.wait_ge(s_small, ATTN_SMALL)
            for t in range(TILES):
                pe.wait_ge(s_normed, t + 1)
                if t >= ATTN_RING:
                    pe.wait_ge(s_lo, t - ATTN_RING + 1)
                for k in range(KD):
                    last = nc.tensor.transpose(ps[:, (Q, K, V, SC)[t % ATTN_RING], k * P:(k + 1) * P], xnorm[:, t % ATTN_RING, k * P:(k + 1) * P], core.ident)
                last.then_inc(s_turned, 1)
            pe.wait_ge(s_lo, TILES)

            def body(i, alive):
                for t in range(ATTN_HEADS):
                    h = t - 1
                    if alive(h):
                        pe.wait_ge(q_kept.sem, q_kept.at(i, h + 1))
                        pe.wait_ge(k_kept.sem, k_kept.at(i, h + 1))
                        pe.wait_ge(shifted.sem, shifted.at(i, h))
                        for s in range(SUBS):
                            for b in range(2):
                                c = s * P + b * S
                                last = nc.tensor.matmul(scores[b * S:(b + 1) * S, h % 2, s, :], qT[:, h % 2, c:c + S],
                                                        kT[:, h % 2, c:c + S], start=True, stop=True)
                        last.then_inc(scored.sem, 1)
                    h = t - 3
                    if alive(h):
                        pe.wait_ge(probs.sem, probs.at(i, 2 * h + 2))
                        pe.wait_ge(pT_kept.sem, pT_kept.at(i, h))
                        for s in range(SUBS):
                            last = nc.tensor.transpose(ps[:, T, s * P:(s + 1) * P], prob[:, h % 2, s, :], core.ident[:, :])
                        last.then_inc(turned.sem, 1)
                    if alive(t):
                        h, g, s = t, t // ATTN_GROUP, t % ATTN_GROUP
                        if t == 0:
                            pe.wait_ge(x_set.sem, x_set.at(i, 2))
                        if s == 0:
                            pe.wait_ge(s_made, ATTN_PER_GROUP * g + 6)
                        for c, bank, kept, ready in ((0, Q, q_kept, q_ready), (1, K, k_kept, k_ready)):
                            pe.wait_ge(kept.sem, kept.at(i, h))
                            for k in range(KD):
                                last = product(nc, ps[:, bank, :], [w.qkv[:, c, k, h * ATTN_HD:(h + 1) * ATTN_HD]], [q[:, k, :] for q in xT],
                                               k == 0, k == KD - 1)
                            last.then_inc(ready.sem, 1)
                        pe.wait_ge(v_kept.sem, v_kept.at(i, t))
                        for k in range(KD):
                            last = product(nc, ps[:, V, :], [q[:, k, s * P:(s + 1) * P] for q in xT],
                                           [w.qkv[:, 2, k, g * ATTN_GROUP * ATTN_HD:(g + 1) * ATTN_GROUP * ATTN_HD]], k == 0, k == KD - 1)
                        last.then_inc(v_ready.sem, 1)
                    h = t - 3
                    if alive(h):
                        g = h // ATTN_GROUP
                        pe.wait_ge(pT_kept.sem, pT_kept.at(i, h + 1))
                        pe.wait_ge(v_kept.sem, v_kept.at(i, (g + 1) * ATTN_GROUP))
                        pe.wait_ge(o_lo.sem, o_lo.at(i, h))
                        for s in range(SUBS):
                            last = nc.tensor.matmul(ps[:, O, s * P:(s + 1) * P], v[:, g % 2, s, h % ATTN_GROUP * ATTN_HD:(h % ATTN_GROUP + 1) * ATTN_HD],
                                                    pT[:, h % 2, s * P:(s + 1) * P], start=True, stop=True)
                        last.then_inc(mixed.sem, 1)
                    h = t - 4
                    if alive(h):
                        hh = h % ATTN_HEADS
                        pe.wait_ge(o_hi.sem, o_hi.at(i, h + 1))
                        pe.wait_ge(o_lo.sem, o_lo.at(i, h + 1))
                        if hh == 0:
                            pe.wait_ge(added.sem, added.at(i, 0))
                        if hh % ATTN_GROUP == 0:
                            pe.wait_ge(s_made, ATTN_PER_GROUP * (hh // ATTN_GROUP + 1))
                        for s in range(SUBS):
                            last = product(nc, ps[:, A[s // 2], s % 2 * D:(s % 2 + 1) * D], [q[:, h % 2, s * P:(s + 1) * P] for q in oT],
                                           [w.out[:, hh, :]], hh == 0 and s % 2 == 0, hh == ATTN_HEADS - 1, group=False)
                        last.then_inc(projected.sem, 1)

            steps(pe, body)

        @block.scalar
        def _(act):
            credit(act, q_kept, v_kept, exped, pT_kept, o_hi)
            for t in range(TILES):
                act.wait_ge(s_turned, t + 1)
                nc.scalar.activation(x_all[0][:, t // SUBS, :, t % SUBS * P:(t % SUBS + 1) * P],
                                     ps[:, (Q, K, V, SC)[t % ATTN_RING], 0:D].rearrange("p (k q) -> p k q", q=P), ACT.Copy).then_inc(s_hi, 1)
            act.wait_ge(s_small, ATTN_SMALL)

            def body(i, alive):
                for t in range(ATTN_HEADS):
                    h = t - 1
                    if alive(h):
                        act.wait_ge(shifted.sem, shifted.at(i, h + 1))
                        act.wait_ge(probs.sem, probs.at(i, 2 * h - 2))
                        nc.scalar.activation(e[:, h % 2], shift[:, h % 2], ACT.Exp, scale=ATTN_SCALE).then_inc(exped.sem, 1)
                    h = t - 3
                    if alive(h):
                        act.wait_ge(turned.sem, turned.at(i, h + 1))
                        act.wait_ge(mixed.sem, mixed.at(i, h - 1))
                        nc.scalar.activation(pT[:, h % 2, :], ps[:, T, :], ACT.Copy).then_inc(pT_kept.sem, 1)
                    if alive(t):
                        h, g, s = t, t // ATTN_GROUP, t % ATTN_GROUP
                        act.wait_ge(q_ready.sem, q_ready.at(i, h + 1))
                        act.wait_ge(scored.sem, scored.at(i, h - 1))
                        nc.scalar.activation(qT[:, h % 2, :], ps[:, Q, :], ACT.Identity, bias=bias[:, 0, h:h + 1]).then_inc(q_kept.sem, 1)
                        act.wait_ge(v_ready.sem, v_ready.at(i, t + 1))
                        act.wait_ge(mixed.sem, mixed.at(i, (g - 1) * ATTN_GROUP))
                        nc.scalar.activation(v[:, g % 2, s, :], ps[:, V, :], ACT.Copy).then_inc(v_kept.sem, 1)
                    h = t - 3
                    if alive(h):
                        hh = h % ATTN_HEADS
                        act.wait_ge(mixed.sem, mixed.at(i, h + 1))
                        act.wait_ge(projected.sem, projected.at(i, h - 1))
                        nc.scalar.activation(oT[0][:, h % 2, :], ps[:, O, :], ACT.Identity, bias=bias[:, 2, hh:hh + 1]).then_inc(o_hi.sem, 1)

            steps(act, body)

        @block.vector
        def _(dve):
            credit(dve, x_set, k_kept, maxed, shifted, summed, inverse, o_lo, added)
            for t in range(TILES):
                if t % SUBS == 0:
                    dve.wait_ge(x_in[t // SUBS], 16)
                measure(core, dve, t)
            dve.drain()
            settle(core, dve, "attn")
            lag = 2
            for t in range(TILES + lag):
                if t < TILES:
                    if t >= ATTN_RING:
                        dve.wait_ge(s_turned, t - ATTN_RING + 1)
                    normalise(core, dve, xnorm[:, t % ATTN_RING, :], t).then_inc(s_normed, 1)
                if t >= lag:
                    c = t - lag
                    dve.wait_ge(s_hi, c + 1)
                    part = (slice(None), c // SUBS, slice(None), slice(c % SUBS * P, (c % SUBS + 1) * P))
                    nc.vector.tensor_tensor(x_all[1][part], ps[:, (Q, K, V, SC)[c % ATTN_RING], 0:D].rearrange("p (k q) -> p k q", q=P),
                                            x_all[0][part], ALU.subtract).then_inc(s_lo, 1)
            dve.wait_ge(s_lo, TILES)
            dve.wait_ge(s_small, ATTN_SMALL)

            def body(i, alive):
                for t in range(ATTN_HEADS):
                    if alive(t) and t == 0:
                        dve.wait_ge(k_ready.sem, k_ready.at(i, 0))
                        dve.wait_ge(v_ready.sem, v_ready.at(i, 0))
                        dve.sem_inc(core.passed, 1)
                        for p in range(2):
                            nc.vector.tensor_copy(xT[p], x_all[p][:, i]).then_inc(x_set.sem, 1)
                    h = t - 1
                    if alive(h):
                        dve.wait_ge(scored.sem, scored.at(i, h + 1))
                        nc.vector.tensor_reduce(top[:, h % 2, :], scores[:, h % 2], AX.X, ALU.max).then_inc(maxed.sem, 1)
                        dve.wait_ge(maxed.sem, maxed.at(i, h + 1))
                        dve.wait_ge(exped.sem, exped.at(i, h - 1))
                        nc.vector.tensor_tensor(shift[:, h % 2], scores[:, h % 2], spread(top[:, h % 2, :], S), ALU.subtract).then_inc(shifted.sem, 1)
                        dve.wait_ge(exped.sem, exped.at(i, h + 1))
                        dve.wait_ge(probs.sem, probs.at(i, 2 * h - 2))
                        nc.vector.tensor_reduce(total[:, h % 2, :], e[:, h % 2], AX.X, ALU.add).then_inc(summed.sem, 1)
                        dve.wait_ge(summed.sem, summed.at(i, h + 1))
                        nc.vector.reciprocal(inv[:, h % 2, :], total[:, h % 2, :]).then_inc(inverse.sem, 1)
                    if alive(t):
                        h = t
                        dve.wait_ge(k_ready.sem, k_ready.at(i, h + 1))
                        dve.wait_ge(scored.sem, scored.at(i, h - 1))
                        nc.vector.tensor_scalar(kT[:, h % 2, :], ps[:, K, :], bias[:, 1, h:h + 1], None, ALU.add).then_inc(k_kept.sem, 1)
                    h = t - 3
                    if alive(h):
                        hh = h % ATTN_HEADS
                        dve.wait_ge(o_hi.sem, o_hi.at(i, h + 1))
                        dve.wait_ge(projected.sem, projected.at(i, h - 1))
                        nc.vector.scalar_tensor_tensor(out=oT[1][:, h % 2, :], in0=ps[:, O, :], scalar=bias[:, 2, hh:hh + 1], in1=oT[0][:, h % 2, :],
                                                       op0=ALU.add, op1=ALU.subtract).then_inc(o_lo.sem, 1)
                    if alive(t - 4) and t == 3:
                        dve.wait_ge(s_biased, TILES)
                        dve.wait_ge(projected.sem, projected.at(i, 0))
                        for s in range(SUBS):
                            xs = core.x[:, (i - 1) * SUBS + s, :]
                            nc.vector.tensor_tensor(xs, ps[:, A[s // 2], s % 2 * D:(s % 2 + 1) * D], xs, ALU.add).then_inc(added.sem, 1)
                        for s in range(SUBS):
                            dve.wait_ge(added.sem, added.before(i, s + 1))
                            measure(core, dve, (i - 1) * SUBS + s)

            steps(dve, body)

        @block.gpsimd
        def _(pool):
            credit(pool, probs)
            nc.gpsimd.memset(prob[:, :, :, :], 0.0).then_inc(s_cleared, 1)
            pool.wait_ge(s_cleared, 1)

            def make(j):
                src, sc, dst = raw[j]
                pool.wait_ge(s_raw[j % ATTN_RAWS], 80 * (j // ATTN_RAWS + 1))
                a, b = (q[:, j % ATTN_RAWS, 0:int(np.prod(src.shape[1:]))] for q in (codes, scales))
                if len(src.shape) == 3:
                    a, b = (q.rearrange("p (t d) -> p t d", d=D) for q in (a, b))
                nc.gpsimd.tensor_tensor(dst, a, b, ALU.mult).then_inc(s_made, 1)

            for j in range(ATTN_PER_GROUP):
                make(j)
            pool.wait_ge(s_made, ATTN_PER_GROUP)
            assert ATTN_HEADS == TILES
            done, later = ATTN_PER_GROUP, 0
            for i in range(STEPS + 1):
                alive = (lambda k: k >= 0) if i == 0 else (lambda k: k < 0) if i == STEPS else (lambda k: True)
                for t in range(ATTN_HEADS):
                    h = t - 1
                    if done < len(raw):
                        if alive(h - 1):
                            pool.wait_ge(probs.sem, probs.at(i, 2 * h))
                        for j in range(done, min(len(raw), done + 2)):
                            make(j)
                            done += 1
                        pool.wait_ge(s_made, done)
                    if alive(h):
                        pool.wait_ge(inverse.sem, inverse.at(i, h + 1))
                        pool.wait_ge(turned.sem, turned.at(i, h - 1))
                        for b in range(2):
                            r = slice(b * S, (b + 1) * S)
                            nc.gpsimd.tensor_tensor(prob[r, h % 2, :, b * S:(b + 1) * S], e[r, h % 2], spread(inv[r, h % 2, :], S),
                                                    ALU.mult).then_inc(probs.sem, 1)
                    if i == 0:
                        if alive(h):
                            pool.wait_ge(probs.sem, probs.at(i, 2 * h + 2))
                        pool.wait_ge(s_normed, t + 1)
                        pool.wait_ge(s_small, ATTN_SMALL)
                        nc.gpsimd.tensor_tensor(core.x[:, t, :], core.x[:, t, :], bo, ALU.add).then_inc(s_biased, 1)
                        pool.wait_ge(s_biased, t + 1)
                    if 1 <= i < STEPS and later < len(jobs):
                        pool.wait_ge(probs.sem, probs.at(i, 2 * h + 2))
                        split_weights(core, pool, jobs[later:later + 1], first + later, core.own)
                        later += 1
            assert later == len(jobs)



CROSS_HEADS, CROSS_KVH, CROSS_HD = 16, 4, 128
CROSS_REP = CROSS_HEADS // CROSS_KVH
CROSS_GW = CROSS_REP * CROSS_HD
CROSS_SCALE = 1.0 / float(np.sqrt(CROSS_HD))
CROSS_RMS_EPS = 1e-6
CROSS_UNITS = SUBS * CROSS_KVH
CROSS_TURNS = 2 + CROSS_KVH
CROSS_NORMS = 2 * CROSS_KVH + CROSS_HEADS
CROSS_KEYS = 2 * S


class CrossWeights:
    def __init__(self, region):
        self.q = [region.take([P, KD, CROSS_HEADS * CROSS_HD], F16) for p in range(2)]
        self.kv = [region.take([P, 4, KD, CROSS_KVH * CROSS_HD], F16) for p in range(2)]
        self.out = [region.take([P, CROSS_HEADS, D], F16) for p in range(2)]

    def jobs(self, core):
        out = []
        for k in range(KD):
            out += chunks(core.ins["L0_xattn_wq"][k * P:(k + 1) * P, :], [q[:, k, :] for q in self.q])
        for n, name in enumerate(("wk_ctx", "wk", "wv_ctx", "wv")):
            for k in range(KD):
                out += chunks(core.ins["L0_xattn_" + name][k * P:(k + 1) * P, :], [q[:, n, k, :] for q in self.kv])
        for t in range(CROSS_HEADS):
            out += chunks(core.ins["L0_xattn_wo"][t * P:(t + 1) * P, :], [q[:, t, :] for q in self.out])
        return out


def cross_stage(core, w, jobs=(), first=0):
    nc, ps = core.nc, core.ps
    QP, KVP, TQ, SC, PT, O, ACC, LNB = range(8)
    tally = lambda name, per: Tally(core, "x_" + name, per)
    xn = tally("xn", SUBS)
    xn_turned = tally("xn_turned", SUBS)
    x_hi = tally("x_hi", SUBS)
    x_lo = tally("x_lo", SUBS)
    c_hi, c_lo = tally("c_hi", SUBS), tally("c_lo", SUBS)
    kv_ready, q_ready = tally("kv_ready", CROSS_UNITS), tally("q_ready", CROSS_UNITS)
    kv_kept, q_kept = tally("kv_kept", CROSS_UNITS), tally("q_kept", CROSS_UNITS)
    squared = tally("squared", SUBS * CROSS_TURNS)
    summed = tally("summed", SUBS * CROSS_TURNS)
    rooted = tally("rooted", SUBS * RSQRT_STEPS)
    roped = tally("roped", SUBS * CROSS_TURNS)
    joined = tally("joined", SUBS * CROSS_TURNS)
    scaled = tally("scaled", SUBS * CROSS_TURNS)
    turned, turn_kept = tally("turned", SUBS * CROSS_TURNS), tally("turn_kept", SUBS * CROSS_TURNS)
    scored = tally("scored", CROSS_UNITS)
    maxed, shifted, totalled, inverse = (tally(c, CROSS_UNITS) for c in ("maxed", "shifted", "totalled", "inverse"))
    exped = tally("exped", CROSS_UNITS)
    probs = tally("probs", CROSS_UNITS)
    p_turned, pT_kept = tally("p_turned", CROSS_UNITS), tally("pT_kept", CROSS_UNITS)
    mixed, o_hi, o_lo = tally("mixed", CROSS_UNITS), tally("o_hi", CROSS_UNITS), tally("o_lo", CROSS_UNITS)
    projected = tally("projected", CROSS_UNITS)
    added = tally("added", SUBS)
    s_ctx = [core.sem("x_ctx0"), core.sem("x_ctx1")]
    s_const, s_tables = core.sem("x_const"), core.sem("x_tables")
    L_TURN, L_PROJ, L_ROPE, L_FLIP, L_SCORE, L_PROB, L_PTURN, L_MIX, L_OUT = 1, 4, 8, 9, 11, 12, 13, 14, 15
    region = Region(core, AT_CROSS)
    with ExitStack() as own:
        def sb(name, shape, dt):
            return region.take(shape, dt)
        xT = [sb(f"xT{p}", [P, 2, KD, P], F16) for p in range(2)]
        cT = [sb(f"cT{p}", [P, 2, KD, P], F16) for p in range(2)]
        xnorm = sb("xnorm", [P, 2, D], F32)
        root = sb("root", [P, 3, CROSS_NORMS], F32)
        qs = sb("qs", [P, 2, CROSS_KVH, CROSS_GW], F32)
        ks = sb("ks", [P, 2, CROSS_KVH * CROSS_HD], F32)
        cRaw = sb("cRaw", [P, 2, KD, P], F32)
        v = sb("v", [P, SUBS, 2, CROSS_KVH * CROSS_HD], F32)
        square = sb("square", [P, 2, CROSS_GW], F32)
        sums, rms = sb("sums", [P, 2, CROSS_NORMS], F32), sb("rms", [P, 2, CROSS_NORMS], F32)
        ropeA, ropeB = sb("ropeA", [P, 4, CROSS_GW], F32), sb("ropeB", [P, 2, CROSS_GW], F32)
        kT = sb("kT", [P, 2, CROSS_KVH, 2, CROSS_KEYS], F32)
        qT = sb("qT", [P, 2, 2, CROSS_REP * S], F32)
        top, total, inv = (sb(c, [P, 2, 4], F32) for c in ("top", "total", "inv"))
        shift, prob = (sb(c, [P, 2, 4, CROSS_KEYS], F32) for c in ("shift", "prob"))
        e = shift
        pT = sb("pT", [P, 2, 2, CROSS_REP * S], F32)
        oT = [sb(f"oT{p}", [P, 2, CROSS_REP, P], F16) for p in range(2)]
        raw = sb("raw", [P, 4, CROSS_HD], F32)
        table = sb("table", [P, 2, 2, CROSS_HD], F32)
        mask = sb("mask", [P, 4, CROSS_KEYS], BF16)
        maskf = sb("maskf", [P, CROSS_KEYS], F32)
        ident = sb("ident", [P, P], BF16)
        block = own.enter_context(nc.Block())

        def turns_at(g):
            return ([0, 1], [2], [3, 4], [5])[g]

        def unit(t, lag):
            k = t - lag
            return k, k // CROSS_KVH, k % CROSS_KVH

        @block.sync
        def _(sp):
            for n, name in enumerate(("cos", "sin", "L0_xattn_q_norm_w", "L0_xattn_k_norm_w")):
                sp.dma_start(raw[:, n, :], core.ins[name]).then_inc(s_const, 16)
            sp.dma_start(maskf[:, :], core.ins["mask"]).then_inc(s_const, 16)
            stage_weights(core, sp, jobs, first)

        @block.tensor
        def _(pe):
            credit(pe, xn_turned, kv_ready, q_ready, turned, scored, p_turned, mixed, projected)

            def body(i, alive):
                for t in range(CROSS_UNITS):
                    k, s, g = unit(t, L_TURN)
                    if alive(k) and g == 0:
                        pe.wait_ge(xn.sem, xn.at(i, s + 1))
                        pe.wait_ge(x_lo.sem, x_lo.at(i, s))
                        for c in range(KD):
                            last = nc.tensor.transpose(ps[:, LNB, c * P:(c + 1) * P], xnorm[:, s % 2, c * P:(c + 1) * P], core.ident[:, :])
                        last.then_inc(xn_turned.sem, 1)
                    k, s, g = unit(t, L_PROJ)
                    if alive(k):
                        src = cT if g % 2 == 0 else xT
                        if g == 0:
                            pe.wait_ge(c_lo.sem, c_lo.at(i, s + 1))
                            pe.wait_ge(x_lo.sem, x_lo.at(i, s + 1))
                        pe.wait_ge(kv_kept.sem, kv_kept.at(i, k))
                        for c in range(KD):
                            last = product(nc, ps[:, KVP, :], [q[:, s % 2, c, :] for q in src], [q[:, g, c, :] for q in w.kv], c == 0, c == KD - 1)
                        last.then_inc(kv_ready.sem, 1)
                        pe.wait_ge(q_kept.sem, q_kept.at(i, k))
                        pe.wait_ge(squared.sem, squared.at(i, CROSS_TURNS * s + min(g, 2) + g))
                        for c in range(KD):
                            last = product(nc, ps[:, QP, :], [q[:, s % 2, c, :] for q in xT], [q[:, c, g * CROSS_GW:(g + 1) * CROSS_GW] for q in w.q], c == 0, c == KD - 1)
                        last.then_inc(q_ready.sem, 1)
                    k, s, g = unit(t, L_SCORE)
                    if alive(k):
                        pe.wait_ge(s_tables, 1)
                        pe.wait_ge(turn_kept.sem, turn_kept.at(i, CROSS_TURNS * s + g + 3))
                        pe.wait_ge(shifted.sem, shifted.at(i, k))
                        nc.tensor.matmul(ps[:, SC, :], ident[:, :], mask[:, :, :].rearrange("p a b -> p (a b)"), start=True, stop=False, skip_group_check=True)
                        for b in range(2):
                            for r in range(2):
                                c = b * 2 + r
                                last = nc.tensor.matmul(ps[:, SC, c * CROSS_KEYS:(c + 1) * CROSS_KEYS], qT[:, k % 2, b, r * P:(r + 1) * P],
                                                        kT[:, s % 2, g, b, :], start=False, stop=True, skip_group_check=True)
                        last.then_inc(scored.sem, 1)
                    k, s, g = unit(t, L_MIX)
                    if alive(k):
                        pe.wait_ge(pT_kept.sem, pT_kept.at(i, k + 1))
                        pe.wait_ge(o_lo.sem, o_lo.at(i, k))
                        for b in range(2):
                            last = nc.tensor.matmul(ps[:, O, b * CROSS_REP * S:(b + 1) * CROSS_REP * S], v[:, s % SUBS, b, g * CROSS_HD:(g + 1) * CROSS_HD],
                                                    pT[:, k % 2, b, :], start=True, stop=True)
                        last.then_inc(mixed.sem, 1)
                    k, s, g = unit(t, L_PTURN)
                    if alive(k):
                        pe.wait_ge(probs.sem, probs.at(i, k + 1))
                        pe.wait_ge(pT_kept.sem, pT_kept.at(i, k))
                        for c in range(4):
                            last = nc.tensor.transpose(ps[:, PT, c * P:(c + 1) * P], prob[:, k % 2, c, :], core.ident[:, :])
                        last.then_inc(p_turned.sem, 1)
                    k, s, g = unit(t, L_FLIP)
                    if alive(k):
                        for u in turns_at(g)[0:1]:
                            n = CROSS_TURNS * s + u
                            pe.wait_ge(scaled.sem, scaled.at(i, n + 1))
                            pe.wait_ge(turn_kept.sem, turn_kept.at(i, n))
                            for r in range(CROSS_REP):
                                last = nc.tensor.transpose(ps[:, TQ, r * P:(r + 1) * P], ropeA[:, n % 4, r * CROSS_HD:(r + 1) * CROSS_HD], core.ident[:, :])
                            last.then_inc(turned.sem, 1)
                    k, s, g = unit(t, L_OUT)
                    if alive(k):
                        pe.wait_ge(o_lo.sem, o_lo.at(i, k + 1))
                        if g == 0:
                            pe.wait_ge(added.sem, added.at(i, s))
                        for r in range(CROSS_REP):
                            last = product(nc, ps[:, ACC, 0:D], [q[:, k % 2, r, :] for q in oT], [q[:, g * CROSS_REP + r, :] for q in w.out],
                                           g == 0 and r == 0, g == CROSS_KVH - 1 and r == CROSS_REP - 1)
                        last.then_inc(projected.sem, 1)
                    k, s, g = unit(t, L_FLIP)
                    if alive(k):
                        for u in turns_at(g)[1:2]:
                            n = CROSS_TURNS * s + u
                            pe.wait_ge(scaled.sem, scaled.at(i, n + 1))
                            pe.wait_ge(turn_kept.sem, turn_kept.at(i, n))
                            for r in range(CROSS_REP):
                                last = nc.tensor.transpose(ps[:, TQ, r * P:(r + 1) * P], ropeA[:, n % 4, r * CROSS_HD:(r + 1) * CROSS_HD], core.ident[:, :])
                            last.then_inc(turned.sem, 1)

            steps(pe, body)

        @block.scalar
        def _(act):
            credit(act, x_hi, kv_kept, q_kept, squared, turn_kept, exped, pT_kept, o_hi)


            def body(i, alive):
                for t in range(CROSS_UNITS):
                    k, s, g = unit(t, L_TURN)
                    if alive(k) and g == 0:
                        act.wait_ge(xn_turned.sem, xn_turned.at(i, s + 1))
                        act.wait_ge(q_ready.sem, q_ready.at(i, CROSS_KVH * (s - 1)))
                        nc.scalar.activation(xT[0][:, s % 2], ps[:, LNB, 0:D].rearrange("p (c q) -> p c q", c=KD), ACT.Copy).then_inc(x_hi.sem, 1)
                    k, s, g = unit(t, L_PROJ)
                    if alive(k):
                        act.wait_ge(kv_ready.sem, kv_ready.at(i, k + 1))
                        if g < 2:
                            n = CROSS_TURNS * s + 2 * g
                            act.wait_ge(roped.sem, roped.at(i, CROSS_TURNS * (s - 1) + g + 1))
                            nc.scalar.activation(ks[:, g, :], ps[:, KVP, :], ACT.Copy)
                            act.wait_ge(summed.sem, summed.at(i, n - 1))
                            nc.scalar.activation(square[:, n % 2, :], ps[:, KVP, :], ACT.Square, scale=CROSS_SCALE).then_inc(squared.sem, 1)
                            act.wait_ge(squared.sem, squared.at(i, n + 1))
                            act.sem_inc(kv_kept.sem, 1)
                        else:
                            half = g - 2
                            act.wait_ge(mixed.sem, mixed.at(i, CROSS_KVH * (s - 3)))
                            nc.scalar.activation(v[half * S:(half + 1) * S, s % SUBS, 0, :], ps[0:S, KVP, :], ACT.Copy)
                            nc.scalar.activation(v[half * S:(half + 1) * S, s % SUBS, 1, :], ps[S:P, KVP, :], ACT.Copy).then_inc(kv_kept.sem, 1)
                        act.wait_ge(q_ready.sem, q_ready.at(i, k + 1))
                        n = CROSS_TURNS * s + min(g + 1, 2) + g
                        act.wait_ge(roped.sem, roped.at(i, CROSS_TURNS * (s - 2) + g + 3))
                        nc.scalar.activation(qs[:, s % 2, g, :], ps[:, QP, :], ACT.Copy).then_inc(q_kept.sem, 1)
                        act.wait_ge(summed.sem, summed.at(i, n - 1))
                        nc.scalar.activation(square[:, n % 2, :], ps[:, QP, :], ACT.Square, scale=CROSS_SCALE).then_inc(squared.sem, 1)
                    k, s, g = unit(t, L_SCORE)
                    if alive(k):
                        act.wait_ge(shifted.sem, shifted.at(i, k + 1))
                        act.wait_ge(probs.sem, probs.at(i, k - 1))
                        nc.scalar.activation(e[:, k % 2], shift[:, k % 2], ACT.Exp, scale=CROSS_SCALE).then_inc(exped.sem, 1)
                    k, s, g = unit(t, L_MIX)
                    if alive(k):
                        act.wait_ge(mixed.sem, mixed.at(i, k + 1))
                        act.wait_ge(projected.sem, projected.at(i, k - 1))
                        nc.scalar.activation(oT[0][:, k % 2].rearrange("p r (b q) -> p b r q", b=2),
                                             ps[:, O, :].rearrange("p (b r q) -> p b r q", b=2, r=CROSS_REP), ACT.Copy).then_inc(o_hi.sem, 1)
                    k, s, g = unit(t, L_PTURN)
                    if alive(k):
                        act.wait_ge(p_turned.sem, p_turned.at(i, k + 1))
                        act.wait_ge(mixed.sem, mixed.at(i, k - 1))
                        nc.scalar.activation(pT[:, k % 2], ps[:, PT, :].rearrange("p (b n) -> p b n", b=2), ACT.Copy).then_inc(pT_kept.sem, 1)
                    k, s, g = unit(t, L_FLIP)
                    if alive(k):
                        for u in turns_at(g):
                            n = CROSS_TURNS * s + u
                            act.wait_ge(turned.sem, turned.at(i, n + 1))
                            if u < 2:
                                act.wait_ge(scored.sem, scored.at(i, CROSS_KVH * (s - 1)))
                                nc.scalar.activation(kT[:, s % 2, :, :, u * S:(u + 1) * S],
                                                     ps[:, TQ, :].rearrange("p (g b m) -> p g b m", g=CROSS_KVH, b=2), ACT.Copy).then_inc(turn_kept.sem, 1)
                            else:
                                kq = CROSS_KVH * s + u - 2
                                act.wait_ge(scored.sem, scored.at(i, kq - 1))
                                nc.scalar.activation(qT[:, kq % 2].rearrange("p b (r q) -> p r b q", r=CROSS_REP),
                                                     ps[:, TQ, :].rearrange("p (r b q) -> p r b q", r=CROSS_REP, b=2), ACT.Copy).then_inc(turn_kept.sem, 1)

            steps(act, body)

        @block.vector
        def _(dve):
            settle(core, dve, "x")
            credit(dve, xn, x_lo, summed, rooted, roped, maxed, shifted, totalled, inverse, o_lo, added)

            half = CROSS_HD // 2

            def make_tables():
                dve.wait_ge(s_const, 80)
                for n in range(2):
                    nc.vector.tensor_tensor(table[:, n, 0, :], raw[:, 0, :], raw[:, 2 + n, :], ALU.mult)
                    for a, b in ((0, half), (half, 0)):
                        nc.vector.tensor_tensor(table[:, n, 1, a:a + half], raw[:, 1, a:a + half], raw[:, 2 + n, b:b + half], ALU.mult)
                nc.vector.tensor_copy(ident[:, :], core.ident[:, :])
                nc.vector.tensor_copy(mask[:, :, :], maskf[:, :].unsqueeze(1).broadcast_to([P, 4, CROSS_KEYS]))
                dve.drain().then_inc(s_tables, 1)
                dve.wait_ge(s_tables, 1)

            def body(i, alive):
                for t in range(CROSS_UNITS):
                    k, s, g = unit(t, 0)
                    if alive(k) and g == 0:
                        dve.wait_ge(xn_turned.sem, xn_turned.at(i, s - 1))
                        normalise(core, dve, xnorm[:, s % 2, :], i * SUBS + s).then_inc(xn.sem, 1)
                    if alive(t) and not alive(-1) and t == 1:
                        make_tables()
                    k, s, g = unit(t, L_ROPE)
                    if alive(k):
                        for u in turns_at(g):
                            n = CROSS_TURNS * s + u
                            src = ks[:, u, :] if u < 2 else qs[:, s % 2, u - 2, :]
                            tab = table[:, 1 if u < 2 else 0]
                            dve.wait_ge(turned.sem, turned.at(i, n - 3))
                            dve.wait_ge(joined.sem, joined.at(i, n - 1))
                            a4, b4, s4 = (q.rearrange("p (r d) -> p r d", d=CROSS_HD) for q in (ropeA[:, n % 4, :], ropeB[:, n % 2, :], src))
                            if u == 0:
                                last = nc.vector.tensor_tensor(a4, s4, raw[:, 3, :].unsqueeze(1).broadcast_to([P, CROSS_REP, CROSS_HD]), ALU.mult)
                            else:
                                nc.vector.tensor_tensor(a4, s4, tab[:, 0, :].unsqueeze(1).broadcast_to([P, CROSS_REP, CROSS_HD]), ALU.mult)
                                for a, b in ((0, half), (half, 0)):
                                    last = nc.vector.tensor_tensor(b4[:, :, a:a + half], s4[:, :, b:b + half],
                                                                   tab[:, 1, a:a + half].unsqueeze(1).broadcast_to([P, CROSS_REP, half]), ALU.mult)
                            last.then_inc(roped.sem, 1)
                    k, s, g = unit(t, L_SCORE)
                    if alive(k):
                        sc = ps[:, SC, :].rearrange("p (c m) -> p c m", c=4)
                        dve.wait_ge(scored.sem, scored.at(i, k + 1))
                        nc.vector.tensor_reduce(top[:, k % 2, :], sc, AX.X, ALU.max).then_inc(maxed.sem, 1)
                        dve.wait_ge(maxed.sem, maxed.at(i, k + 1))
                        dve.wait_ge(probs.sem, probs.at(i, k - 1))
                        nc.vector.tensor_tensor(shift[:, k % 2], sc, spread(top[:, k % 2, :], CROSS_KEYS), ALU.subtract).then_inc(shifted.sem, 1)
                    k, s, g = unit(t, 1)
                    if alive(k) and g == 0:
                        dve.wait_ge(x_hi.sem, x_hi.at(i, s + 1))
                        nc.vector.tensor_tensor(xT[1][:, s % 2], ps[:, LNB, 0:D].rearrange("p (c q) -> p c q", c=KD),
                                                xT[0][:, s % 2], ALU.subtract).then_inc(x_lo.sem, 1)
                    k, s, g = unit(t, L_PROJ)
                    if alive(k):
                        for n, row in {0: [(0, 0), (1, 2)], 1: [(2, 1), (3, 3)], 2: [(4, 4)], 3: [(5, 5)]}[g]:
                            dve.wait_ge(squared.sem, squared.at(i, CROSS_TURNS * s + n + 1))
                            if n == 0:
                                dve.wait_ge(rooted.sem, rooted.at(i, RSQRT_STEPS * (s - 1)))
                            nc.vector.tensor_reduce(sums[:, s % 2, row * CROSS_KVH:(row + 1) * CROSS_KVH],
                                                    square[:, n % 2, :].rearrange("p (r d) -> p r d", d=CROSS_HD), AX.X, ALU.add).then_inc(summed.sem, 1)
                        if g == CROSS_KVH - 1:
                            dve.wait_ge(summed.sem, summed.at(i, CROSS_TURNS * (s + 1)))
                            dve.wait_ge(scaled.sem, scaled.at(i, CROSS_TURNS * (s - 1)))
                            rsqrt(core, dve, rooted, i, RSQRT_STEPS * s, sums[:, s % 2, :], CROSS_RMS_EPS, rms[:, s % 2, :], root)
                    k, s, g = unit(t, L_MIX)
                    if alive(k):
                        dve.wait_ge(o_hi.sem, o_hi.at(i, k + 1))
                        nc.vector.tensor_tensor(oT[1][:, k % 2].rearrange("p r (b q) -> p b r q", b=2),
                                                ps[:, O, :].rearrange("p (b r q) -> p b r q", b=2, r=CROSS_REP),
                                                oT[0][:, k % 2].rearrange("p r (b q) -> p b r q", b=2), ALU.subtract).then_inc(o_lo.sem, 1)
                    k, s, g = unit(t, L_SCORE)
                    if alive(k):
                        dve.wait_ge(exped.sem, exped.at(i, k + 1))
                        dve.wait_ge(probs.sem, probs.at(i, k - 1))
                        nc.vector.tensor_reduce(total[:, k % 2, :], e[:, k % 2], AX.X, ALU.add).then_inc(totalled.sem, 1)
                        dve.wait_ge(totalled.sem, totalled.at(i, k + 1))
                        nc.vector.reciprocal(inv[:, k % 2, :], total[:, k % 2, :]).then_inc(inverse.sem, 1)
                    k, s, g = unit(t, L_OUT)
                    if alive(k) and g == CROSS_KVH - 1:
                        dve.wait_ge(projected.sem, projected.at(i, k + 1))
                        tile = core.x[:, i * SUBS + s, :]
                        nc.vector.tensor_tensor(tile, ps[:, ACC, 0:D], tile, ALU.add).then_inc(added.sem, 1)
                        dve.wait_ge(added.sem, added.at(i, s + 1))
                        measure(core, dve, i * SUBS + s)

            steps(dve, body)

        @block.gpsimd
        def _(pool):
            credit(pool, c_hi, c_lo, joined, scaled, probs)
            ctx = core.ins["ctxT"].rearrange("(k p) n -> p k n", p=P)

            def load_context(tile):
                pool.dma_start(cRaw[:, tile % 2], ctx[:, :, tile * P:(tile + 1) * P]).then_inc(s_ctx[tile % 2], 16)

            load_context(0)
            load_context(1)
            for i in range(STEPS + 1):
                alive = (lambda k: k >= 0) if i == 0 else (lambda k: k < 0) if i == STEPS else (lambda k: True)
                for t in range(CROSS_UNITS):
                    k, s, g = unit(t, L_ROPE)
                    if alive(k):
                        if g == 0:
                            pool.wait_ge(rooted.sem, rooted.at(i, RSQRT_STEPS * (s + 1)))
                        for u in turns_at(g):
                            n = CROSS_TURNS * s + u
                            pool.wait_ge(roped.sem, roped.at(i, n + 1))
                            a = ropeA[:, n % 4, :]
                            if u > 0:
                                nc.gpsimd.tensor_tensor(a, a, ropeB[:, n % 2, :], ALU.add).then_inc(joined.sem, 1)
                                pool.wait_ge(joined.sem, joined.at(i, n + 1))
                            else:
                                pool.sem_inc(joined.sem, 1)
                            a4 = a.rearrange("p (r d) -> p r d", d=CROSS_HD)
                            nc.gpsimd.tensor_tensor(a4, a4, spread(rms[:, s % 2, u * CROSS_KVH:(u + 1) * CROSS_KVH], CROSS_HD), ALU.mult).then_inc(scaled.sem, 1)
                    k, s, g = unit(t, L_PROB)
                    if alive(k):
                        pool.wait_ge(inverse.sem, inverse.at(i, k + 1))
                        pool.wait_ge(p_turned.sem, p_turned.at(i, k - 1))
                        nc.gpsimd.tensor_tensor(prob[:, k % 2], e[:, k % 2], spread(inv[:, k % 2, :], CROSS_KEYS), ALU.mult).then_inc(probs.sem, 1)
                    k, s, g = unit(t, 0)
                    if alive(k) and g == 0:
                        tile = i * SUBS + s
                        src = cRaw[:, s % 2]
                        pool.wait_ge(s_ctx[s % 2], 16 * (tile // 2 + 1))
                        pool.wait_ge(kv_ready.sem, kv_ready.at(i, CROSS_KVH * (s - 1)))
                        pool.sem_inc(core.passed, 1)
                        nc.gpsimd.tensor_copy(cT[0][:, s % 2], src).then_inc(c_hi.sem, 1)
                        pool.wait_ge(c_hi.sem, c_hi.at(i, s + 1))
                        nc.gpsimd.tensor_tensor(cT[1][:, s % 2], src, cT[0][:, s % 2], ALU.subtract).then_inc(c_lo.sem, 1)
                        if tile + 2 < TILES:
                            pool.wait_ge(c_lo.sem, c_lo.at(i, s + 1))
                            load_context(tile + 2)
                    if i < STEPS:
                        a, b = (len(jobs) * (i * CROSS_UNITS + t + c) // (STEPS * CROSS_UNITS) for c in (0, 1))
                        split_weights(core, pool, jobs[a:b], first + a, core.own)



FFN_FF = 1024
FFN_FFT = FFN_FF // P
FFN_HALF = 512
FFN_QUARTER = FFN_FF // 4


class FfnWeights:
    def __init__(self, region):
        self.gate = [region.take([P, KD, FFN_FF], F16) for p in range(2)]
        self.up = [region.take([P, KD, FFN_FF], F16) for p in range(2)]
        self.down = [region.take([P, FFN_FFT, D], F16) for p in range(2)]

    def jobs(self, core):
        out = []
        for name, w in (("L0_ffn_w_gate", self.gate), ("L0_ffn_w_up", self.up)):
            for k in range(KD):
                out += chunks(core.ins[name][k * P:(k + 1) * P, :], [q[:, k, :] for q in w])
        for t in range(FFN_FFT):
            out += chunks(core.ins["L0_ffn_w_down"][t * P:(t + 1) * P, :], [q[:, t, :] for q in self.down])
        return out


def ffn_stage(core, w, jobs=(), first=0):
    nc, ps = core.nc, core.ps
    G, U, T, O, LN = (0, 1), (2, 3), (4, 5), 6, 7
    region = Region(core, AT_FFN)
    sb = lambda shape, dt=F32: region.take(shape, dt)
    tally = lambda name, per: Tally(core, "ffn_" + name, per)
    normed, x_turned = tally("normed", SUBS), tally("x_turned", SUBS)
    x_hi, x_lo = tally("x_hi", SUBS), tally("x_lo", SUBS)
    gate_ready, up_ready = tally("gate", 2 * SUBS), tally("up", 2 * SUBS)
    silu_ready = tally("silu", 2 * SUBS)
    h_ready = tally("h", 2 * SUBS)
    mag_ready = tally("mag", SUBS)
    step = tally("step", 11 * SUBS)
    kept_ready = tally("kept", 4 * SUBS)
    hT_ready = tally("hT", 2 * SUBS)
    hT_hi, hT_lo = tally("hT_hi", 2 * SUBS), tally("hT_lo", 2 * SUBS)
    out_ready, added = tally("out", SUBS), tally("added", SUBS)
    xnorm = sb([P, 2, D])
    xT = [sb([P, 2, KD, P], F16) for p in range(2)]
    silu = sb([P, 2, FFN_HALF])
    h = sb([P, 2, FFN_FF])
    mag = sb([P, FFN_FF])
    beats = sb([P, 3, 2, FFN_QUARTER], F16)
    wins = sb([P, 2, 2, FFN_QUARTER], F16)
    votes = sb([P, 4, FFN_QUARTER], F16)
    kept = sb([P, 2, FFN_FF])
    hT = [sb([P, FFN_FFT, P], F16) for p in range(2)]

    with nc.Block() as block:
        @block.sync
        def _(sp):
            stage_weights(core, sp, jobs, first)

        @block.gpsimd
        def _(pool):
            split_weights(core, pool, jobs, first, core.own)

        @block.vector
        def _(dve):
            settle(core, dve, "ffn")
            credit(dve, normed, x_lo, h_ready, step, kept_ready, hT_lo, added)

            def choose_first(i, s):
                dve.wait_ge(mag_ready.sem, mag_ready.at(i, s + 1))
                m4 = mag.rearrange("p (g f) -> p f g", f=4)
                nc.vector.tensor_tensor(beats[:, 0], m4[:, 0:4:2], m4[:, 1:4:2], ALU.is_ge).then_inc(step.sem, 1)
                nc.vector.tensor_tensor(beats[:, 1], m4[:, 0:2], m4[:, 2:4], ALU.is_ge).then_inc(step.sem, 1)
                nc.vector.tensor_tensor(beats[:, 2, 0], m4[:, 0], m4[:, 3], ALU.is_ge).then_inc(step.sem, 1)
                nc.vector.tensor_tensor(beats[:, 2, 1], m4[:, 1], m4[:, 2], ALU.is_ge).then_inc(step.sem, 1)

            def choose_last(i, s):
                k = s * 11
                hv = h[:, s % 2, :]
                b0, b1, b2 = (beats[:, c] for c in range(3))
                w0, w1 = (wins[:, c] for c in range(2))
                dve.wait_ge(step.sem, step.at(i, k + 4))
                nc.vector.tensor_tensor(w0, b1, b2, ALU.add).then_inc(step.sem, 1)
                nc.vector.tensor_tensor(w1[:, 0], b1[:, 0], b2[:, 1], ALU.add).then_inc(step.sem, 1)
                nc.vector.tensor_tensor(w1[:, 1], b1[:, 1], b2[:, 0], ALU.add).then_inc(step.sem, 1)
                dve.wait_ge(step.sem, step.at(i, k + 7))
                nc.vector.tensor_tensor(votes[:, 0], b0[:, 0], w0[:, 0], ALU.add).then_inc(step.sem, 1)
                nc.vector.tensor_tensor(votes[:, 1], w0[:, 1], b0[:, 0], ALU.subtract).then_inc(step.sem, 1)
                nc.vector.tensor_tensor(votes[:, 2], b0[:, 1], w1[:, 0], ALU.subtract).then_inc(step.sem, 1)
                nc.vector.tensor_tensor(votes[:, 3], b0[:, 1], w1[:, 1], ALU.add).then_inc(step.sem, 1)
                dve.wait_ge(step.sem, step.at(i, k + 11))
                h4 = hv.rearrange("p (g f) -> p g f", f=4)
                kv = kept[:, s % 2, :].rearrange("p (g f) -> p g f", f=4)
                dve.wait_ge(hT_ready.sem, hT_ready.at(i, 2 * s - 2))
                for f, (least, op) in enumerate(((2.0, ALU.is_ge), (1.0, ALU.is_ge), (0.0, ALU.is_ge), (1.0, ALU.is_le))):
                    nc.vector.scalar_tensor_tensor(out=kv[:, :, f], in0=votes[:, f], scalar=least, in1=h4[:, :, f], op0=op,
                                                   op1=ALU.mult).then_inc(kept_ready.sem, 1)

            def gated(i, s, a):
                dve.wait_ge(silu_ready.sem, silu_ready.at(i, 2 * s + a + 1))
                dve.wait_ge(up_ready.sem, up_ready.at(i, 2 * s + a + 1))
                dve.wait_ge(kept_ready.sem, kept_ready.at(i, 4 * (s - 1)))
                nc.vector.tensor_tensor(h[:, s % 2, a * FFN_HALF:(a + 1) * FFN_HALF], ps[:, U[a], :], silu[:, a, :],
                                        ALU.mult).then_inc(h_ready.sem, 1)

            def body(i, alive):
                for t in range(SUBS):
                    if alive(t - 1):
                        gated(i, t - 1, 0)
                    if alive(t):
                        dve.wait_ge(x_turned.sem, x_turned.at(i, t - 1))
                        normalise(core, dve, xnorm[:, t % 2, :], i * SUBS + t).then_inc(normed.sem, 1)
                    if alive(t - 2):
                        choose_first(i, t - 2)
                    if alive(t):
                        dve.wait_ge(x_hi.sem, x_hi.at(i, t + 1))
                        nc.vector.tensor_tensor(xT[1][:, t % 2], ps[:, LN, 0:D].rearrange("p (k q) -> p k q", q=P), xT[0][:, t % 2],
                                                ALU.subtract).then_inc(x_lo.sem, 1)
                    if alive(t - 3):
                        s = t - 3
                        for a in range(2):
                            dve.wait_ge(hT_hi.sem, hT_hi.at(i, 2 * s + a + 1))
                            nc.vector.tensor_tensor(hT[1][:, 4 * a:4 * a + 4, :], ps[:, T[a], :].rearrange("p (t q) -> p t q", q=P),
                                                    hT[0][:, 4 * a:4 * a + 4, :], ALU.subtract).then_inc(hT_lo.sem, 1)
                    if alive(t - 1):
                        gated(i, t - 1, 1)
                    if alive(t - 2):
                        choose_last(i, t - 2)
                    if alive(t - 3):
                        s = t - 3
                        tile = core.x[:, i * SUBS + s, :]
                        dve.wait_ge(out_ready.sem, out_ready.at(i, s + 1))
                        nc.vector.tensor_tensor(tile, ps[:, O, 0:D], tile, ALU.add).then_inc(added.sem, 1)
                        dve.wait_ge(added.sem, added.at(i, s + 1))
                        measure(core, dve, i * SUBS + s)

            steps(dve, body)

        @block.tensor
        def _(pe):
            credit(pe, x_turned, gate_ready, up_ready, hT_ready, out_ready)

            def project(i, s, a):
                for bank, ww, ready in ((G[a], w.gate, gate_ready), (U[a], w.up, up_ready)):
                    for k in range(KD):
                        last = product(nc, ps[:, bank, :], [q[:, s % 2, k, :] for q in xT],
                                       [q[:, k, a * FFN_HALF:(a + 1) * FFN_HALF] for q in ww], k == 0, k == KD - 1)
                    last.then_inc(ready.sem, 1)

            def body(i, alive):
                for t in range(SUBS):
                    if alive(t - 1):
                        pe.wait_ge(x_lo.sem, x_lo.at(i, t))
                        pe.wait_ge(h_ready.sem, h_ready.at(i, 2 * (t - 2) + 1))
                        project(i, t - 1, 0)
                    if alive(t - 3):
                        s = t - 3
                        pe.wait_ge(kept_ready.sem, kept_ready.at(i, 4 * s + 4))
                        for a in range(2):
                            pe.wait_ge(hT_lo.sem, hT_lo.at(i, 2 * (s - 1) + a + 1))
                            for q in range(4 * a, 4 * a + 4):
                                last = nc.tensor.transpose(ps[:, T[a], (q % 4) * P:(q % 4 + 1) * P], kept[:, s % 2, q * P:(q + 1) * P],
                                                           core.ident[:, :])
                            last.then_inc(hT_ready.sem, 1)
                    if alive(t):
                        pe.wait_ge(normed.sem, normed.at(i, t + 1))
                        pe.wait_ge(x_lo.sem, x_lo.at(i, t))
                        for k in range(KD):
                            last = nc.tensor.transpose(ps[:, LN, k * P:(k + 1) * P], xnorm[:, t % 2, k * P:(k + 1) * P], core.ident)
                        last.then_inc(x_turned.sem, 1)
                    if alive(t - 1):
                        pe.wait_ge(h_ready.sem, h_ready.at(i, 2 * (t - 2) + 2))
                        project(i, t - 1, 1)
                    if alive(t - 3):
                        s = t - 3
                        pe.wait_ge(added.sem, added.at(i, s))
                        for q in range(FFN_FFT):
                            if q % 4 == 0:
                                pe.wait_ge(hT_lo.sem, hT_lo.at(i, 2 * s + q // 4 + 1))
                            last = product(nc, ps[:, O, 0:D], [z[:, q, :] for z in hT], [z[:, q, :] for z in w.down], q == 0, q == FFN_FFT - 1)
                        last.then_inc(out_ready.sem, 1)

            steps(pe, body)

        @block.scalar
        def _(act):
            credit(act, x_hi, silu_ready, mag_ready, hT_hi)

            def gate(i, s, a):
                act.wait_ge(gate_ready.sem, gate_ready.at(i, 2 * s + a + 1))
                act.wait_ge(h_ready.sem, h_ready.at(i, 2 * (s - 1) + a + 1))
                nc.scalar.activation(silu[:, a, :], ps[:, G[a], :], ACT.Silu).then_inc(silu_ready.sem, 1)

            def body(i, alive):
                for t in range(SUBS):
                    if alive(t - 1):
                        gate(i, t - 1, 0)
                    if alive(t - 3):
                        s = t - 3
                        act.wait_ge(out_ready.sem, out_ready.at(i, s))
                        for a in range(2):
                            act.wait_ge(hT_ready.sem, hT_ready.at(i, 2 * s + a + 1))
                            nc.scalar.activation(hT[0][:, 4 * a:4 * a + 4, :], ps[:, T[a], :].rearrange("p (t q) -> p t q", q=P),
                                                 ACT.Copy).then_inc(hT_hi.sem, 1)
                    if alive(t):
                        act.wait_ge(x_turned.sem, x_turned.at(i, t + 1))
                        act.wait_ge(up_ready.sem, up_ready.at(i, 2 * (t - 1)))
                        nc.scalar.activation(xT[0][:, t % 2], ps[:, LN, 0:D].rearrange("p (k q) -> p k q", q=P), ACT.Copy).then_inc(x_hi.sem, 1)
                    if alive(t - 1):
                        gate(i, t - 1, 1)
                        act.wait_ge(h_ready.sem, h_ready.at(i, 2 * t))
                        act.wait_ge(step.sem, step.at(i, 11 * (t - 2) + 4))
                        nc.scalar.activation(mag, h[:, (t - 1) % 2, :], ACT.Abs).then_inc(mag_ready.sem, 1)

            steps(act, body)



ALIBI_HEADS, ALIBI_KVH, ALIBI_HD = 16, 4, 16
ALIBI_PAIRS = 2
ALIBI_UNITS = SUBS * ALIBI_PAIRS
ALIBI_SCALE = 0.25
ALIBI_KV = ALIBI_KVH * ALIBI_HD


class AlibiWeights:

    def __init__(self, region):
        self.q = [region.take([P, KD, D], F16) for p in range(2)]
        self.k = [region.take([P, KD, 2 * ALIBI_KV], F16) for p in range(2)]
        self.v = [region.take([P, KD, ALIBI_KV], F16) for p in range(2)]
        self.out = [region.take([P, KD, D], F16) for p in range(2)]

    def jobs(self, core):
        out = []
        for name, w in (("L1_attn_Wq", self.q), ("L1_attn_Wk", self.k), ("L1_attn_Wv", self.v), ("L1_attn_Wo", self.out)):
            for k in range(KD):
                out += chunks(core.ins[name][k * P:(k + 1) * P, :], [q[:, k, :] for q in w])
        return out


def alibi_stage(core, w, jobs=(), first=0):
    nc, ps = core.nc, core.ps
    LNB, QB, KB_, VB, SC, PT, O, ACC = range(8)
    tally = lambda name, per: Tally(core, "al_" + name, per)
    normed, x_lo = tally("normed", SUBS), tally("x_lo", SUBS)
    xn_turned, x_hi = tally("xn_turned", SUBS), tally("x_hi", SUBS)
    q_ready, k_ready, v_ready = (tally(c, SUBS) for c in ("q_ready", "k_ready", "v_ready"))
    q_kept, k_kept, v_kept = (tally(c, SUBS) for c in ("q_kept", "k_kept", "v_kept"))
    scored = tally("scored", ALIBI_UNITS)
    biased, maxed, shifted, totalled, inverse = (tally(c, ALIBI_UNITS) for c in ("biased", "maxed", "shifted", "totalled", "inverse"))
    exped, probs = tally("exped", ALIBI_UNITS), tally("probs", ALIBI_UNITS)
    p_turned, pT_kept = tally("p_turned", ALIBI_UNITS), tally("pT_kept", ALIBI_UNITS)
    mixed, o_hi, o_lo = tally("mixed", ALIBI_UNITS), tally("o_hi", ALIBI_UNITS), tally("o_lo", ALIBI_UNITS)
    projected, added = tally("projected", SUBS), tally("added", SUBS)
    s_const, s_zero = core.sem("al_const"), core.sem("al_zero")
    L_TURN, L_PROJ, L_SCORE, L_PROB, L_PTURN, L_MIX, L_OUT = 1, 2, 4, 5, 7, 7, 8
    region = Region(core, AT_FFN)
    sb = lambda name, shape, dt: region.take(shape, dt)
    xT = [sb(f"xT{p}", [P, 2, KD, P], F16) for p in range(2)]
    xnorm = sb("xnorm", [P, 2, D], F32)
    qT = sb("qT", [P, 2, ALIBI_PAIRS, P], F32)
    kT = sb("kT", [P, 2, 2, 8, S], F32)
    v = sb("v", [P, SUBS, 2, 2, 2 * ALIBI_HD], F32)
    bias = sb("bias", [P, ALIBI_KVH, S], F32)
    logits, e, prob = (sb(c, [P, 2, 8, S], F32) for c in ("logits", "e", "prob"))
    top, total, inv = (sb(c, [P, 2, 8], F32) for c in ("top", "total", "inv"))
    pT = sb("pT", [P, 2, 4, P], F32)
    oT = [sb(f"oT{p}", [P, 2, ALIBI_PAIRS, P], F16) for p in range(2)]

    def unit(t, lag):
        k = t - lag
        return k, k // ALIBI_PAIRS, k % ALIBI_PAIRS

    with nc.Block() as block:
        @block.sync
        def _(sp):
            sp.dma_start(bias, core.ins["alibi"]).then_inc(s_const, 16)
            stage_weights(core, sp, jobs, first)

        @block.tensor
        def _(pe):
            credit(pe, xn_turned, q_ready, k_ready, v_ready, scored, p_turned, mixed, projected)

            def body(i, alive):
                for t in range(ALIBI_UNITS):
                    k, s, a = unit(t, L_PTURN)
                    if alive(k):
                        pe.wait_ge(probs.sem, probs.at(i, k + 1))
                        pe.wait_ge(pT_kept.sem, pT_kept.at(i, k))
                        for c in range(4):
                            last = nc.tensor.transpose(ps[:, PT, c * P:(c + 1) * P], prob[:, k % 2, 2 * c:2 * c + 2, :].rearrange("p h k -> p (h k)"), core.ident)
                        last.then_inc(p_turned.sem, 1)
                    k, s, a = unit(t, L_TURN)
                    if alive(k) and a == 0:
                        pe.wait_ge(normed.sem, normed.at(i, s + 1))
                        pe.wait_ge(x_lo.sem, x_lo.at(i, s))
                        for c in range(KD):
                            last = nc.tensor.transpose(ps[:, LNB, c * P:(c + 1) * P], xnorm[:, s % 2, c * P:(c + 1) * P], core.ident)
                        last.then_inc(xn_turned.sem, 1)
                    k, s, a = unit(t, L_PROJ)
                    if alive(k) and a == 0:
                        x = [q[:, s % 2] for q in xT]
                        pe.wait_ge(x_lo.sem, x_lo.at(i, s + 1))
                        pe.wait_ge(q_kept.sem, q_kept.at(i, s))
                        for a in range(ALIBI_PAIRS):
                            for c in range(KD):
                                last = product(nc, ps[:, QB, a * P:(a + 1) * P], [q[:, c, a * P:(a + 1) * P] for q in w.q],
                                               [q[:, c, :] for q in x], c == 0, c == KD - 1)
                        last.then_inc(q_ready.sem, 1)
                        pe.wait_ge(k_kept.sem, k_kept.at(i, s))
                        for c in range(KD):
                            last = product(nc, ps[:, KB_, 0:P], [q[:, c, :] for q in w.k], [q[:, c, :] for q in x], c == 0, c == KD - 1)
                        last.then_inc(k_ready.sem, 1)
                        pe.wait_ge(v_kept.sem, v_kept.at(i, s))
                        for c in range(KD):
                            last = product(nc, ps[:, VB, 0:ALIBI_KV], [q[:, c, :] for q in x], [q[:, c, :] for q in w.v], c == 0, c == KD - 1)
                        last.then_inc(v_ready.sem, 1)
                    k, s, a = unit(t, L_SCORE)
                    if alive(k):
                        pe.wait_ge(k_kept.sem, k_kept.at(i, s + 1))
                        pe.wait_ge(q_kept.sem, q_kept.at(i, s + 1))
                        pe.wait_ge(biased.sem, biased.at(i, k))
                        for b in range(2):
                            last = nc.tensor.matmul(ps[b * S:(b + 1) * S, SC, :], qT[:, s % 2, a, b * S:(b + 1) * S],
                                                    kT[:, s % 2, b].rearrange("p h k -> p (h k)"), start=True, stop=True)
                        last.then_inc(scored.sem, 1)
                    k, s, a = unit(t, L_MIX)
                    if alive(k):
                        pe.wait_ge(pT_kept.sem, pT_kept.at(i, k + 1))
                        pe.wait_ge(v_kept.sem, v_kept.at(i, s + 1))
                        pe.wait_ge(o_lo.sem, o_lo.at(i, k))
                        for b in range(2):
                            for c in range(4):
                                last = nc.tensor.matmul(ps[c * 32:(c + 1) * 32, O, b * S:(b + 1) * S], v[:, s % SUBS, b, c % 2, :],
                                                        pT[:, k % 2, c, b * S:(b + 1) * S], start=True, stop=True,
                                                        tile_position=(0, c * 32))
                        last.then_inc(mixed.sem, 1)
                    k, s, a = unit(t, L_OUT)
                    if alive(k) and a == ALIBI_PAIRS - 1:
                        pe.wait_ge(o_lo.sem, o_lo.at(i, k + 1))
                        pe.wait_ge(added.sem, added.at(i, s))
                        for a in range(ALIBI_PAIRS):
                            last = product(nc, ps[:, ACC, 0:D], [q[:, s % 2, a, :] for q in oT], [q[:, a, :] for q in w.out], a == 0, a == ALIBI_PAIRS - 1)
                        last.then_inc(projected.sem, 1)

            steps(pe, body)

        @block.scalar
        def _(act):
            credit(act, x_hi, q_kept, k_kept, v_kept, exped, pT_kept, o_hi)
            act.wait_ge(s_zero, 2)

            def body(i, alive):
                for t in range(ALIBI_UNITS):
                    k, s, a = unit(t, L_PTURN)
                    if alive(k):
                        act.wait_ge(p_turned.sem, p_turned.at(i, k + 1))
                        act.wait_ge(mixed.sem, mixed.at(i, k - 1))
                        nc.scalar.activation(pT[:, k % 2], ps[:, PT, :].rearrange("p (c q) -> p c q", c=4), ACT.Copy).then_inc(pT_kept.sem, 1)
                    k, s, a = unit(t, L_TURN)
                    if alive(k) and a == 0:
                        act.wait_ge(xn_turned.sem, xn_turned.at(i, s + 1))
                        act.wait_ge(v_ready.sem, v_ready.at(i, s - 1))
                        nc.scalar.activation(xT[0][:, s % 2], ps[:, LNB, 0:D].rearrange("p (c q) -> p c q", c=KD), ACT.Copy).then_inc(x_hi.sem, 1)
                    k, s, a = unit(t, L_PROJ)
                    if alive(k) and a == 0:
                        act.wait_ge(q_ready.sem, q_ready.at(i, s + 1))
                        act.wait_ge(scored.sem, scored.at(i, ALIBI_PAIRS * (s - 1)))
                        nc.scalar.activation(qT[:, s % 2], ps[:, QB, 0:D].rearrange("p (a q) -> p a q", a=ALIBI_PAIRS), ACT.Copy).then_inc(q_kept.sem, 1)
                        act.wait_ge(v_ready.sem, v_ready.at(i, s + 1))
                        act.wait_ge(mixed.sem, mixed.at(i, ALIBI_PAIRS * (s - 3)))
                        for b in range(2):
                            for c in range(2):
                                last = nc.scalar.activation(v[c * S:(c + 1) * S, s % SUBS, b, :, c * ALIBI_HD:(c + 1) * ALIBI_HD],
                                                            ps[b * S:(b + 1) * S, VB, 0:ALIBI_KV].rearrange("p (g c d) -> p g c d", c=2, d=ALIBI_HD)[:, :, c, :], ACT.Copy)
                        last.then_inc(v_kept.sem, 1)
                        act.wait_ge(k_ready.sem, k_ready.at(i, s + 1))
                        for j in range(8):
                            last = nc.scalar.activation(kT[:, s % 2, :, j, :], ps[:, KB_, 0:P].rearrange("p (b k) -> p b k", b=2), ACT.Copy,
                                                        scale=core.headmask[:, j:j + 1])
                        last.then_inc(k_kept.sem, 1)
                    k, s, a = unit(t, L_SCORE)
                    if alive(k):
                        act.wait_ge(shifted.sem, shifted.at(i, k + 1))
                        act.wait_ge(probs.sem, probs.at(i, k - 1))
                        nc.scalar.activation(e[:, k % 2], logits[:, k % 2], ACT.Exp).then_inc(exped.sem, 1)
                    k, s, a = unit(t, L_MIX)
                    if alive(k):
                        act.wait_ge(mixed.sem, mixed.at(i, k + 1))
                        act.wait_ge(projected.sem, projected.at(i, s - 1))
                        nc.scalar.activation(oT[0][:, s % 2, a, :], ps[:, O, 0:P], ACT.Copy).then_inc(o_hi.sem, 1)

            steps(act, body)

        @block.vector
        def _(dve):
            settle(core, dve, "al")
            credit(dve, normed, x_lo, biased, maxed, shifted, totalled, inverse, o_lo, added)
            nc.vector.memset(v, 0.0).then_inc(s_zero, 1)
            dve.wait_ge(s_zero, 1)
            dve.wait_ge(s_const, 16)
            dve.sem_inc(s_zero, 1)

            def body(i, alive):
                for t in range(ALIBI_UNITS):
                    k, s, a = unit(t, 0)
                    if alive(k) and a == 0:
                        dve.wait_ge(xn_turned.sem, xn_turned.at(i, s - 1))
                        normalise(core, dve, xnorm[:, s % 2, :], i * SUBS + s).then_inc(normed.sem, 1)
                    k, s, a = unit(t, L_SCORE)
                    if alive(k):
                        lg = logits[:, k % 2]
                        dve.wait_ge(scored.sem, scored.at(i, k + 1))
                        dve.wait_ge(exped.sem, exped.at(i, k - 1))
                        nc.vector.scalar_tensor_tensor(out=lg.rearrange("p (r g) k -> p r (g k)", r=2), in0=ps[:, SC, :].rearrange("p (r n) -> p r n", r=2),
                                                       scalar=ALIBI_SCALE, in1=bias.rearrange("p g k -> p (g k)").unsqueeze(1).broadcast_to([P, 2, ALIBI_KVH * S]),
                                                       op0=ALU.mult, op1=ALU.add).then_inc(biased.sem, 1)
                        dve.wait_ge(biased.sem, biased.at(i, k + 1))
                        nc.vector.tensor_reduce(top[:, k % 2, :], lg, AX.X, ALU.max).then_inc(maxed.sem, 1)
                        dve.wait_ge(maxed.sem, maxed.at(i, k + 1))
                        nc.vector.tensor_tensor(lg, lg, spread(top[:, k % 2, :], S), ALU.subtract).then_inc(shifted.sem, 1)
                    k, s, a = unit(t, L_TURN)
                    if alive(k) and a == 0:
                        dve.wait_ge(x_hi.sem, x_hi.at(i, s + 1))
                        nc.vector.tensor_tensor(xT[1][:, s % 2], ps[:, LNB, 0:D].rearrange("p (c q) -> p c q", c=KD),
                                                xT[0][:, s % 2], ALU.subtract).then_inc(x_lo.sem, 1)
                    k, s, a = unit(t, L_PROB)
                    if alive(k):
                        dve.wait_ge(exped.sem, exped.at(i, k + 1))
                        dve.wait_ge(probs.sem, probs.at(i, k - 1))
                        nc.vector.tensor_reduce(total[:, k % 2, :], e[:, k % 2], AX.X, ALU.add).then_inc(totalled.sem, 1)
                        dve.wait_ge(totalled.sem, totalled.at(i, k + 1))
                        nc.vector.reciprocal(inv[:, k % 2, :], total[:, k % 2, :]).then_inc(inverse.sem, 1)
                    k, s, a = unit(t, L_MIX)
                    if alive(k):
                        dve.wait_ge(o_hi.sem, o_hi.at(i, k + 1))
                        nc.vector.tensor_tensor(oT[1][:, s % 2, a, :], ps[:, O, 0:P], oT[0][:, s % 2, a, :], ALU.subtract).then_inc(o_lo.sem, 1)
                    k, s, a = unit(t, L_OUT)
                    if alive(k) and a == ALIBI_PAIRS - 1:
                        dve.wait_ge(projected.sem, projected.at(i, s + 1))
                        tile = core.x[:, i * SUBS + s, :]
                        nc.vector.tensor_tensor(tile, ps[:, ACC, 0:D], tile, ALU.add).then_inc(added.sem, 1)
                        dve.wait_ge(added.sem, added.at(i, s + 1))
                        measure(core, dve, i * SUBS + s)

            steps(dve, body)

        @block.gpsimd
        def _(pool):
            credit(pool, probs)
            for i in range(STEPS + 1):
                alive = (lambda k: k >= 0) if i == 0 else (lambda k: k < 0) if i == STEPS else (lambda k: True)
                for t in range(ALIBI_UNITS):
                    k, s, a = unit(t, L_PROB)
                    if alive(k):
                        pool.wait_ge(inverse.sem, inverse.at(i, k + 1))
                        pool.wait_ge(p_turned.sem, p_turned.at(i, k - 1))
                        nc.gpsimd.tensor_tensor(prob[:, k % 2], e[:, k % 2], spread(inv[:, k % 2, :], S), ALU.mult).then_inc(probs.sem, 1)
                    if t % 2 and i < STEPS:
                        a, b = (len(jobs) * (i * ALIBI_UNITS + t + n) // (STEPS * ALIBI_UNITS) for n in (-1, 1))
                        split_weights(core, pool, jobs[a:b], first + a, core.own)



CH_CH = 4
CH_GROUPS, CH_IN_GROUP = 2, 8
CH_QUADS, CH_UNITS_B = 4, 4
CH_GT = CH_IN_GROUP * CH_CH
CH_BT = CH_GROUPS * CH_GT
CH_ROWS = 3 * CH_GT
CH_ONES = CH_ROWS + CH_IN_GROUP
CH_STEP_TILES = 2
CH_BLOCKS = CH_STEP_TILES * 2
CH_SLOTS = CH_BLOCKS * CH_UNITS_B
CH_STEPS5 = TILES // CH_STEP_TILES
CH_K_LAG, CH_A_LAG, CH_T_LAG, CH_V_LAG, CH_O_LAG = 4, 7, 12, 13, 16
CH_APART = 2
CH_FINISH = 4
CH_SCALE = 0.5


def steps5(engine, body):
    body(0, lambda k: k >= 0)
    with engine.Fori(1, CH_STEPS5) as i:
        body(i, lambda k: True)
    body(CH_STEPS5, lambda k: k < 0)


def channel_stage(core, jobs=(), first=0):
    nc, ps = core.nc, core.ps
    A, T, O, M = (0, 1), (2, 4), 6, 7
    tally = lambda name, per: Tally(core, "ch_" + name, per)
    normed = tally("normed", CH_STEP_TILES)
    ctx_in = [tally(f"ctx_in{n}", 32 * CH_BLOCKS // 2) for n in range(2)]
    v_in = [tally(f"v_in{n}", 16 * CH_BLOCKS // 2) for n in range(2)]
    q_in = [tally(f"q_in{n}", 96 * CH_BLOCKS // 2) for n in range(2)]
    k_hi, k_lo, q_hi, q_lo = (tally(c, CH_BLOCKS) for c in ("k_hi", "k_lo", "q_hi", "q_lo"))
    k_apart = tally("k_apart", CH_BLOCKS)
    k_apart2 = tally("k_apart2", CH_BLOCKS)
    k_apart3 = tally("k_apart3", CH_BLOCKS)
    v_set = tally("v_set", CH_BLOCKS)
    scored = tally("scored", CH_BLOCKS * 16)
    maxed = tally("maxed", CH_BLOCKS * 16)
    m_turned, m_set = tally("m_turned", CH_BLOCKS), tally("m_set", CH_BLOCKS)
    scoredT = tally("scoredT", CH_BLOCKS * 8)
    exped = tally("exped", CH_BLOCKS * 8)
    mixed = tally("mixed", CH_SLOTS)
    o_kept = tally("o_kept", CH_BLOCKS)
    o_moved = [tally(f"o_moved{n}", 128 * CH_BLOCKS // 2) for n in range(2)]
    finished = tally("finished", CH_FINISH * CH_STEP_TILES)
    s_const, s_zero, s_ones = core.sem("ch_const"), core.sem("ch_zero"), core.sem("ch_ones")
    region = Region(core, AT_CHANNEL)
    sb = lambda shape, dt=F32: region.take(shape, dt)
    xnorm = sb([P, 2, D])
    kraw, qraw = sb([P, 2, CH_GROUPS, D]), sb([P, 2, CH_GROUPS, D])
    vraw = sb([P, 2, KD, CH_BT])
    kg = sb([P, 2, CH_GROUPS, D], F16)
    ka = sb([P, CH_BLOCKS, CH_GROUPS, CH_IN_GROUP, D], F16)
    qg = sb([P, CH_BLOCKS, CH_GROUPS, D], F16)
    vz = sb([P, 2, KD, CH_QUADS, CH_UNITS_B, 32])
    m = sb([P, 2, CH_GROUPS, KD, CH_IN_GROUP])
    pT = sb([P, 2, 2, 2, KD, D])
    osb = sb([P, 2, D])
    oo, ss = sb([P, D]), sb([P, D])

    def block_of(t, lag):
        k = t - lag
        return k, k // CH_UNITS_B, k % CH_UNITS_B

    with nc.Block() as block:
        @block.sync
        def _(sp):
            credit(sp, *ctx_in, *v_in, *q_in, *o_moved)
            sp.dma_start(core.apart, core.ins["apart"]).then_inc(s_const, 16)
            rows = core.ins["ctx_2048"].rearrange("(n g p) d -> n p g d", g=CH_GROUPS, p=CH_GT)
            cols = core.ins["ctxT"].rearrange("(k p) n -> p k n", p=P)

            def body(i, alive):
                for b in range(CH_BLOCKS):
                    n = i * CH_BLOCKS + b
                    if alive(b):
                        sp.wait_ge(k_lo.sem, k_lo.at(i, b - 1))
                        sp.sem_inc(core.passed, 1)
                        for g in range(CH_GROUPS):
                            sp.dma_start(kraw[0:CH_ROWS, b % 2, g], rows[n, :, g].unsqueeze(0).broadcast_to([3, CH_GT, D])).then_inc(ctx_in[b % 2].sem, 16)
                        sp.wait_ge(q_lo.sem, q_lo.at(i, b - 1))
                        sp.sem_inc(core.passed, 1)
                        sp.wait_ge(normed.sem, normed.at(i, b // 2 + 1))
                        for g in range(CH_GROUPS):
                            r0 = (b % 2 * CH_GROUPS + g) * CH_GT
                            for r in range(3):
                                sp.dma_start(qraw[r * CH_GT:(r + 1) * CH_GT, b % 2, g], xnorm[r0:r0 + CH_GT, b // 2 % 2]).then_inc(q_in[b % 2].sem, 16)
                    k4, b4, _ = block_of(b * CH_UNITS_B, CH_O_LAG)
                    if alive(k4):
                        sp.wait_ge(o_kept.sem, o_kept.at(i, b4 + 1))
                        sp.sem_inc(core.passed, 1)
                        sp.wait_ge(finished.sem, finished.at(i, CH_FINISH * (b4 // 2)))
                        for q in range(CH_QUADS):
                            to = slice(b % 2 * CH_BT + q * 16, b % 2 * CH_BT + (q + 1) * 16)
                            sp.dma_start(oo[to], osb[q * 32:q * 32 + 16, b % 2]).then_inc(o_moved[b % 2].sem, 16)
                            sp.dma_start(ss[to], osb[q * 32 + 16:(q + 1) * 32, b % 2]).then_inc(o_moved[b % 2].sem, 16)
                    if alive(b):
                        sp.wait_ge(v_set.sem, v_set.at(i, b - 1))
                        sp.sem_inc(core.passed, 1)
                        sp.dma_start(vraw[:, b % 2], cols[:, :, bass.ts(n, CH_BT)]).then_inc(v_in[b % 2].sem, 16)

            steps5(sp, body)
            stage_weights(core, sp, jobs, first)

        @block.tensor
        def _(pe):
            credit(pe, scored, m_turned, scoredT, mixed)

            def body(i, alive):
                for t in range(CH_SLOTS):
                    k, b, j = block_of(t, CH_A_LAG)
                    k2, b2, j2 = block_of(t, CH_T_LAG)
                    k3, b3, j3 = block_of(t, CH_V_LAG)
                    for q in range(CH_QUADS):
                        if alive(k):
                            if q == 0 and j == 0:
                                pe.wait_ge(k_apart.sem, k_apart.at(i, b + 1))
                                pe.wait_ge(k_apart2.sem, k_apart2.at(i, b + 1))
                                pe.wait_ge(k_apart3.sem, k_apart3.at(i, b + 1))
                                pe.wait_ge(q_lo.sem, q_lo.at(i, b + 1))
                            n = k * CH_QUADS + q
                            g, hd = q // 2, q % 2 * 4 + j
                            pe.wait_ge(maxed.sem, maxed.at(i, n - 1))
                            for u in range(KD):
                                last = nc.tensor.matmul(ps[:, A[q % 2], u * D:(u + 1) * D], qg[0:CH_ROWS, b % CH_BLOCKS, g, u * P:(u + 1) * P],
                                                        ka[0:CH_ROWS, b % CH_BLOCKS, g, hd, :], start=True, stop=True)
                            last.then_inc(scored.sem, 1)
                        if alive(k2):
                            if q == 0 and j2 == 0:
                                pe.wait_ge(s_ones, CH_BLOCKS * CH_GROUPS)
                                pe.wait_ge(m_set.sem, m_set.at(i, b2 + 1))
                            g, hd = q // 2, q % 2 * 4 + j2
                            if q % 2 == 0:
                                pe.wait_ge(exped.sem, exped.at(i, 2 * k2 + q // 2 - 1))
                            for u in range(KD):
                                last = nc.tensor.matmul(ps[:, T[q // 2] + q % 2, u * D:(u + 1) * D], ka[0:CH_ONES, b2 % CH_BLOCKS, g, hd, u * P:(u + 1) * P],
                                                        qg[0:CH_ONES, b2 % CH_BLOCKS, g, :], start=True, stop=True)
                            if q % 2 == 1:
                                last.then_inc(scoredT.sem, 1)
                        if q == 1 and j == 0 and alive(k - CH_UNITS_B):
                            pe.wait_ge(maxed.sem, maxed.at(i, b * 16))
                            pe.wait_ge(m_set.sem, m_set.at(i, b - 1))
                            for g in range(CH_GROUPS):
                                for u in range(KD):
                                    last = nc.tensor.transpose(ps[0:CH_IN_GROUP, M, (g * KD + u) * P:(g * KD + u + 1) * P], m[:, (b - 1) % 2, g, u, :], core.ident)
                            last.then_inc(m_turned.sem, 1)
                        if alive(k3) and q % 2 == 1:
                            u = q // 2
                            if u == 0:
                                pe.wait_ge(exped.sem, exped.at(i, 2 * k3 + 2))
                                if j3 == 0:
                                    pe.wait_ge(o_kept.sem, o_kept.at(i, b3))
                                    pe.wait_ge(v_set.sem, v_set.at(i, b3 + 1))
                            for c in range(CH_QUADS):
                                last = nc.tensor.matmul(ps[c * 32:(c + 1) * 32, O, 0:D], vz[:, b3 % 2, u, c, j3, :], pT[:, k3 % 2, c // 2, c % 2, u, :],
                                                        start=j3 == 0 and u == 0, stop=j3 == CH_UNITS_B - 1 and u == KD - 1,
                                                        tile_position=(0, c * 32), skip_group_check=True)
                            if u == KD - 1:
                                last.then_inc(mixed.sem, 1)

            steps5(pe, body)

        @block.scalar
        def _(act):
            credit(act, k_apart3, v_set, m_set, exped, o_kept)
            act.wait_ge(s_const, 16)

            def body(i, alive):
                for t in range(CH_SLOTS):
                    if alive(t) and not alive(-1) and 8 <= t < 8 + CH_BLOCKS:
                        for g in range(CH_GROUPS):
                            nc.scalar.activation(ka[CH_ROWS:CH_ONES, t - 8, g], spread(core.apart[CH_ROWS:CH_ONES, :], D), ACT.Copy).then_inc(s_ones, 1)
                    k, b, j = block_of(t, CH_K_LAG)
                    if alive(k) and j in (1, 2):
                        if j == 1:
                            act.wait_ge(k_lo.sem, k_lo.at(i, b + 1))
                            act.wait_ge(scoredT.sem, scoredT.at(i, 8 * (b - 3)))
                        for hd in range(2 * CH_APART + (4 - CH_APART) * (j - 1), 2 * CH_APART + (4 - CH_APART) * j):
                            last = nc.scalar.activation(ka[0:CH_ROWS, b % CH_BLOCKS, 1, hd, :], kg[0:CH_ROWS, b % 2, 1, :], ACT.Copy, scale=core.apart[0:CH_ROWS, hd:hd + 1])
                        if j == 2:
                            last.then_inc(k_apart3.sem, 1)
                    k, b, j = block_of(t, CH_A_LAG + 1)
                    if alive(k) and j == 1:
                        act.wait_ge(s_zero, 1 + 2 * CH_UNITS_B)
                        act.wait_ge(v_in[b % 2].sem, v_in[b % 2].at(i, 16 * (b // 2 + 1)))
                        act.wait_ge(mixed.sem, mixed.at(i, CH_UNITS_B * (b - 1)))
                        src = vraw[:, b % 2].rearrange("p u (q j c) -> p u q j c", q=CH_QUADS, c=CH_CH)
                        for jj in range(CH_UNITS_B):
                            last = nc.scalar.activation(vz[:, b % 2, :, :, jj, CH_CH * jj:CH_CH * (jj + 1)], src[:, :, :, jj, :], ACT.Copy)
                        last.then_inc(v_set.sem, 1)
                    k, b, j = block_of(t, CH_T_LAG)
                    if alive(k):
                        for a in range(2):
                            act.wait_ge(scoredT.sem, scoredT.at(i, 2 * k + a + 1))
                            act.wait_ge(mixed.sem, mixed.at(i, k - 1))
                            nc.scalar.activation(pT[:, k % 2, a], ps[:, T[a]:T[a] + 2, :].rearrange("p h (u t) -> p h u t", u=KD), ACT.Exp,
                                                 scale=CH_SCALE).then_inc(exped.sem, 1)
                    k, b, j = block_of(t, CH_T_LAG - 1)
                    if alive(k) and j == 0:
                        act.wait_ge(m_turned.sem, m_turned.at(i, b + 1))
                        nc.scalar.activation(qg[CH_ROWS:CH_ONES, b % CH_BLOCKS], ps[0:CH_IN_GROUP, M, :].rearrange("p (g t) -> p g t", g=CH_GROUPS),
                                             ACT.Copy, scale=-1.0).then_inc(m_set.sem, 1)
                    k, b, j = block_of(t, CH_O_LAG)
                    if alive(k) and j == 0:
                        act.wait_ge(mixed.sem, mixed.at(i, k + CH_UNITS_B))
                        act.wait_ge(o_moved[b % 2].sem, o_moved[b % 2].at(i, 128 * (b // 2)))
                        nc.scalar.activation(osb[:, b % 2], ps[:, O, 0:D], ACT.Copy).then_inc(o_kept.sem, 1)

            steps5(act, body)

        @block.vector
        def _(dve):
            settle(core, dve, "ch")

            def finish(i, s, q):
                n = CH_FINISH * s
                half = slice(q % 2 * P, (q % 2 + 1) * P)
                tile = core.x[:, i * CH_STEP_TILES + s, :]
                if q < 2:
                    if q == 0:
                        for c in range(2):
                            dve.wait_ge(o_moved[c].sem, o_moved[c].at(i, 128 * (s + 1)))
                    nc.vector.reciprocal(ss[:, half], ss[:, half]).then_inc(finished.sem, 1)
                elif q == 2:
                    dve.wait_ge(finished.sem, finished.at(i, n + 2))
                    nc.vector.tensor_tensor(oo, oo, ss, ALU.mult).then_inc(finished.sem, 1)
                else:
                    dve.wait_ge(finished.sem, finished.at(i, n + 3))
                    nc.vector.tensor_tensor(tile, tile, oo, ALU.add).then_inc(finished.sem, 1)
                    dve.wait_ge(finished.sem, finished.at(i, n + 4))
                    measure(core, dve, i * CH_STEP_TILES + s)

            credit(dve, normed, k_apart2, maxed, finished)
            dve.wait_ge(s_const, 16)

            def set_up():
                nc.vector.memset(vz, 0.0).then_inc(s_zero, 1)
                dve.wait_ge(s_zero, 1)
                for j in range(CH_UNITS_B):
                    for n in range(2):
                        nc.vector.memset(vz[:, n, :, :, j, 16 + CH_CH * j:16 + CH_CH * (j + 1)].rearrange("p u q c -> p (u q) c"), 1.0).then_inc(s_zero, 1)

            def body(i, alive):
                for t in range(CH_SLOTS):
                    if alive(t) and t % 8 == 0:
                        s = t // 8
                        for n in range(2):
                            dve.wait_ge(q_in[n].sem, q_in[n].at(i, 96 * (s - 1)))
                        normalise(core, dve, xnorm[:, s % 2, :], i * CH_STEP_TILES + s).then_inc(normed.sem, 1)
                    if alive(t) and not alive(-1) and t == 1:
                        set_up()
                    k, b, j = block_of(t, CH_K_LAG)
                    if alive(k) and j in (1, 2):
                        if j == 1:
                            dve.wait_ge(k_lo.sem, k_lo.at(i, b + 1))
                            dve.wait_ge(scoredT.sem, scoredT.at(i, 8 * (b - 3)))
                        for hd in range(CH_APART * (j - 1), CH_APART * j):
                            last = nc.vector.tensor_scalar(ka[0:CH_ROWS, b % CH_BLOCKS, 1, hd, :], kg[0:CH_ROWS, b % 2, 1, :], core.apart[0:CH_ROWS, hd:hd + 1], None, ALU.mult)
                        if j == 2:
                            last.then_inc(k_apart2.sem, 1)
                    k, b, j = block_of(t, CH_A_LAG)
                    k4, b4, j4 = block_of(t, CH_O_LAG)
                    for q in range(CH_QUADS):
                        if alive(k):
                            n = k * CH_QUADS + q
                            dve.wait_ge(scored.sem, scored.at(i, n + 1))
                            if j == 0 and q == 0:
                                dve.wait_ge(m_turned.sem, m_turned.at(i, b - 1))
                            nc.vector.tensor_reduce(m[:, b % 2, q // 2, :, q % 2 * 4 + j], ps[:, A[q % 2], :].rearrange("p (u s) -> p u s", u=KD),
                                                    AX.X, ALU.max).then_inc(maxed.sem, 1)
                        if alive(k4) and b4 % 2 == 1 and j4 == 3:
                            finish(i, b4 // 2, q)

            steps5(dve, body)

        @block.gpsimd
        def _(pool):
            credit(pool, k_hi, k_lo, q_hi, q_lo, k_apart)

            def body(i, alive):
                for b0 in range(CH_BLOCKS):
                    k, b, j = block_of(b0 * CH_UNITS_B, CH_K_LAG)
                    if alive(k):
                        lo = slice(CH_GT, 2 * CH_GT)
                        pool.wait_ge(ctx_in[b % 2].sem, ctx_in[b % 2].at(i, 32 * (b // 2 + 1)))
                        pool.wait_ge(k_apart3.sem, k_apart3.at(i, b - 1))
                        pool.wait_ge(k_apart2.sem, k_apart2.at(i, b - 1))
                        pool.wait_ge(q_lo.sem, q_lo.at(i, b))
                        pool.sem_inc(core.passed, 1)
                        nc.gpsimd.tensor_copy(kg[0:CH_ROWS, b % 2], kraw[0:CH_ROWS, b % 2]).then_inc(k_hi.sem, 1)
                        pool.wait_ge(k_hi.sem, k_hi.at(i, b + 1))
                        nc.gpsimd.tensor_tensor(kg[lo, b % 2], kraw[lo, b % 2], kg[lo, b % 2], ALU.subtract).then_inc(k_lo.sem, 1)
                        pool.wait_ge(k_lo.sem, k_lo.at(i, b + 1))
                        pool.wait_ge(scoredT.sem, scoredT.at(i, 8 * (b - 3)))
                        nc.gpsimd.tensor_tensor(ka[0:CH_ROWS, b % CH_BLOCKS, 0], kg[0:CH_ROWS, b % 2, 0, :].unsqueeze(1).broadcast_to([CH_ROWS, CH_IN_GROUP, D]),
                                                spread(core.apart[0:CH_ROWS, :], D), ALU.mult).then_inc(k_apart.sem, 1)
                        pool.wait_ge(q_in[b % 2].sem, q_in[b % 2].at(i, 96 * (b // 2 + 1)))
                        pool.wait_ge(k_apart.sem, k_apart.at(i, b + 1))
                        pool.sem_inc(core.passed, 1)
                        nc.gpsimd.tensor_copy(qg[0:CH_ROWS, b % CH_BLOCKS], qraw[0:CH_ROWS, b % 2]).then_inc(q_hi.sem, 1)
                        pool.wait_ge(q_hi.sem, q_hi.at(i, b + 1))
                        lo = slice(2 * CH_GT, 3 * CH_GT)
                        nc.gpsimd.tensor_tensor(qg[lo, b % CH_BLOCKS], qraw[lo, b % 2], qg[lo, b % CH_BLOCKS], ALU.subtract).then_inc(q_lo.sem, 1)

            pool.wait_ge(s_const, 16)
            steps5(pool, body)
            split_weights(core, pool, jobs, first, core.own)



MOE_EXPERTS, MOE_TOPK, MOE_PRIMARY, MOE_FF = 32, 8, 4, 96
MOE_SECOND = MOE_TOPK - MOE_PRIMARY
MOE_UNITS = MOE_EXPERTS * MOE_FF // P
MOE_THRESHOLD = 0.5
MOE_FRONT = 16


class MoeWeights:
    def __init__(self, region):
        self.up = [region.take([P, KD, MOE_UNITS * 2 * P], F16) for p in range(2)]
        self.down = [region.take([P, MOE_UNITS, D], F16) for p in range(2)]

    def jobs(self, core):
        out = []
        for k in range(KD):
            out += chunks(core.ins["L1_ffn_gate_up_proj"][k * P:(k + 1) * P, :], [q[:, k, :] for q in self.up])
        src = core.ins["L1_ffn_down_proj"].rearrange("f u d -> f (u d)")
        out += chunks(src, [q.rearrange("f u d -> f (u d)") for q in self.down])
        return out


def moe_stage(core, w):
    nc, ps = core.nc, core.ps
    G, U, CW, ACC, R = (0, 1), (2, 3), 4, (5, 6), 7
    tally = lambda name, per: Tally(core, "moe_" + name, per)
    normed = tally("normed", SUBS)
    xn_turned, next_hi, next_lo = tally("xn_turned", KD), tally("next_hi", KD), tally("next_lo", KD)
    routed = tally("routed", 1)
    rexp = tally("rexp", 1)
    route = tally("route", 44)
    sec_turned, sec_kept, similar = tally("sec_turned", 1), tally("sec_kept", 1), tally("similar", 1)
    cw_turned, cw_hi, cw_lo = tally("cw_turned", 1), tally("cw_hi", 1), tally("cw_lo", 1)
    moved = tally("moved", 3)
    gate_ready, up_ready, cw_ready = (tally(c, MOE_UNITS) for c in ("gate_ready", "up_ready", "cw_ready"))
    silu_ready = tally("silu_ready", MOE_UNITS)
    gated, weighed = tally("gated", MOE_UNITS), tally("weighed", MOE_UNITS)
    h_hi, h_lo = tally("h_hi", MOE_UNITS), tally("h_lo", MOE_UNITS)
    down = tally("down", MOE_UNITS)
    added = tally("added", SUBS)
    s_const, s_out, s_setup = core.sem("moe_const"), core.sem("out"), core.sem("moe_setup")
    region = Region(core, AT_MOE)
    sb = lambda shape, dt=F32: region.take(shape, dt)
    xnorm = sb([P, SUBS, D])
    nextT = [sb([P, KD, TOK], F16) for p in range(2)]
    xT = [sb([P, KD, TOK], F16) for p in range(2)]
    router = [sb([P, KD, MOE_EXPERTS], F16) for p in range(2)]
    router_raw = sb([P, KD, MOE_EXPERTS])
    pr = sb([P, SUBS, MOE_EXPERTS])
    s4 = sb([P, SUBS])
    best8 = sb([P, SUBS, MOE_TOPK])
    at8 = sb([P, SUBS, MOE_TOPK], I32)
    at8f = sb([P, SUBS * MOE_TOPK])
    iota = sb([P, MOE_EXPERTS])
    hot = sb([P, SUBS * MOE_TOPK, MOE_EXPERTS])
    picked = sb([P, SUBS * MOE_TOPK, MOE_EXPERTS])
    hotT = sb([P, SUBS, P])
    simdiag = sb([P, P])
    unit_diag = sb([P, P])
    cand = sb([P, SUBS * MOE_SECOND, MOE_PRIMARY])
    prod = sb([P, MOE_SECOND, MOE_PRIMARY * MOE_EXPERTS])
    take = sb([P, SUBS * MOE_SECOND, MOE_PRIMARY])
    best = sb([P, SUBS * MOE_SECOND])
    keep = sb([P, SUBS * MOE_SECOND])
    rest = sb([P, SUBS * MOE_SECOND])
    coef = sb([P, SUBS, MOE_TOPK])
    extra = sb([P, SUBS, MOE_PRIMARY])
    comb = sb([P, SUBS, MOE_EXPERTS])
    cwn = sb([P, TOK], F16)
    cwT = sb([P, TOK], F16)
    select = sb([P, MOE_UNITS, P], F16)
    silu = sb([P, 2, TOK])
    h = sb([P, 2, TOK])
    hT = [sb([P, 2, TOK], F16) for p in range(2)]

    def unit(t, lag):
        return t - lag

    with nc.Block() as block:
        @block.sync
        def _(sp):
            sp.dma_start(router_raw, core.ins["L1_ffn_gate_weight"].rearrange("(k p) e -> p k e", p=P)).then_inc(s_const, 16)
            sp.dma_start(iota, core.ins["iota"]).then_inc(s_const, 16)
            sp.dma_start(select, core.ins["select"]).then_inc(s_const, 16)
            sp.wait_ge(s_setup, 1)
            for m in range(MOE_SECOND):
                r = slice(m * MOE_EXPERTS, (m + 1) * MOE_EXPERTS)
                sp.dma_start(simdiag[r, r], core.ins["L1_ffn_similarity"]).then_inc(s_const, 16)
            out = core.out.rearrange("(t p) d -> p t d", p=P)
            for i in range(STEPS):
                sp.wait_ge(added.sem, added.at(i, SUBS))
                sp.dma_start(out[:, i * SUBS:(i + 1) * SUBS, :], core.x[:, i * SUBS:(i + 1) * SUBS, :]).then_inc(s_out, 16)
            sp.wait_ge(s_out, 16 * STEPS)

        @block.tensor
        def _(pe):
            credit(pe, xn_turned, routed, sec_turned, similar, cw_turned, gate_ready, up_ready, cw_ready, down)
            def body(i, alive):
                for t in range(MOE_UNITS):
                    if alive(t) and t in (1, 2):
                        c = t - 1
                        pe.wait_ge(normed.sem, normed.at(i, SUBS))
                        pe.wait_ge(next_lo.sem, next_lo.at(i, c))
                        pe.wait_ge(cw_lo.sem, cw_lo.at(i, 0))
                        for s in range(SUBS):
                            last = nc.tensor.transpose(ps[:, R, s * P:(s + 1) * P], xnorm[:, s, c * P:(c + 1) * P], core.ident)
                        last.then_inc(xn_turned.sem, 1)
                    if alive(t) and t == 4:
                        pe.wait_ge(s_setup, 6)
                        pe.wait_ge(next_lo.sem, next_lo.at(i, KD))
                        for s in range(SUBS):
                            for c in range(KD):
                                last = product(nc, ps[:, R, s * MOE_EXPERTS:(s + 1) * MOE_EXPERTS], [q[:, c, s * P:(s + 1) * P] for q in nextT],
                                               [q[:, c, :] for q in router], c == 0, c == KD - 1)
                        last.then_inc(routed.sem, 1)
                    if alive(t) and t == 8:
                        pe.wait_ge(route.sem, route.at(i, MOE_R_HOT))
                        for s in range(SUBS):
                            last = nc.tensor.transpose(ps[:, R, s * P:(s + 1) * P], hot[:, s * MOE_TOPK + MOE_PRIMARY:(s + 1) * MOE_TOPK, :].rearrange("p m e -> p (m e)"), core.ident)
                        last.then_inc(sec_turned.sem, 1)
                    if alive(t) and t == 9:
                        pe.wait_ge(sec_kept.sem, sec_kept.at(i, 1))
                        for s in range(SUBS):
                            last = nc.tensor.matmul(ps[:, R, s * P:(s + 1) * P], hotT[:, s, :], simdiag, start=True, stop=True)
                        last.then_inc(similar.sem, 1)
                    if alive(t) and t == 14:
                        pe.wait_ge(route.sem, route.at(i, route.per))
                        for s in range(SUBS):
                            last = nc.tensor.transpose(ps[0:MOE_EXPERTS, R, s * P:(s + 1) * P], comb[:, s, :], core.ident)
                        last.then_inc(cw_turned.sem, 1)
                    e = unit(t, MOE_FRONT)
                    if alive(e):
                        if e % MOE_UNITS == 0:
                            pe.wait_ge(moved.sem, moved.at(i, 3))
                        pe.wait_ge(silu_ready.sem, silu_ready.at(i, e - 1))
                        pe.wait_ge(gated.sem, gated.at(i, e - 1))
                        ee = e % MOE_UNITS
                        for off, bank, ready in ((0, G, gate_ready), (P, U, up_ready)):
                            for c in range(KD):
                                col = ee * 2 * P + off
                                last = product(nc, ps[:, bank[e % 2], :], [q[:, c, col:col + P] for q in w.up], [q[:, c, :] for q in xT],
                                               c == 0, c == KD - 1)
                            last.then_inc(ready.sem, 1)
                        pe.wait_ge(weighed.sem, weighed.at(i, e))
                        nc.tensor.matmul(ps[:, CW, :], select[0:2 * MOE_EXPERTS, ee, :], cwT[0:2 * MOE_EXPERTS, :], start=True, stop=True).then_inc(cw_ready.sem, 1)
                    e = unit(t, MOE_FRONT + 2)
                    if alive(e):
                        ee = e % MOE_UNITS
                        pe.wait_ge(h_lo.sem, h_lo.at(i, e + 1))
                        if ee == 0:
                            pe.wait_ge(added.sem, added.at(i, 0))
                        for s in range(SUBS):
                            last = product(nc, ps[:, ACC[s // 2], s % 2 * D:(s % 2 + 1) * D], [q[:, e % 2, s * P:(s + 1) * P] for q in hT],
                                           [q[:, ee, :] for q in w.down], ee == 0 and s % 2 == 0, ee == MOE_UNITS - 1, group=False)
                        last.then_inc(down.sem, 1)

            steps(pe, body)

        @block.scalar
        def _(act):
            credit(act, next_hi, rexp, sec_kept, cw_hi, silu_ready, h_hi)

            def body(i, alive):
                for t in range(MOE_UNITS):
                    if alive(t) and t in (1, 2):
                        c = t - 1
                        act.wait_ge(xn_turned.sem, xn_turned.at(i, c + 1))
                        act.wait_ge(moved.sem, moved.at(i, 0))
                        nc.scalar.activation(nextT[0][:, c, :], ps[:, R, :], ACT.Copy).then_inc(next_hi.sem, 1)
                    if alive(t) and t == 5:
                        act.wait_ge(route.sem, route.at(i, MOE_R_SHIFT))
                        nc.scalar.activation(pr, pr, ACT.Exp).then_inc(rexp.sem, 1)
                    if alive(t) and t == 8:
                        act.wait_ge(sec_turned.sem, sec_turned.at(i, 1))
                        nc.scalar.activation(hotT, ps[:, R, :].rearrange("p (s q) -> p s q", s=SUBS), ACT.Copy).then_inc(sec_kept.sem, 1)
                    if alive(t) and t == 14:
                        act.wait_ge(cw_turned.sem, cw_turned.at(i, 1))
                        nc.scalar.activation(cwn[0:MOE_EXPERTS, :], ps[0:MOE_EXPERTS, R, :], ACT.Copy).then_inc(cw_hi.sem, 1)
                    e = unit(t, MOE_FRONT + 1)
                    if alive(e):
                        act.wait_ge(weighed.sem, weighed.at(i, e + 1))
                        act.wait_ge(down.sem, down.at(i, e - 1))
                        nc.scalar.activation(hT[0][:, e % 2, :], h[:, e % 2, :], ACT.Copy).then_inc(h_hi.sem, 1)
                    e = unit(t, MOE_FRONT)
                    if alive(e):
                        act.wait_ge(gate_ready.sem, gate_ready.at(i, e + 1))
                        act.wait_ge(gated.sem, gated.at(i, e - 1))
                        nc.scalar.activation(silu[:, e % 2, :], ps[:, G[e % 2], :], ACT.Silu).then_inc(silu_ready.sem, 1)

            steps(act, body)

        @block.vector
        def _(dve):
            settle(core, dve, "moe")
            credit(dve, normed, next_lo, route, cw_lo, moved, gated, weighed, h_lo, added)
            nc.vector.memset(simdiag, 0.0).then_inc(s_setup, 1)

            def set_up():
                dve.wait_ge(s_const, 16 * 7)
                nc.vector.tensor_copy(router[0], router_raw).then_inc(s_setup, 1)
                dve.wait_ge(s_setup, 2)
                nc.vector.tensor_tensor(router[1], router_raw, router[0], ALU.subtract).then_inc(s_setup, 1)
                nc.vector.tensor_scalar(unit_diag, core.ident, -1.0, 1.0, ALU.mult, ALU.add).then_inc(s_setup, 1)
                dve.wait_ge(s_setup, 4)
                nc.vector.tensor_tensor(simdiag, simdiag, unit_diag, ALU.mult).then_inc(s_setup, 1)
                dve.wait_ge(s_setup, 5)
                nc.vector.tensor_tensor(simdiag, simdiag, core.ident, ALU.add).then_inc(s_setup, 1)
                dve.wait_ge(s_setup, 6)

            def router_first(i, step):
                lg = ps[:, R, 0:SUBS * MOE_EXPERTS].rearrange("p (s e) -> p s e", s=SUBS)
                step(nc.vector.tensor_reduce(s4, lg, AX.X, ALU.max))
                step(nc.vector.tensor_tensor(pr, lg, spread(s4, MOE_EXPERTS), ALU.subtract))

            def router_choose(i, step):
                step(nc.vector.tensor_reduce(s4, pr, AX.X, ALU.add))
                step(nc.vector.reciprocal(s4, s4))
                step(nc.vector.tensor_tensor(pr, pr, spread(s4, MOE_EXPERTS), ALU.mult))
                for s in range(SUBS):
                    dve.sem_inc(core.passed, 1)
                    step(nc.vector.max(best8[:, s, :], pr[:, s, :]))
                    dve.sem_inc(core.passed, 1)
                    step(nc.vector.max_index(at8[:, s, :].bitcast(mybir.dt.uint32), best8[:, s, :], pr[:, s, :]))

            def router_hot(i, step):
                step(nc.vector.tensor_copy(at8f, at8.rearrange("p s k -> p (s k)").bitcast(mybir.dt.uint32)))
                step(nc.vector.tensor_tensor(hot, iota.unsqueeze(1).broadcast_to([P, SUBS * MOE_TOPK, MOE_EXPERTS]), spread(at8f, MOE_EXPERTS), ALU.is_equal))

            def router_weights(i, step):
                step(nc.vector.tensor_reduce(s4, best8, AX.X, ALU.add))
                step(nc.vector.tensor_scalar(s4, s4, 1e-12, None, ALU.max))
                step(nc.vector.reciprocal(s4, s4))
                step(nc.vector.tensor_tensor(best8, best8, spread(s4, MOE_TOPK), ALU.mult))

            def router_similar(i, s, step):
                sim = ps[:, R, s * P:(s + 1) * P].rearrange("p (m e) -> p m e", m=MOE_SECOND)
                pv = prod.rearrange("p m (j e) -> p m j e", j=MOE_PRIMARY)
                step(nc.vector.tensor_tensor(pv, sim.unsqueeze(2).broadcast_to([P, MOE_SECOND, MOE_PRIMARY, MOE_EXPERTS]),
                                             hot[:, s * MOE_TOPK:s * MOE_TOPK + MOE_PRIMARY, :].unsqueeze(1).broadcast_to([P, MOE_SECOND, MOE_PRIMARY, MOE_EXPERTS]), ALU.mult))
                step(nc.vector.tensor_reduce(cand[:, s * MOE_SECOND:(s + 1) * MOE_SECOND, :], pv, AX.X, ALU.add))

            def router_combine(i, step):
                step(nc.vector.tensor_reduce(best, cand, AX.X, ALU.max))
                step(nc.vector.tensor_scalar(keep, best, MOE_THRESHOLD, None, ALU.is_lt))
                step(nc.vector.tensor_scalar(rest, keep, -1.0, 1.0, ALU.mult, ALU.add))
                step(nc.vector.tensor_tensor(take, cand, spread(best, MOE_PRIMARY), ALU.is_ge))
                for j in range(MOE_PRIMARY):
                    step(nc.vector.tensor_tensor(take[:, :, j], take[:, :, j], rest, ALU.mult))
                    if j < MOE_PRIMARY - 1:
                        step(nc.vector.tensor_tensor(rest, rest, take[:, :, j], ALU.subtract))

            def router_weigh(i, step):
                second = best8[:, :, MOE_PRIMARY:MOE_TOPK]
                t4 = take.rearrange("p (s m) j -> p s m j", s=SUBS)
                step(nc.vector.tensor_tensor(t4, t4, spread(second, MOE_PRIMARY), ALU.mult))
                step(nc.vector.tensor_reduce(extra, take.rearrange("p (s m) j -> p s j m", s=SUBS), AX.X, ALU.add))
                step(nc.vector.tensor_tensor(coef[:, :, 0:MOE_PRIMARY], best8[:, :, 0:MOE_PRIMARY], extra, ALU.add))
                step(nc.vector.tensor_tensor(coef[:, :, MOE_PRIMARY:MOE_TOPK], second, keep.rearrange("p (s m) -> p s m", s=SUBS), ALU.mult))
                step(nc.vector.tensor_tensor(picked, hot, spread(coef.rearrange("p s k -> p (s k)"), MOE_EXPERTS), ALU.mult))
                step(nc.vector.tensor_reduce(comb, picked.rearrange("p (s k) e -> p s e k", s=SUBS), AX.X, ALU.add))

            def body(i, alive):
                done = 0

                def step(instruction):
                    nonlocal done
                    done += 1
                    instruction.then_inc(route.sem, 1)
                    dve.wait_ge(route.sem, route.at(i, done))

                for t in range(MOE_UNITS):
                    if alive(t) and t == 0:
                        for s in range(SUBS):
                            if s == 0:
                                dve.wait_ge(xn_turned.sem, xn_turned.at(i, 0))
                            normalise(core, dve, xnorm[:, s, :], i * SUBS + s).then_inc(normed.sem, 1)
                    if alive(t) and t in (1, 2):
                        c = t - 1
                        dve.wait_ge(next_hi.sem, next_hi.at(i, c + 1))
                        nc.vector.tensor_tensor(nextT[1][:, c, :], ps[:, R, :], nextT[0][:, c, :], ALU.subtract).then_inc(next_lo.sem, 1)
                    if alive(t) and not alive(-1) and t == 3:
                        set_up()
                    if alive(t) and t == 4:
                        dve.wait_ge(routed.sem, routed.at(i, 1))
                        router_first(i, step)
                        assert done == MOE_R_SHIFT
                    if alive(t) and t == 6:
                        dve.wait_ge(rexp.sem, rexp.at(i, 1))
                        router_choose(i, step)
                    if alive(t) and t == 7:
                        router_hot(i, step)
                        assert done == MOE_R_HOT
                    if alive(t) and t == 8:
                        router_weights(i, step)
                    if alive(t) and t in (10, 11):
                        dve.wait_ge(similar.sem, similar.at(i, 1))
                        for s in range(2 * (t - 10), 2 * (t - 9)):
                            router_similar(i, s, step)
                    if alive(t) and t == 12:
                        router_combine(i, step)
                    if alive(t) and t == 13:
                        router_weigh(i, step)
                        assert done == route.per, done
                    if alive(t) and t == 14:
                        dve.wait_ge(cw_hi.sem, cw_hi.at(i, 1))
                        nc.vector.tensor_tensor(cwn[MOE_EXPERTS:2 * MOE_EXPERTS, :], ps[0:MOE_EXPERTS, R, :], cwn[0:MOE_EXPERTS, :], ALU.subtract).then_inc(cw_lo.sem, 1)
                    if alive(t) and t == MOE_FRONT:
                        dve.wait_ge(cw_ready.sem, cw_ready.at(i, 0))
                        dve.wait_ge(cw_lo.sem, cw_lo.at(i, 1))
                        for q in range(2):
                            nc.vector.tensor_copy(xT[q], nextT[q]).then_inc(moved.sem, 1)
                        nc.vector.tensor_copy(cwT[0:2 * MOE_EXPERTS, :], cwn[0:2 * MOE_EXPERTS, :]).then_inc(moved.sem, 1)
                    e = unit(t, MOE_FRONT)
                    if alive(e):
                        hv = h[:, e % 2, :]
                        dve.wait_ge(silu_ready.sem, silu_ready.at(i, e + 1))
                        dve.wait_ge(up_ready.sem, up_ready.at(i, e + 1))
                        dve.wait_ge(h_hi.sem, h_hi.at(i, e - 1))
                        nc.vector.tensor_tensor(hv, ps[:, U[e % 2], :], silu[:, e % 2, :], ALU.mult).then_inc(gated.sem, 1)
                    e = unit(t, MOE_FRONT + 1)
                    if alive(e):
                        dve.wait_ge(h_hi.sem, h_hi.at(i, e + 1))
                        nc.vector.tensor_tensor(hT[1][:, e % 2, :], h[:, e % 2, :], hT[0][:, e % 2, :], ALU.subtract).then_inc(h_lo.sem, 1)
                    e = unit(t, MOE_FRONT)
                    if alive(e):
                        hv = h[:, e % 2, :]
                        dve.wait_ge(gated.sem, gated.at(i, e + 1))
                        dve.wait_ge(cw_ready.sem, cw_ready.at(i, e + 1))
                        nc.vector.tensor_tensor(hv, ps[:, CW, :], hv, ALU.mult).then_inc(weighed.sem, 1)
                    e = unit(t, MOE_FRONT + 2)
                    if alive(e) and e % MOE_UNITS == MOE_UNITS - 1:
                        dve.wait_ge(down.sem, down.at(i, e + 1))
                        for s in range(SUBS):
                            tile = core.x[:, (i - 1) * SUBS + s, :]
                            nc.vector.tensor_tensor(tile, ps[:, ACC[s // 2], s % 2 * D:(s % 2 + 1) * D], tile, ALU.add).then_inc(added.sem, 1)

            steps(dve, body)


MOE_R_SHIFT, MOE_R_HOT = 2, 15


def build(nc, ins, out):
    with ExitStack() as ctx:
        core = Core(nc, ctx, ins, out)
        attn = AttnWeights(Region(core, AT_ATTN_W))
        cross = CrossWeights(Region(core, AT_CROSS_W))
        ffn_region = Region(core, AT_FFN_W)
        ffn, alibi = FfnWeights(ffn_region), AlibiWeights(ffn_region)
        moe = MoeWeights(Region(core, AT_MOE_W))
        later = [cross.jobs(core), ffn.jobs(core) + alibi.jobs(core), moe.jobs(core)]
        first = [sum(len(j) for j in later[:n]) for n in range(3)]
        with core.stage():
            attn_stage(core, attn, later[0], first[0])
        with core.stage():
            cross_stage(core, cross, later[1], first[1])
        with core.stage():
            ffn_stage(core, ffn, later[2], first[2])
        with core.stage():
            alibi_stage(core, alibi)
        with core.stage():
            channel_stage(core)
        with core.stage():
            moe_stage(core, moe)


def constants():
    half = CROSS_HD // 2
    inv = (1.0 / 10000.0 ** (np.arange(0, CROSS_HD, 2, dtype=np.float32) / CROSS_HD)).astype(np.float32)
    angle = np.outer(np.arange(S, dtype=np.float32), inv).astype(np.float32)
    angle = np.concatenate([angle, angle], -1)
    sine = np.sin(angle)
    sine[:, :half] *= -1
    query, key = np.arange(P) % S, np.arange(S)
    future = key[None, :] > query[:, None]
    mask = np.concatenate([np.zeros((P, S)), np.where(future, -1e9, 0.0)], 1)
    start = 2.0 ** (-2.0 ** (-(np.log2(ALIBI_HEADS) - 3)))
    slopes = np.array([start * start ** n for n in range(ALIBI_KVH)], np.float32)
    rel = (key[None, :] - query[:, None]).astype(np.float32)
    alibi = np.where(future[:, None, :], np.float32(-1e30), slopes[None, :, None] * rel[:, None, :])
    row = np.arange(P)
    apart = (row[:, None] % CH_GT // CH_CH == np.arange(CH_IN_GROUP)[None]) & (row[:, None] < CH_ROWS)
    apart |= row[:, None] == CH_ROWS + np.arange(CH_IN_GROUP)[None]
    column = np.arange(MOE_EXPERTS * MOE_FF) // MOE_FF
    select = (row[:, None] % MOE_EXPERTS == column[None]) & (row[:, None] < 2 * MOE_EXPERTS)
    f32 = lambda a: np.ascontiguousarray(a, dtype=np.float32)
    return {
        "ident": np.eye(P, dtype=np.float32),
        "headmask": f32(row[:, None] // ALIBI_HD == np.arange(8)[None]),
        "cos": f32(np.tile(np.cos(angle), (2, 1))),
        "sin": f32(np.tile(sine, (2, 1))),
        "mask": f32(mask),
        "alibi": f32(alibi),
        "apart": f32(apart),
        "iota": f32(np.tile(np.arange(MOE_EXPERTS), (P, 1))),
        "select": np.ascontiguousarray(select.reshape(P, MOE_UNITS, P), dtype=np.float16),
    }


def kernel(**inputs):
    import concourse.bacc as bacc
    from concourse.bass_utils import run_bass_kernel_spmd

    a = {name: np.asarray(value) for name, value in inputs.items()}
    a["x"] = a["x"].reshape(TOKENS, D)
    a["ctx_2048"] = a["ctx_2048"].reshape(TOKENS, D)
    a["ctxT"] = a["ctx_2048"].T
    for n in "qkv":
        a[f"L0_attn_b{n}"] = a[f"L0_attn_b{n}"].reshape(ATTN_HEADS, ATTN_HD).T
    a["L0_attn_bo"] = np.broadcast_to(a["L0_attn_bo"], (P, D))
    for n in "qk":
        a[f"L0_xattn_{n}_norm_w"] = np.broadcast_to(a[f"L0_xattn_{n}_norm_w"], (P, CROSS_HD))
    a["L1_attn_Wq"] = a["L1_attn_Wq"].reshape(D, ALIBI_KVH, 2, 2, ALIBI_HD).transpose(0, 2, 3, 1, 4).reshape(D, D)
    a["L1_attn_Wo"] = a["L1_attn_Wo"].reshape(ALIBI_KVH, 2, 2, ALIBI_HD, D).transpose(1, 2, 0, 3, 4).reshape(D, D)
    a["L1_attn_Wk"] = np.tile(a["L1_attn_Wk"], (1, 2))
    a["L1_ffn_gate_weight"] = a["L1_ffn_gate_weight"].T
    gate_up = a["L1_ffn_gate_up_proj"].reshape(MOE_EXPERTS, 2, MOE_FF, D).transpose(1, 0, 2, 3).reshape(2, MOE_UNITS, P, D)
    a["L1_ffn_gate_up_proj"] = gate_up.transpose(1, 0, 2, 3).reshape(MOE_UNITS * 2 * P, D).T
    a["L1_ffn_down_proj"] = a["L1_ffn_down_proj"].transpose(0, 2, 1).reshape(MOE_UNITS, P, D).transpose(1, 0, 2)
    a.update(constants())
    nc = bacc.Bacc("TRN2", target_bir_lowering=False, num_devices=1)
    arrays = {f"in_{name}": np.ascontiguousarray(value) for name, value in a.items()}
    ins = {name: nc.dram_tensor(f"in_{name}", arrays[f"in_{name}"].shape, mybir.dt.from_np(arrays[f"in_{name}"].dtype),
                                kind="ExternalInput").ap() for name in a}
    out = nc.dram_tensor("out", (TOKENS, D), F32, kind="ExternalOutput").ap()
    build(nc, ins, out)
    result = run_bass_kernel_spmd(nc, [arrays], core_ids=[0])
    return result.results[0]["out"].reshape(B, S, D)
```
